# Optimizing a Trainium2 kernel written in Bass

```python
import numpy as np
import jax
import jax.numpy as jnp

def _softmax(x, axis=-1):
    return jax.nn.softmax(x, axis=axis)

def _gelu(x):
    return jax.nn.gelu(x, approximate=True)

def _silu(x):
    return jax.nn.silu(x)

def _sigmoid(x):
    return jax.nn.sigmoid(x)

def _layernorm(x, axis=-1, eps=1e-05):
    m = jnp.mean(x, axis=axis, keepdims=True)
    v = jnp.var(x, axis=axis, keepdims=True)
    return (x - m) / jnp.sqrt(v + eps)

def _scatter_add(tgt, idx, src, axis=0):
    return tgt.at[idx].add(src)

def _segment_sum(src, seg, n):
    return jax.ops.segment_sum(src, seg, n)
kernel_name = 'mk_seq_postln_d1_jaxref_r8_57fcf7'

def setup_inputs(seed: int=0):
    np.random.seed(seed)
    _w = jnp.asarray

    def _L0_attn_setup():
        import jax, jax.numpy as jnp
        import numpy as np
        B, S, E = (2, 256, 128)
        INNER = 256
        NH = 4
        K = 4
        PH, PD = (64, 4)

        def _forward(x, W_up, conv_w, conv_b, Wq, Wk, Wv, W_ig, b_ig, W_fg, b_fg, norm_w, skip, W_down):
            Bx, Sx, _ = x.shape
            x_inner = x @ W_up
            x_mlstm, z = jnp.split(x_inner, 2, axis=-1)
            Kk = conv_w.shape[0]
            x_pad = jnp.pad(x_mlstm, ((0, 0), (Kk - 1, 0), (0, 0)))
            x_conv = sum((x_pad[:, i:i + Sx, :] * conv_w[i] for i in range(Kk))) + conv_b
            x_act = jax.nn.swish(x_conv)

            def headwise(t, W):
                H, o, d = W.shape
                return jnp.einsum('bshd,hod->bsho', t.reshape(Bx, Sx, H, d), W).reshape(Bx, Sx, H * o)
            q = headwise(x_act, Wq)
            k = headwise(x_act, Wk)
            v = headwise(x_mlstm, Wv)
            Dm = q.shape[-1]
            NHn = b_ig.shape[0]
            DH = Dm // NHn
            qh = q.reshape(Bx, Sx, NHn, DH).transpose(0, 2, 1, 3)
            kh = k.reshape(Bx, Sx, NHn, DH).transpose(0, 2, 1, 3)
            vh = v.reshape(Bx, Sx, NHn, DH).transpose(0, 2, 1, 3)
            if_in = jnp.concatenate([q, k, v], axis=-1)
            ig = (if_in @ W_ig + b_ig).transpose(0, 2, 1)[..., None]
            fg = (if_in @ W_fg + b_fg).transpose(0, 2, 1)[..., None]
            log_f = jax.nn.log_sigmoid(fg)
            lfc = jnp.concatenate([jnp.zeros((Bx, NHn, 1, 1), log_f.dtype), jnp.cumsum(log_f, axis=2)], axis=2)
            lfm = lfc - jnp.swapaxes(lfc, -2, -1)
            mask = jnp.tril(jnp.ones((Sx + 1, Sx + 1), bool))
            lfm = jnp.where(mask, lfm, -jnp.inf)[:, :, 1:, 1:]
            logD = lfm + jnp.swapaxes(ig, -2, -1)
            mD = jnp.max(logD, axis=-1, keepdims=True)
            Dmat = jnp.exp(logD - mD)
            C = jnp.einsum('bnsd,bntd->bnst', qh, kh) * DH ** (-0.5) * Dmat
            norm = jnp.maximum(jnp.abs(C.sum(-1, keepdims=True)), jnp.exp(-mD))
            h = jnp.einsum('bnst,bntd->bnsd', C / (norm + 1e-06), vh)
            mu = h.mean(-1, keepdims=True)
            var = ((h - mu) ** 2).mean(-1, keepdims=True)
            hn = ((h - mu) * jax.lax.rsqrt(var + 1e-06)).transpose(0, 2, 1, 3).reshape(Bx, Sx, Dm)
            hn = hn * norm_w
            h_state = (hn + skip * x_act) * jax.nn.swish(z)
            return h_state @ W_down
        key = jax.random.key(seed)
        ks = jax.random.split(key, 10)
        f = lambda k, shape, s=0.02: jax.random.normal(k, shape, jnp.float32) * s
        return dict(x=jax.random.normal(ks[0], (B, S, E), jnp.float32), W_up=f(ks[1], (E, 2 * INNER)), conv_w=f(ks[2], (K, INNER), 0.1), conv_b=jnp.zeros((INNER,), jnp.float32), Wq=f(ks[3], (PH, PD, PD), 0.3), Wk=f(ks[4], (PH, PD, PD), 0.3), Wv=f(ks[5], (PH, PD, PD), 0.3), W_ig=f(ks[6], (3 * INNER, NH), 0.01), b_ig=jnp.zeros((NH,), jnp.float32), W_fg=f(ks[7], (3 * INNER, NH), 0.01), b_fg=jnp.linspace(3.0, 6.0, NH).astype(jnp.float32), norm_w=jnp.ones((INNER,), jnp.float32), skip=jnp.ones((INNER,), jnp.float32), W_down=f(ks[8], (INNER, E)))
    _L0_attn_in = _L0_attn_setup()

    def _L0_ffn_setup():
        import jax, jax.numpy as jnp
        import numpy as np
        B, S, D, H, E, K = (2, 128, 128, 64, 16, 4)
        HS = 2 * H

        def silu(z):
            return z * jax.nn.sigmoid(z)
        key = jax.random.key(seed)
        ks = jax.random.split(key, 8)
        sc = lambda fan_in: 1.0 / np.sqrt(fan_in)
        x = jax.random.normal(ks[0], (B, S, D), jnp.float32)
        gate_w = jax.random.normal(ks[1], (E, D), jnp.float32) * sc(D)
        ws_in = jax.random.normal(ks[2], (D, HS), jnp.float32) * sc(D)
        vs_in = jax.random.normal(ks[3], (D, HS), jnp.float32) * sc(D)
        ws_out = jax.random.normal(ks[4], (HS, D), jnp.float32) * sc(HS)
        e_win = jax.random.normal(ks[5], (E, D, H), jnp.float32) * sc(D)
        e_vin = jax.random.normal(ks[6], (E, D, H), jnp.float32) * sc(D)
        e_wout = jax.random.normal(ks[7], (E, H, D), jnp.float32) * sc(H)
        return {'x': x, 'gate_w': gate_w, 'ws_in': ws_in, 'vs_in': vs_in, 'ws_out': ws_out, 'e_win': e_win, 'e_vin': e_vin, 'e_wout': e_wout}
    _L0_ffn_in = _L0_ffn_setup()
    _d = {'L0_attn_x': _L0_attn_in['x'], 'L0_attn_W_up': _L0_attn_in['W_up'], 'L0_attn_conv_w': _L0_attn_in['conv_w'], 'L0_attn_conv_b': _L0_attn_in['conv_b'], 'L0_attn_Wq': _L0_attn_in['Wq'], 'L0_attn_Wk': _L0_attn_in['Wk'], 'L0_attn_Wv': _L0_attn_in['Wv'], 'L0_attn_W_ig': _L0_attn_in['W_ig'], 'L0_attn_b_ig': _L0_attn_in['b_ig'], 'L0_attn_W_fg': _L0_attn_in['W_fg'], 'L0_attn_b_fg': _L0_attn_in['b_fg'], 'L0_attn_norm_w': _L0_attn_in['norm_w'], 'L0_attn_skip': _L0_attn_in['skip'], 'L0_attn_W_down': _L0_attn_in['W_down'], 'L0_ffn_gate_w': _L0_ffn_in['gate_w'], 'L0_ffn_ws_in': _L0_ffn_in['ws_in'], 'L0_ffn_vs_in': _L0_ffn_in['vs_in'], 'L0_ffn_ws_out': _L0_ffn_in['ws_out'], 'L0_ffn_e_win': _L0_ffn_in['e_win'], 'L0_ffn_e_vin': _L0_ffn_in['e_vin'], 'L0_ffn_e_wout': _L0_ffn_in['e_wout']}
    _x0 = _d['L0_attn_x']
    _d['L0_attn_x'] = jax.random.normal(jax.random.fold_in(jax.random.key(seed), 1), (8, 1024, 128), dtype=_x0.dtype)
    del _x0
    return _d

def reference(L0_attn_x, L0_attn_W_up, L0_attn_conv_w, L0_attn_conv_b, L0_attn_Wq, L0_attn_Wk, L0_attn_Wv, L0_attn_W_ig, L0_attn_b_ig, L0_attn_W_fg, L0_attn_b_fg, L0_attn_norm_w, L0_attn_skip, L0_attn_W_down, L0_ffn_gate_w, L0_ffn_ws_in, L0_ffn_vs_in, L0_ffn_ws_out, L0_ffn_e_win, L0_ffn_e_vin, L0_ffn_e_wout):

    def _L0_attn_ref(x, W_up, conv_w, conv_b, Wq, Wk, Wv, W_ig, b_ig, W_fg, b_fg, norm_w, skip, W_down):
        import jax, jax.numpy as jnp
        import numpy as np
        B, S, E = (2, 256, 128)
        INNER = 256
        NH = 4
        K = 4
        PH, PD = (64, 4)

        def _forward(x, W_up, conv_w, conv_b, Wq, Wk, Wv, W_ig, b_ig, W_fg, b_fg, norm_w, skip, W_down):
            Bx, Sx, _ = x.shape
            x_inner = x @ W_up
            x_mlstm, z = jnp.split(x_inner, 2, axis=-1)
            Kk = conv_w.shape[0]
            x_pad = jnp.pad(x_mlstm, ((0, 0), (Kk - 1, 0), (0, 0)))
            x_conv = sum((x_pad[:, i:i + Sx, :] * conv_w[i] for i in range(Kk))) + conv_b
            x_act = jax.nn.swish(x_conv)

            def headwise(t, W):
                H, o, d = W.shape
                return jnp.einsum('bshd,hod->bsho', t.reshape(Bx, Sx, H, d), W).reshape(Bx, Sx, H * o)
            q = headwise(x_act, Wq)
            k = headwise(x_act, Wk)
            v = headwise(x_mlstm, Wv)
            Dm = q.shape[-1]
            NHn = b_ig.shape[0]
            DH = Dm // NHn
            qh = q.reshape(Bx, Sx, NHn, DH).transpose(0, 2, 1, 3)
            kh = k.reshape(Bx, Sx, NHn, DH).transpose(0, 2, 1, 3)
            vh = v.reshape(Bx, Sx, NHn, DH).transpose(0, 2, 1, 3)
            if_in = jnp.concatenate([q, k, v], axis=-1)
            ig = (if_in @ W_ig + b_ig).transpose(0, 2, 1)[..., None]
            fg = (if_in @ W_fg + b_fg).transpose(0, 2, 1)[..., None]
            log_f = jax.nn.log_sigmoid(fg)
            lfc = jnp.concatenate([jnp.zeros((Bx, NHn, 1, 1), log_f.dtype), jnp.cumsum(log_f, axis=2)], axis=2)
            lfm = lfc - jnp.swapaxes(lfc, -2, -1)
            mask = jnp.tril(jnp.ones((Sx + 1, Sx + 1), bool))
            lfm = jnp.where(mask, lfm, -jnp.inf)[:, :, 1:, 1:]
            logD = lfm + jnp.swapaxes(ig, -2, -1)
            mD = jnp.max(logD, axis=-1, keepdims=True)
            Dmat = jnp.exp(logD - mD)
            C = jnp.einsum('bnsd,bntd->bnst', qh, kh) * DH ** (-0.5) * Dmat
            norm = jnp.maximum(jnp.abs(C.sum(-1, keepdims=True)), jnp.exp(-mD))
            h = jnp.einsum('bnst,bntd->bnsd', C / (norm + 1e-06), vh)
            mu = h.mean(-1, keepdims=True)
            var = ((h - mu) ** 2).mean(-1, keepdims=True)
            hn = ((h - mu) * jax.lax.rsqrt(var + 1e-06)).transpose(0, 2, 1, 3).reshape(Bx, Sx, Dm)
            hn = hn * norm_w
            h_state = (hn + skip * x_act) * jax.nn.swish(z)
            return h_state @ W_down
        return _forward(x, W_up, conv_w, conv_b, Wq, Wk, Wv, W_ig, b_ig, W_fg, b_fg, norm_w, skip, W_down)

    def _L0_ffn_ref(x, gate_w, ws_in, vs_in, ws_out, e_win, e_vin, e_wout):
        import jax, jax.numpy as jnp
        import numpy as np
        B, S, D, H, E, K = (2, 128, 128, 64, 16, 4)
        HS = 2 * H

        def silu(z):
            return z * jax.nn.sigmoid(z)
        b, s, d = x.shape
        T = b * s
        xf = x.reshape(T, d)
        g = jax.nn.sigmoid(xf @ gate_w.T)
        topv, topi = jax.lax.top_k(g, K)
        wn = topv / jnp.sum(topv, axis=-1, keepdims=True)
        combine = jnp.zeros_like(g).at[jnp.arange(T)[:, None], topi].add(wn)
        hin = jnp.einsum('td,edh->eth', xf, e_win)
        vin = jnp.einsum('td,edh->eth', xf, e_vin)
        h = silu(hin) * vin * combine.T[:, :, None]
        routed = jnp.einsum('eth,ehd->td', h, e_wout)
        shared = silu(xf @ ws_in) * (xf @ vs_in) @ ws_out
        return (shared + routed).reshape(b, s, d)
    x = L0_attn_x
    x = _layernorm(x + _L0_attn_ref(x, L0_attn_W_up, L0_attn_conv_w, L0_attn_conv_b, L0_attn_Wq, L0_attn_Wk, L0_attn_Wv, L0_attn_W_ig, L0_attn_b_ig, L0_attn_W_fg, L0_attn_b_fg, L0_attn_norm_w, L0_attn_skip, L0_attn_W_down), axis=-1)
    x = _layernorm(x + _L0_ffn_ref(x, L0_ffn_gate_w, L0_ffn_ws_in, L0_ffn_vs_in, L0_ffn_ws_out, L0_ffn_e_win, L0_ffn_e_vin, L0_ffn_e_wout), axis=-1)
    return x

_drawn_inputs = setup_inputs


def setup_inputs(seed=0):
    import zlib

    import numpy as np

    out = dict(_drawn_inputs(seed))
    spreads = {'L0_attn_conv_b': (0.0, 0.1),
     'L0_attn_b_ig': (0.0, 0.698),
     'L0_attn_norm_w': (1.0, 0.6),
     'L0_attn_skip': (1.0, 0.6)}
    factors = {'L0_attn_W_ig': 30.767, 'L0_attn_W_fg': 64.0}
    for name, (base, spread) in spreads.items():
        noise = np.random.default_rng([zlib.crc32(name.encode()), seed]).standard_normal(out[name].shape)
        drawn = base * np.exp(spread * noise) if base else spread * noise
        out[name] = jnp.asarray(drawn.astype(out[name].dtype))
    for name, factor in factors.items():
        out[name] = (out[name] * factor).astype(out[name].dtype)
    return out
```

```python
from contextlib import ExitStack

import concourse.bass as bass
from concourse import mybir

F32 = mybir.dt.float32
BF16 = mybir.dt.bfloat16
ALU = mybir.AluOpType
ACT = mybir.ActivationFunctionType
AX = mybir.AxisListType

P = 128
EPS_MIX = 1e-6
EPS_LN = 1e-5
NEG = -1e30


def mixer_moe_block(nc, x, W_up, conv_w, conv_b, Wq, Wk, Wv, W_ig, b_ig, W_fg, b_fg, norm_w, skip,
                    W_down, gate_w, ws_in, vs_in, ws_out, e_win, e_vin, e_wout, out):
    B, S, E = x.shape
    INNER = W_up.shape[1] // 2
    NH = b_ig.shape[0]
    DH = INNER // NH
    DV = DH + 1
    TAPS = conv_w.shape[0]
    HALO = TAPS - 1
    NP = INNER // P
    NX, _, HX = e_win.shape
    NJ = NX * HX // P
    TOPK = 4
    G = 512
    NC = G // P
    HALVES = S // G
    NG = B * HALVES
    CS = S // P
    R = B * NH
    QD = Wq.shape[1]
    assert E == P and INNER == 2 * P and DH == 64 and NH == 4 and HX == 64 and HALVES == 2

    x_g = x.rearrange("b (f k p) e -> (b f) p k e", f=HALVES, p=P)
    out_g = out.rearrange("b (f k p) e -> (b f) p k e", f=HALVES, p=P)
    xact_d = nc.dram_tensor("xact_scratch", [NG, P, NP * G], F32).ap()
    negm_d = nc.dram_tensor("negm_scratch", [NG, NH, G], F32).ap()
    inter_d = nc.dram_tensor("inter_scratch", [NG, NH, G], F32).ap()
    decay_d = nc.dram_tensor("decay_scratch", [R, CS], F32).ap()

    with ExitStack() as ctx:
        def sb(name, shape, dt=F32):
            return ctx.enter_context(nc.sbuf_tensor(name, shape, dt))

        def sem(name):
            return ctx.enter_context(nc.semaphore(name))

        def sems(name, *counts):
            if not counts:
                return sem(name)
            return [sems(f"{name}_{i}", *counts[1:]) for i in range(counts[0])]

        bank = [ctx.enter_context(nc.psum_tensor(f"bank{i}", [P, 512], F32)) for i in range(8)]

        ident = sb("ident", [P, P])
        ident_bf = sb("ident_bf", [P, P], BF16)
        block_mask = sb("block_mask", [P, P])
        center = sb("center", [P, P])
        pair_rows = sb("pair_rows", [3 * NX, NJ, P], BF16)
        w_up = sb("w_up", [P, 2 * INNER])
        qkv_small = sb("qkv_small", [P, 3, NP, QD])
        qkv_block = sb("qkv_block", [P, 3, NP, P])
        w_gates = sb("w_gates", [P, 3 * NP, 2 * NH])
        rows = sb("rows", [8, INNER])
        vecs = sb("vecs", [P, NP, 8])
        VB, VN, VS = TAPS, TAPS + 1, TAPS + 2
        b_i = sb("b_i", [R, 1])
        b_f = sb("b_f", [R, 1])
        gate_rows = sb("gate_rows", [NX, P])
        w_gate = sb("w_gate", [P, NX])
        w_down = sb("w_down", [P, NP, E])
        ewin = sb("ewin", [P, NX, HX])
        evin = sb("evin", [P, NX, HX])
        ewout = sb("ewout", [P, NJ, E])
        wsin = sb("wsin", [P, P])
        vsin = sb("vsin", [P, P])
        wsout = sb("wsout", [P, P])
        w_key = sb("w_key", [P, NP, P])
        g_act = sb("g_act", [P, NP, 2 * NH])
        g_x = sb("g_x", [P, 2 * NH])
        g_v = sb("g_v", [P, NP, 2 * NH])
        v_center = sb("v_center", [P, NP, P])
        w_up_t = sb("w_up_t", [P, NP, P])
        w_val = sb("w_val", [P, INNER])

        silu_z = sb("silu_z", [P, NP, B * S])
        a_tok = sb("a_tok", [P, B, HALVES, NC, NH])
        w_tok = sb("w_tok", [P, B, HALVES, NC, NH])
        floor_tok = sb("floor_tok", [P, B, HALVES, NC, NH])
        decay = sb("decay", [P, NP, B * CS])

        mixer_w_in = sem("mixer_w_in")
        ffn_w_in = sem("ffn_w_in")
        pool_const = sem("pool_const")
        blocks_made = sem("blocks_made")
        fold1_mm = sem("fold1_mm")
        fold1_out = sem("fold1_out")
        fold2_mm = sem("fold2_mm")
        weights_ready = sem("weights_ready")

        waited = sem("waited")

        block = ctx.enter_context(nc.Block())
        MIXER_DMAS = 18
        FFN_DMAS = 6

        p1 = ExitStack()

        def sb1(name, shape, dt=F32):
            return p1.enter_context(nc.sbuf_tensor(name, shape, dt))

        x_in = sb1("x_in", [P, HALVES, NC, E])
        x_t = sb1("x_t", [P, HALVES, G])
        xm = sb1("xm", [P, HALVES, NP, HALO + G])
        acc = sb1("acc", [P, HALVES, NP, G])
        xact = sb1("xact", [P, HALVES, NP, G])
        gates = sb1("gates", [P, CS, 2, R])
        pre_i = sb1("pre_i", [R, S])
        pre_f = sb1("pre_f", [R, S])
        abs_f = sb1("abs_f", [R, S])
        ones = sb1("ones", [R, S])
        lfc = sb1("lfc", [R, S])
        run_max = sb1("run_max", [R, S])
        before = sb1("before", [R, CS])
        rows_a = sb1("rows_a", [R, S])
        rows_w = sb1("rows_w", [R, S])
        rows_floor = sb1("rows_floor", [R, S])
        rows_inter = sb1("rows_inter", [R, S])
        rows_negm = sb1("rows_negm", [R, S])
        rows_decay = sb1("rows_decay", [R, CS])
        p1.close()

        x_loaded = sems("x_loaded", HALVES)
        xt_mm = sems("xt_mm", HALVES)
        xt_out = sems("xt_out", HALVES)
        up_mm = sems("up_mm", HALVES)
        up_out = sems("up_out", HALVES)
        halo_done = sem("halo_done")
        tap_done = sems("tap_done", HALVES)
        xact_done = sems("xact_done", HALVES)
        xact_stored = sems("xact_stored", HALVES)
        gate_mm = sems("gate_mm", HALVES)
        gate_out = sems("gate_out", HALVES)
        row_mm = sem("row_mm")
        act_scan = sem("act_scan")
        dve_scan = sem("dve_scan")
        back_mm = sem("back_mm")
        back_out = sem("back_out")
        rows_stored = sem("rows_stored")
        decay_in = sem("decay_in")

        xa = sb("xa", [P, NP, G])
        x_new = sb("x_new", [P, NC, E])
        x_res = sb("x_res", [P, NC, E])
        negm = sb("negm", [P, NH, G])
        inter_w = sb("inter_w", [P, NP, G])
        D = sb("D", [P, 2, 2, 2, NP, P])
        C = sb("C", [P, 2, 2, NP, P])
        xT2 = sb("xT2", [P, G])
        keyT = sb("keyT", [P, NP, G])
        vals = sb("vals", [P, NC, NH, DV])
        keys = sb("keys", [P, 2, INNER])
        qs = sb("qs", [P, NP, G])
        state = sb("state", [P, NP, 2 * DV])
        kept = sb("kept", [P, NP, 2 * DV])
        u_sb = sb("u_sb", [P, NC, NH, DV])
        sq = sb("sq", [P, NC, NH, DH])
        ssq = sb("ssq", [P, NC, NH])
        nrm = sb("nrm", [P, NC, NH])
        nrm1 = sb("nrm1", [P, NC, NH])
        nrm2 = sb("nrm2", [P, NC, NH])
        var_h = sb("var_h", [P, NC, NH])
        r_h = sb("r_h", [P, NC, NH])
        half = sb("half", [P, NC * NH])
        hn = sb("hn", [P, NC, INNER])
        skip_x = sb("skip_x", [P, NP, G])
        mixed = sb("mixed", [P, NP, G])
        hs = sb("hs", [P, NP, G])
        y1 = sb("y1", [P, NC, E])
        st1 = sb("st1", [P, NC, 6])
        mv1 = sb("mv1", [P, NC, 2])
        ve1 = sb("ve1", [P, NC])
        rs1 = sb("rs1", [P, NC])
        Y = sb("Y", [P, NC, E])
        yT = sb("yT", [P, G])
        ge = sb("ge", [P, NC, NX])
        ge1 = sb("ge1", [P, NC, NX])
        gext = sb("gext", [P, NC, NX + TOPK])
        top = sb("top", [P, NC, 8])
        rest = sb("rest", [P, NC, NX + TOPK])
        chosen = sb("chosen", [P, NC, NX])
        csum = sb("csum", [P, NC])
        crec = sb("crec", [P, NC])
        comb = sb("comb", [P, NC, NX])
        comb_r = sb("comb_r", [P, 2, NC, NX])
        comb3 = sb("comb3", [P, NC, P // NX, NX], BF16)
        combT = sb("combT", [3 * NX, G], BF16)
        s_in = sb("s_in", [P, 2, G])
        h1 = sb("h1", [P, 2, G])
        h2 = sb("h2", [P, 2, G])
        oT = sb("oT", [P, G])
        z2 = sb("z2", [P, NC, E])
        st2 = sb("st2", [P, NC, 6])
        mv2 = sb("mv2", [P, NC, 2])
        ve2 = sb("ve2", [P, NC])
        rs2 = sb("rs2", [P, NC])
        out_sb = sb("out_sb", [P, NC, E])

        LOADS = ("xa_in", "x_new_in", "x_res_in", "negm_in")
        xa_in, x_new_in, x_res_in, negm_in = (sem(n) for n in LOADS)
        inter_in = sem("inter_in")
        out_stored = sem("out_stored")
        phase2_const = sem("phase2_const")
        arg_sub = sem("arg_sub")
        arg_masked = sem("arg_masked")
        D_done = sem("D_done")
        xT_mm, xT_out = sem("xT_mm"), sem("xT_out")
        key_mm, key_out = sems("key_mm", NP), sems("key_out", NP)
        val_mm, val_out = sems("val_mm", 2), sems("val_out", 2)
        qs_done = sem("qs_done")
        skip_done = sem("skip_done")
        score_mm, C_done = sems("score_mm", 2, 2), sems("C_done", 2, 2)
        keytok_mm, keytok_out = sems("keytok_mm", 2), sems("keytok_out", 2)
        u_mm, u_out = sems("u_mm", NC), sems("u_out", NC)
        upd_mm, kept_done, state_done = sems("upd_mm", NC), sems("kept_done", NC), sems("state_done", NC)
        sq_done, ssq_done = sem("sq_done"), sem("ssq_done")
        nrm_done = sems("nrm_done", 4)
        rh_done = sem("rh_done")
        hn_done = sem("hn_done")
        hnT_mm, mixed_done, hs_done = sems("hnT_mm", NP), sems("mixed_done", NP), sems("hs_done", NP)
        down_mm = sem("down_mm")
        y1_done, st1_done, mv1_done, ve1_done = sem("y1_done"), sem("st1_done"), sem("mv1_done"), sem("ve1_done")
        rs1_done = sem("rs1_done")
        Y_done = sem("Y_done")
        yT_mm, yT_out = sem("yT_mm"), sem("yT_out")
        logit_mm, ge_done = sem("logit_mm"), sem("ge_done")
        route = sem("route")
        combT_mm, combT_out = sem("combT_mm"), sem("combT_out")
        hin_mm, vin_mm = sem("hin_mm"), sem("vin_mm")
        silu_done, h1_done = sem("silu_done"), sem("h1_done")
        bc_mm, h2_done = sem("bc_mm"), sem("h2_done")
        o_mm = sem("o_mm")
        oT_out, ob_mm = sem("oT_out"), sem("ob_mm")
        z2_done, st2_done, mv2_done, ve2_done = sem("z2_done"), sem("st2_done"), sem("mv2_done"), sem("ve2_done")
        rs2_done = sem("rs2_done")
        out_done = sem("out_done")

        def nth(g, per, i):
            return g * per + i + 1

        def alone(eng):
            eng.sem_inc(waited, 1)

        def groups(eng, mix, ffn):
            mix(0, None)
            with eng.Fori(1, NG - 1) as g:
                mix(g, g - 1)
            mix(NG - 1, NG - 2)
            ffn(NG - 1)

        def prev(eng, s, g, per=1):
            if isinstance(g, int) and g == 0:
                return
            eng.wait_ge(s, g * per)

        def prev2(eng, s, f):
            eng.wait_ge(s, f + 1)

        @block.sync
        def _(sp):
            n = [0]

            def load(dst, src, s):
                n[0] += 1
                sp.dma_start(dst, src).then_inc(s, 16)

            for f in range(HALVES):
                load(x_in[:, f], x_g[f], x_loaded[f])
            n[0] = 0
            load(w_up[:], W_up, mixer_w_in)
            for m, w in enumerate((Wq, Wk, Wv)):
                for s in range(NP):
                    load(qkv_small[:, m, s, :], w[s * (P // QD):(s + 1) * (P // QD)].rearrange("b o d -> (b o) d"), mixer_w_in)
            load(w_gates[:, :, 0:NH], W_ig.rearrange("(s p) h -> p s h", p=P), mixer_w_in)
            load(w_gates[:, :, NH:2 * NH], W_fg.rearrange("(s p) h -> p s h", p=P), mixer_w_in)
            load(rows[0:TAPS, :], conv_w, mixer_w_in)
            for i, v in ((VB, conv_b), (VN, norm_w), (VS, skip), (VS + 1, skip)):
                load(rows[i:i + 1, :], v.rearrange("(a n) -> a n", a=1), mixer_w_in)
            load(gate_rows[:], gate_w, mixer_w_in)
            load(b_i[:], b_ig.rearrange("(h a) -> h a", a=1).partition_broadcast(B), mixer_w_in)
            load(b_f[:], b_fg.rearrange("(h a) -> h a", a=1).partition_broadcast(B), mixer_w_in)
            load(w_down[:], W_down.rearrange("(s p) e -> p s e", p=P), mixer_w_in)
            assert n[0] == MIXER_DMAS, n[0]
            load(ewin[:], e_win.rearrange("e d h -> d e h"), ffn_w_in)
            load(evin[:], e_vin.rearrange("e d h -> d e h"), ffn_w_in)
            load(ewout[:], e_wout.rearrange("(j t) h d -> (t h) j d", t=P // HX), ffn_w_in)
            load(wsin[:], ws_in, ffn_w_in)
            load(vsin[:], vs_in, ffn_w_in)
            load(wsout[:], ws_out, ffn_w_in)
            assert n[0] == MIXER_DMAS + FFN_DMAS

            def store_xact(b, f):
                sp.wait_ge(xact_done[f], b + 1)
                sp.dma_start(xact_d[HALVES * b + f], xact[:, f]).then_inc(xact_stored[f], 16)

            def phase1(b):
                first, last = isinstance(b, int) and b == 0, isinstance(b, int) and b == B - 1
                for f in range(HALVES):
                    if not last:
                        sp.wait_ge(xt_mm[f], b + 1)
                        sp.dma_start(x_in[:, f], x_g[HALVES * b + HALVES + f]).then_inc(x_loaded[f], 16)
                    if f == 1:
                        store_xact(b, 0)
                    elif not first:
                        store_xact(b - 1, 1)

            phase1(0)
            with sp.Fori(1, B - 1) as b:
                phase1(b)
            phase1(B - 1)
            store_xact(B - 1, 1)

            sp.wait_ge(dve_scan, DVE_SCAN)
            sp.wait_ge(act_scan, ACT_SCAN)
            for f in range(HALVES):
                half_of = lambda t: t.rearrange("(b f) h t -> f b h t", f=HALVES)[f]
                sp.dma_start(half_of(negm_d), rows_negm[:, f * G:(f + 1) * G]).then_inc(rows_stored, 16)
                sp.dma_start(half_of(inter_d), rows_inter[:, f * G:(f + 1) * G]).then_inc(rows_stored, 16)
            sp.dma_start(decay_d, rows_decay[:]).then_inc(rows_stored, 16)
            sp.wait_ge(rows_stored, 16 * (2 * HALVES + 1))
            for f in range(HALVES):
                sp.wait_ge(xact_stored[f], 16 * B)
            for par in range(2):
                for p in range(NP):
                    sp.dma_start(decay[par * DH:(par + 1) * DH, p, :].rearrange("q (b c) -> q b c", c=CS),
                                 decay_d.rearrange("(b h) c -> h b c", h=NH)[2 * p + par].partition_broadcast(DH)
                                 ).then_inc(decay_in, 16)

            def load_negm(g):
                sp.dma_start(negm[:], negm_d[g].rearrange("h t -> (h t)").partition_broadcast(P)).then_inc(negm_in, 16)

            def load_inter(g):
                for par in range(2):
                    sp.dma_start(inter_w[par * DH:(par + 1) * DH],
                                 inter_d[g].rearrange("(p two) t -> two p t", two=2)[par].partition_broadcast(DH)
                                 ).then_inc(inter_in, 16)

            def load_xa(g):
                sp.dma_start(xa[:], xact_d[g].rearrange("p (s t) -> p s t", s=NP)).then_inc(xa_in, 16)

            sp.wait_ge(back_out, BACK)
            load_negm(0)
            load_xa(0)
            load_inter(0)
            sp.dma_start(x_new[:], x_g[0]).then_inc(x_new_in, 16)
            sp.dma_start(x_res[:], x_g[0]).then_inc(x_res_in, 16)

            def mix(g, f):
                sp.wait_ge(arg_sub, nth(g, 4, 3))
                if not (isinstance(g, int) and g == NG - 1):
                    load_negm(g + 1)
                    sp.wait_ge(xT_mm, g + 1)
                    sp.dma_start(x_new[:], x_g[g + 1]).then_inc(x_new_in, 16)
                    sp.wait_ge(qs_done, g + 1)
                    load_inter(g + 1)
                    sp.wait_ge(skip_done, g + 1)
                    sp.wait_ge(score_mm[1][1], g + 1)
                    load_xa(g + 1)
                if f is not None:
                    store(f)
                if not (isinstance(g, int) and g == NG - 1):
                    sp.wait_ge(y1_done, g + 1)
                    sp.dma_start(x_res[:], x_g[g + 1]).then_inc(x_res_in, 16)

            def store(f):
                sp.wait_ge(out_done, f + 1)
                sp.dma_start(out_g[f], out_sb[:]).then_inc(out_stored, 16)

            groups(sp, mix, store)
            sp.wait_ge(out_stored, 16 * NG)

        @block.gpsimd
        def _(pool):
            pool.memset(ident[:], 0.0).then_inc(pool_const, 1)
            pool.memset(ident_bf[:], 0.0).then_inc(pool_const, 1)
            pool.memset(block_mask[:], 1.0).then_inc(pool_const, 1)
            pool.memset(center[:], -1.0 / DH).then_inc(pool_const, 1)
            pool.memset(pair_rows[:], 0.0).then_inc(pool_const, 1)
            pool.wait_ge(pool_const, 5)
            for m in (ident, ident_bf):
                pool.affine_select(out=m[:], in_=m[:], compare_op=ALU.not_equal, fill=1.0, base=0,
                                   pattern=[[-1, P]], channel_multiplier=1).then_inc(pool_const, 1)
            bm = block_mask[:].rearrange("p (b d) -> p b d", d=QD)
            pool.affine_select(out=bm, in_=bm, compare_op=ALU.is_ge, fill=0.0, base=0,
                               pattern=[[-QD, P // QD], [0, QD]], channel_multiplier=1).then_inc(pool_const, 1)
            pool.affine_select(out=center[:, 0:DH], in_=center[:, 0:DH], compare_op=ALU.is_ge, fill=0.0,
                               base=DH - 1, pattern=[[0, DH]], channel_multiplier=-1).then_inc(pool_const, 1)
            pool.affine_select(out=center[:, DH:P], in_=center[:, DH:P], compare_op=ALU.is_ge, fill=0.0,
                               base=-DH, pattern=[[0, DH]], channel_multiplier=1).then_inc(pool_const, 1)
            pool.wait_ge(pool_const, 10)
            pool.affine_select(out=bm, in_=bm, compare_op=ALU.is_ge, fill=0.0, base=QD - 1,
                               pattern=[[QD, P // QD], [0, QD]], channel_multiplier=-1).then_inc(pool_const, 1)
            pool.tensor_tensor(center[:], center[:], ident[:], ALU.add).then_inc(pool_const, 1)
            halves = pair_rows[:].rearrange("r j (t m) -> r j t m", t=P // HX)
            for part in range(3):
                pool.affine_select(out=halves, in_=halves, compare_op=ALU.not_equal, fill=1.0, base=-NX * part,
                                   pattern=[[-2, NJ], [-1, 2], [0, HX]], channel_multiplier=1).then_inc(pool_const, 1)
                pool.wait_ge(pool_const, 13 + part)
            pool.memset(xm[:, 0, :, 0:HALO], 0.0).then_inc(pool_const, 1)
            pool.memset(ones[:], 1.0).then_inc(pool_const, 1)

            pool.wait_ge(back_out, BACK)
            pool.memset(state[:], 0.0).then_inc(phase2_const, 1)
            pool.memset(vals[:, :, :, DH:DV], 1.0).then_inc(phase2_const, 1)
            pool.memset(gext[:, :, NX:NX + TOPK], -1.0).then_inc(phase2_const, 1)
            pool.memset(half[:], -0.5).then_inc(phase2_const, 1)
            pool.memset(comb3[:], 0.0).then_inc(phase2_const, 1)

            masked = pool.to_reg(NEG)

            def args(g):
                pool.wait_ge(negm_in, 16 * (g + 1))
                a_g = a_tok[:].rearrange("p b f k h -> p (b f) k h")[:, bass.ds(g, 1)].rearrange("p g k h -> p (g k) h")
                for q in range(4):
                    kp, par = q // 2, q % 2
                    prev(pool, C_done[kp][par], g)
                    pool.tensor_tensor(
                        D[:, kp, par],
                        negm[:].rearrange("p (s two) (k t) -> p two k s t", two=2, k=NC)[:, par, 2 * kp:2 * kp + 2],
                        a_g.rearrange("p k (s two) -> p two k s", two=2)[:, par, 2 * kp:2 * kp + 2]
                        .unsqueeze(3).to_broadcast([P, 2, NP, P]),
                        ALU.add).then_inc(arg_sub, 1)
                for q in range(4):
                    kp, par = q // 2, q % 2
                    pool.wait_ge(arg_sub, nth(g, 4, q))
                    alone(pool)
                    d = D[:, kp, par].rearrange("p k s t -> p (k s) t")
                    pool.affine_select(out=d, in_=d, compare_op=ALU.is_ge, fill=masked, base=0,
                                       pattern=[[0, 2 * NP], [1, P]], channel_multiplier=-1).then_inc(arg_masked, 1)

            def power(dst, src, s):
                pool.tensor_tensor(dst, src, half[:, 0:NC], ALU.pow).then_inc(s, 1)

            def mix(g, f):
                pool.wait_ge(xa_in, 16 * (g + 1))
                pool.wait_ge(inter_in, 32 * (g + 1))
                prev(pool, u_mm[NC - 1], g)
                prev(pool, mixed_done[1], g)
                pool.tensor_tensor(qs[:], xa[:], inter_w[:], ALU.mult).then_inc(qs_done, 1)
                for p in range(NP):
                    i = pool.tensor_scalar(skip_x[:, p], xa[:, p], vecs[:, p, VS:VS + 1], None, ALU.mult)
                i.then_inc(skip_done, 1)
                dec = decay[:].rearrange("p s (g k) -> p g k s", k=NC)[:, bass.ds(g, 1)].rearrange("p g k s -> p (g k) s")
                for k in range(NC):
                    if k:
                        pool.wait_ge(state_done[k - 1], g + 1)
                    else:
                        prev(pool, state_done[NC - 1], g)
                    pool.tensor_tensor(kept[:], state[:], dec[:, k, :].unsqueeze(2).to_broadcast([P, NP, 2 * DV]),
                                       ALU.mult).then_inc(kept_done[k], 1)
                    if k == 2 and not (isinstance(g, int) and g == NG - 1):
                        args(g + 1)
                pool.wait_ge(nrm_done[3], g + 1)
                pool.tensor_tensor(r_h[:].rearrange("p k h -> p (k h)"), var_h[:].rearrange("p k h -> p (k h)"),
                                   half[:], ALU.pow).then_inc(rh_done, 1)
                pool.wait_ge(rh_done, g + 1)
                pool.tensor_tensor(hn[:].rearrange("p k (h d) -> p (k h) d", d=DH),
                                   u_sb[:].rearrange("p k h d -> p (k h) d")[:, :, 0:DH],
                                   r_h[:].rearrange("p k h -> p (k h)").unsqueeze(2).to_broadcast([P, NC * NH, DH]),
                                   ALU.mult).then_inc(hn_done, 1)
                pool.wait_ge(ve1_done, g + 1)
                power(rs1[:], ve1[:], rs1_done)
                if f is not None:
                    ffn(f)

            def ffn(f):
                pool.wait_ge(ve2_done, f + 1)
                power(rs2[:], ve2[:], rs2_done)

            pool.wait_ge(decay_in, 16 * 2 * NP)
            pool.wait_ge(phase2_const, 5)
            args(0)
            groups(pool, mix, ffn)

        @block.scalar
        def _(act):
            def copy(dst, src):
                return act.activation(dst, src, ACT.Copy)

            def phase1_xact(b, f):
                if not (isinstance(b, int) and b == 0):
                    act.wait_ge(xact_stored[f], 16 * b)
                    act.wait_ge(gate_mm[f], b)
                for p in range(NP):
                    act.wait_ge(tap_done[f], b * NP * TAPS + HALO * NP + p + 1)
                    i = act.activation(xact[:, f, p], acc[:, f, p], ACT.Silu)
                i.then_inc(xact_done[f], 1)

            def phase1_xt(b, f):
                act.wait_ge(xt_mm[f], b + 1)
                if not (isinstance(b, int) and b == 0):
                    act.wait_ge(gate_mm[f], b)
                copy(x_t[:, f], bank[0][:]).then_inc(xt_out[f], 1)

            def phase1(b):
                first, last = isinstance(b, int) and b == 0, isinstance(b, int) and b == B - 1
                for f in range(HALVES):
                    if f == 1:
                        phase1_xact(b, 0)
                    elif not first:
                        phase1_xact(b - 1, 1)
                    if not first:
                        act.wait_ge(tap_done[f], b * NP * TAPS)
                    for p in range(NP):
                        act.wait_ge(up_mm[f], b * 2 * NP + p + 1)
                        copy(xm[:, f, p, HALO:], bank[1 + p][:]).then_inc(up_out[f], 1)
                    if f == 0:
                        phase1_xt(b, 1)
                        act.wait_ge(up_out[0], b * 2 * NP + NP)
                        copy(xm[:, 1, :, 0:HALO], xm[:, 0, :, G:G + HALO]).then_inc(halo_done, 1)
                    elif not last:
                        phase1_xt(b + 1, 0)
                    for p in range(NP):
                        act.wait_ge(up_mm[f], b * 2 * NP + NP + p + 1)
                        act.activation(silu_z[:, p, bass.ds(b * S + f * G, G)], bank[3 + p][:], ACT.Silu
                                       ).then_inc(up_out[f], 1)

            phase1_xt(0, 0)
            phase1(0)
            with act.Fori(1, B - 1) as b:
                phase1(b)
            phase1(B - 1)
            phase1_xact(B - 1, 1)

            act.wait_ge(row_mm, 1)
            for c in range(2):
                act.activation(pre_i[:, c * 512:(c + 1) * 512], bank[c][0:R, :], ACT.Identity, bias=b_i[:]).then_inc(act_scan, 1)
                act.activation(pre_f[:, c * 512:(c + 1) * 512], bank[2 + c][0:R, :], ACT.Identity, bias=b_f[:]).then_inc(act_scan, 1)
            act.wait_ge(act_scan, 4)
            act.activation(abs_f[:], pre_f[:], ACT.Abs).then_inc(act_scan, 1)
            act.wait_ge(act_scan, 5)
            act.activation(rows_a[:], abs_f[:], ACT.Exp, scale=-1.0).then_inc(act_scan, 1)
            act.wait_ge(act_scan, 6)
            act.activation(abs_f[:], rows_a[:], ACT.Ln, bias=1.0).then_inc(act_scan, 1)
            act.wait_ge(dve_scan, 9)
            act.activation(rows_w[:], rows_w[:], ACT.Exp).then_inc(act_scan, 1)
            act.activation(rows_floor[:], rows_floor[:], ACT.Exp, scale=-1.0).then_inc(act_scan, 1)
            act.activation(rows_inter[:], rows_inter[:], ACT.Exp).then_inc(act_scan, 1)
            act.activation(rows_decay[:], rows_decay[:], ACT.Exp).then_inc(act_scan, 1)

            act.wait_ge(back_out, BACK)

            def mix(g, f):
                act.wait_ge(xT_mm, g + 1)
                prev(act, val_mm[1], g)
                copy(xT2[:], bank[0][:]).then_inc(xT_out, 1)
                for q in range(4):
                    act.wait_ge(arg_masked, nth(g, 4, q))
                    d = D[:, q // 2, q % 2].rearrange("p k s t -> p (k s t)")
                    act.activation(d, d, ACT.Exp).then_inc(D_done, 1)
                if f is not None:
                    ffn_head(f)
                for j in range(NJ + 1):
                    if f is not None:
                        ffn_slot(f, j)
                    if j in U_SLOT:
                        for k in U_SLOT[j]:
                            act.wait_ge(u_mm[k], g + 1)
                            if k == 0:
                                prev(act, hn_done, g)
                            copy(u_sb[:, k].rearrange("p h d -> p (h d)"), bank[3][:, 0:NH * DV]).then_inc(u_out[k], 1)
                        if NC - 1 in U_SLOT[j]:
                            act.wait_ge(u_out[NC - 1], g + 1)
                            prev(act, ssq_done, g)
                            act.activation(sq[:].rearrange("p k h d -> p (k h) d"),
                                           u_sb[:].rearrange("p k h d -> p (k h) d")[:, :, 0:DH],
                                           ACT.Square).then_inc(sq_done, 1)
                if f is not None:
                    ffn_tail(f)

            def ffn_head(f):
                act.wait_ge(yT_mm, f + 1)
                prev2(act, z2_done, f)
                copy(yT[:], bank[7][:]).then_inc(yT_out, 1)
                act.wait_ge(logit_mm, f + 1)
                act.activation(ge[:].rearrange("p k e -> p (k e)"), bank[6][:, 0:NC * NX], ACT.Exp,
                               scale=-1.0).then_inc(ge_done, 1)

            def ffn_slot(f, j):
                act.wait_ge(hin_mm, nth(f, NJ + 1, j))
                if j >= 2:
                    act.wait_ge(h1_done, nth(f, NJ + 1, j - 2))
                act.activation(s_in[:, j % 2], bank[4][:], ACT.Silu).then_inc(silu_done, 1)
                if j == 1:
                    act.wait_ge(combT_mm, f + 1)
                    copy(combT[:], bank[6][0:3 * NX, 0:G // 2].bitcast(BF16)).then_inc(combT_out, 1)

            def ffn_tail(f):
                act.wait_ge(o_mm, f + 1)
                copy(oT[:], bank[7][:]).then_inc(oT_out, 1)

            def ffn(f):
                ffn_head(f)
                for j in range(NJ + 1):
                    ffn_slot(f, j)
                ffn_tail(f)

            groups(act, mix, ffn)

        @block.vector
        def _(dve):
            dve.wait_ge(pool_const, 17)
            dve.wait_ge(mixer_w_in, 16 * MIXER_DMAS)
            mask = block_mask[:].rearrange("p (b d) -> p b d", d=QD)
            for m in range(3):
                for s in range(NP):
                    i = dve.tensor_tensor(qkv_block[:, m, s].rearrange("p (b d) -> p b d", d=QD), mask,
                                          qkv_small[:, m, s].unsqueeze(1).to_broadcast([P, P // QD, QD]), ALU.mult)
            i.then_inc(blocks_made, 1)
            dve.wait_ge(fold1_mm, 1)
            dve.tensor_scalar(w_key[:].rearrange("p s d -> p (s d)"), bank[0][:, 0:INNER], DH ** -0.5, None, ALU.mult)
            dve.tensor_copy(v_center[:].rearrange("p s d -> p (s d)"), bank[1][:, 0:INNER])
            dve.tensor_copy(w_up_t[:].rearrange("p s d -> p (s d)"), bank[2][:, 0:INNER])
            n8 = 2 * NH * NP
            dve.tensor_copy(g_act[:].rearrange("p s d -> p (s d)"), bank[3][:, 0:n8])
            dve.tensor_copy(g_v[:].rearrange("p s d -> p (s d)"), bank[3][:, n8:2 * n8])
            dve.tensor_copy(vecs[:].rearrange("p s d -> p (s d)"), bank[3][:, 2 * n8:3 * n8])
            dve.tensor_copy(w_gate[:], bank[3][:, 3 * n8:3 * n8 + NX]).then_inc(fold1_out, 1)
            dve.wait_ge(fold2_mm, 1)
            dve.tensor_copy(w_val[:], bank[4][:, 0:INNER])
            dve.tensor_copy(g_x[:], bank[4][:, INNER:INNER + 2 * NH]).then_inc(weights_ready, 1)

            def phase1_gates(b, f):
                dve.wait_ge(gate_mm[f], b + 1)
                dst = gates[:, f * NC:(f + 1) * NC].rearrange("p k t r -> p (k t) r")[:, :, bass.ds(b * NH, NH)]
                dve.tensor_copy(dst, bank[5 + f][:, 0:NC * 2 * NH].rearrange("p (k h) -> p k h", h=NH)
                                ).then_inc(gate_out[f], 1)

            def phase1(b):
                first = isinstance(b, int) and b == 0
                for f in range(HALVES):
                    for t in range(TAPS):
                        for p in range(NP):
                            a, src = acc[:, f, p], xm[:, f, p, t:t + G]
                            if t == 0:
                                dve.wait_ge(up_out[f], b * 2 * NP + p + 1)
                                if f == 1:
                                    dve.wait_ge(halo_done, b + 1)
                                if not first:
                                    dve.wait_ge(xact_done[f], b)
                                i = dve.tensor_scalar(a, src, vecs[:, p, 0:1], vecs[:, p, VB:VB + 1], ALU.mult, ALU.add)
                            else:
                                dve.wait_ge(tap_done[f], b * NP * TAPS + (t - 1) * NP + p + 1)
                                i = dve.scalar_tensor_tensor(a, src, vecs[:, p, t:t + 1], a, ALU.mult, ALU.add)
                            i.then_inc(tap_done[f], 1)
                    if f == 1:
                        phase1_gates(b, 0)
                    elif not first:
                        phase1_gates(b - 1, 1)

            phase1(0)
            with dve.Fori(1, B) as b:
                phase1(b)
            phase1_gates(B - 1, 1)

            dve.wait_ge(act_scan, 7)
            dve.scalar_tensor_tensor(pre_f[:], pre_f[:], 0.0, abs_f[:], ALU.min, ALU.subtract).then_inc(dve_scan, 1)
            dve.wait_ge(dve_scan, 1)
            dve.tensor_tensor_scan(lfc[:], ones[:], pre_f[:], 0.0, ALU.mult, ALU.add).then_inc(dve_scan, 1)
            dve.wait_ge(dve_scan, 2)
            dve.tensor_tensor(rows_a[:], pre_i[:], lfc[:], ALU.subtract).then_inc(dve_scan, 1)
            dve.wait_ge(dve_scan, 3)
            dve.tensor_tensor_scan(run_max[:], rows_a[:], rows_a[:], -3e38, ALU.max, ALU.max).then_inc(dve_scan, 1)
            dve.memset(before[:, 0:1], NEG)
            dve.wait_ge(dve_scan, 4)
            ends = run_max[:].rearrange("r (c t) -> r c t", t=P)[:, :, P - 1]
            dve.tensor_copy(before[:, 1:CS], ends[:, 0:CS - 1]).then_inc(dve_scan, 1)
            dve.tensor_tensor(rows_floor[:], lfc[:], run_max[:], ALU.add).then_inc(dve_scan, 1)
            chunks = lambda t: t[:].rearrange("r (c t) -> r c t", t=P)
            wide = lambda t: t.unsqueeze(2).to_broadcast([R, CS, P])
            dve.tensor_tensor(chunks(rows_w), chunks(rows_a), wide(ends), ALU.subtract).then_inc(dve_scan, 1)
            dve.wait_ge(dve_scan, 5)
            dve.tensor_tensor(chunks(rows_inter), wide(before[:]), chunks(run_max), ALU.subtract).then_inc(dve_scan, 1)
            dve.tensor_tensor(rows_decay[:], before[:], ends, ALU.subtract).then_inc(dve_scan, 1)
            dve.tensor_scalar(rows_negm[:], run_max[:], -1.0, None, ALU.mult).then_inc(dve_scan, 1)
            for i, dst in enumerate((a_tok, w_tok, floor_tok)):
                dve.wait_ge(back_mm, i + 1)
                d = dst[:].rearrange("p b f k h -> p b (f k) h")
                s = bank[4 + i][:, 0:CS * R].rearrange("p (c b h) -> p b c h", b=B, h=NH)
                if dst is floor_tok:
                    dve.tensor_scalar(d, s, EPS_MIX, None, ALU.add).then_inc(back_out, 1)
                else:
                    dve.tensor_copy(d, s).then_inc(back_out, 1)

            dve.wait_ge(phase2_const, 5)
            dve.sem_inc(z2_done, 1)
            all_tok = lambda t: t[:].rearrange("p b f k h -> p (b f) (k h)")

            def of_group(t, g):
                return all_tok(t)[:, bass.ds(g, 1)].rearrange("p g (k h) -> p (g k) h", h=NH)

            def key_evac(g, p):
                dve.wait_ge(key_mm[p], g + 1)
                dve.tensor_copy(keyT[:, p], bank[1 + p][:]).then_inc(key_out[p], 1)

            def val_evac(g, i):
                dve.wait_ge(val_mm[i], g + 1)
                dve.tensor_copy(vals[:, 2 * i:2 * i + 2, :, 0:DH].rearrange("p k h d -> p (k h) d"),
                                bank[3 if i == 0 else 0][:].rearrange("p (q d) -> p q d", d=DH)).then_inc(val_out[i], 1)

            def weigh_scores(g, kp):
                for par in range(2):
                    dve.wait_ge(D_done, nth(g, 4, 2 * kp + par))
                    dve.wait_ge(score_mm[kp][par], g + 1)
                    if kp:
                        dve.wait_ge(u_mm[1], g + 1)
                    dve.tensor_tensor(C[:, par].rearrange("p k s t -> p (k s t)"), bank[1 + par][:],
                                      D[:, kp, par].rearrange("p k s t -> p (k s t)"), ALU.mult
                                      ).then_inc(C_done[kp][par], 1)

            def weigh_keys(g, kp):
                dve.wait_ge(keytok_mm[kp], g + 1)
                dve.tensor_tensor(keys[:].rearrange("p k (h d) -> p (k h) d", d=DH),
                                  bank[0][:].rearrange("p (q d) -> p q d", d=DH),
                                  of_group(w_tok, g)[:, 2 * kp:2 * kp + 2, :].rearrange("p k h -> p (k h)")
                                  .unsqueeze(2).to_broadcast([P, 2 * NH, DH]), ALU.mult).then_inc(keytok_out[kp], 1)

            def update_state(g, k):
                dve.wait_ge(upd_mm[k], g + 1)
                dve.wait_ge(kept_done[k], g + 1)
                new = bank[0][:, 0:NP * 2 * DV].rearrange("p (s d) -> p s d", s=NP)
                for par in range(2):
                    r, c = slice(par * DH, (par + 1) * DH), slice(par * DV, (par + 1) * DV)
                    i = dve.tensor_tensor(state[r, :, c], kept[r, :, c], new[r, :, c], ALU.add)
                i.then_inc(state_done[k], 1)

            def head_scale(g):
                dve.wait_ge(u_out[NC - 1], g + 1)
                total = u_sb[:, :, :, DH]
                dve.scalar_tensor_tensor(nrm[:], total, -1.0, total, ALU.mult, ALU.max).then_inc(nrm_done[0], 1)
                dve.wait_ge(nrm_done[0], g + 1)
                dve.scalar_tensor_tensor(nrm1[:], nrm[:], EPS_MIX, of_group(floor_tok, g), ALU.add, ALU.max
                                         ).then_inc(nrm_done[1], 1)
                dve.wait_ge(sq_done, g + 1)
                dve.tensor_reduce(ssq[:].rearrange("p k h -> p (k h)"), sq[:].rearrange("p k h d -> p (k h) d"),
                                  AX.X, ALU.add).then_inc(ssq_done, 1)
                dve.wait_ge(nrm_done[1], g + 1)
                dve.scalar_tensor_tensor(nrm2[:], nrm1[:], EPS_MIX, nrm1[:], ALU.mult, ALU.mult).then_inc(nrm_done[2], 1)
                dve.wait_ge(ssq_done, g + 1)
                dve.wait_ge(nrm_done[2], g + 1)
                dve.scalar_tensor_tensor(var_h[:], ssq[:], 1.0 / DH, nrm2[:], ALU.mult, ALU.add).then_inc(nrm_done[3], 1)

            def gate_heads(g):
                dve.wait_ge(skip_done, g + 1)
                for p in range(NP):
                    dve.wait_ge(hnT_mm[p], g + 1)
                    dve.scalar_tensor_tensor(mixed[:, p], bank[1 + p][:], vecs[:, p, VN:VN + 1], skip_x[:, p],
                                             ALU.mult, ALU.add).then_inc(mixed_done[p], 1)
                for p in range(NP):
                    dve.wait_ge(mixed_done[p], g + 1)
                    dve.tensor_tensor(hs[:, p], mixed[:, p], silu_z[:, p, bass.ds(g * G, G)], ALU.mult
                                      ).then_inc(hs_done[p], 1)

            flat = lambda t: t[:].rearrange("p k e -> p (k e)")

            def statistics(g, src, st, mv, ve, st_s, mv_s, ve_s):
                for k in range(NC):
                    i = dve.bn_stats(st[:, k], src[:, k])
                i.then_inc(st_s, 1)
                dve.wait_ge(st_s, g + 1)
                alone(dve)
                for k in range(NC):
                    i = dve.bn_aggr(mv[:, k], st[:, k])
                i.then_inc(mv_s, 1)
                dve.wait_ge(mv_s, g + 1)
                dve.tensor_scalar(ve[:], mv[:, :, 1], EPS_LN, None, ALU.add).then_inc(ve_s, 1)

            def normalise(dst, src, mv, rs, s):
                for k in range(NC):
                    i = dve.tensor_scalar(dst[:, k], src[:, k], mv[:, k, 0:1], rs[:, k:k + 1], ALU.subtract, ALU.mult)
                i.then_inc(s, 1)

            def mixer_out(g):
                dve.wait_ge(down_mm, g + 1)
                dve.wait_ge(x_res_in, 16 * (g + 1))
                dve.tensor_tensor(flat(y1), bank[3][:], flat(x_res), ALU.add).then_inc(y1_done, 1)
                dve.wait_ge(y1_done, g + 1)
                statistics(g, y1, st1, mv1, ve1, st1_done, mv1_done, ve1_done)

            def mixer_norm(g):
                dve.wait_ge(rs1_done, g + 1)
                normalise(Y, y1, mv1, rs1, Y_done)

            def mix(g, f):
                for p in range(NP):
                    key_evac(g, p)
                for i in range(2):
                    val_evac(g, i)
                if f is not None:
                    routing(f)
                for j in range(NJ + 1):
                    if f is not None:
                        ffn_slot(f, j)
                    for what, arg in DVE_SLOT.get(j, ()):
                        {"C": weigh_scores, "K": weigh_keys, "S": update_state}[what](g, arg) if arg is not None \
                            else {"R": head_scale, "H": gate_heads, "O": mixer_out}[what](g)
                if f is not None:
                    ffn_tail(f)
                mixer_norm(g)

            def routing(f):
                step = [0]

                def then(ins):
                    step[0] += 1
                    ins.then_inc(route, 1)
                    dve.wait_ge(route, f * ROUTE + step[0])
                    if step[0] in (2, 4):
                        alone(dve)

                dve.wait_ge(ge_done, f + 1)
                then(dve.tensor_scalar(ge1[:], ge[:], 1.0, None, ALU.add))
                then(dve.reciprocal(gext[:, :, 0:NX], ge1[:]))
                for k in range(NC):
                    i = dve.max(top[:, k], gext[:, k])
                then(i)
                then(dve.memset(top[:, :, TOPK:8], -1.0))
                for k in range(NC):
                    i = dve.match_replace(rest[:, k], top[:, k], gext[:, k], 0.0)
                then(i)
                then(dve.tensor_tensor(chosen[:], gext[:, :, 0:NX], rest[:, :, 0:NX], ALU.subtract))
                then(dve.tensor_reduce(csum[:], chosen[:], AX.X, ALU.add))
                then(dve.reciprocal(crec[:], csum[:]))
                then(dve.tensor_tensor(comb[:], chosen[:], crec[:].unsqueeze(2).to_broadcast([P, NC, NX]), ALU.mult))
                then(dve.tensor_copy(comb3[:, :, 0], comb[:]))
                then(dve.tensor_tensor(comb_r[:, 0], comb[:], comb3[:, :, 0], ALU.subtract))
                then(dve.tensor_copy(comb3[:, :, 1], comb_r[:, 0]))
                then(dve.tensor_tensor(comb_r[:, 1], comb_r[:, 0], comb3[:, :, 1], ALU.subtract))
                dve.tensor_copy(comb3[:, :, 2], comb_r[:, 1]).then_inc(route, 1)
                assert step[0] + 1 == ROUTE

            def ffn_slot(f, j):
                dve.wait_ge(silu_done, nth(f, NJ + 1, j))
                dve.wait_ge(vin_mm, nth(f, NJ + 1, j))
                dst = h2 if j == 0 else h1
                dve.tensor_tensor(dst[:, j % 2], s_in[:, j % 2], bank[5][:], ALU.mult).then_inc(h1_done, 1)
                if j:
                    dve.wait_ge(h1_done, nth(f, NJ + 1, j))
                    dve.wait_ge(bc_mm, nth(f, NJ, j - 1))
                    dve.tensor_tensor(h2[:, j % 2], h1[:, j % 2], bank[6][:], ALU.mult).then_inc(h2_done, 1)

            def ffn_tail(f):
                dve.wait_ge(ob_mm, f + 1)
                dve.tensor_tensor(flat(z2), bank[4][:], flat(Y), ALU.add).then_inc(z2_done, 1)
                dve.wait_ge(z2_done, f + 2)
                statistics(f, z2, st2, mv2, ve2, st2_done, mv2_done, ve2_done)
                dve.wait_ge(rs2_done, f + 1)
                prev(dve, out_stored, f, 16)
                normalise(out_sb, z2, mv2, rs2, out_done)

            def ffn(f):
                routing(f)
                for j in range(NJ + 1):
                    ffn_slot(f, j)
                ffn_tail(f)

            groups(dve, mix, ffn)

        @block.tensor
        def _(pe):
            pe.wait_ge(blocks_made, 1)
            pe.wait_ge(pool_const, 17)
            n8 = 2 * NH * NP
            for s in range(NP):
                q, k, v = (qkv_block[:, m, s] for m in range(3))
                c = slice(s * P, (s + 1) * P)
                pe.matmul(bank[0][:, c], k, q, start=True, stop=True)
                pe.matmul(bank[1][:, c], v, center[:], start=True, stop=True)
                pe.transpose(bank[2][:, c], w_up[:, c], ident[:])
                c8 = slice(s * 2 * NH, (s + 1) * 2 * NH)
                pe.matmul(bank[3][:, c8], q, w_gates[:, s], start=True, stop=False)
                pe.matmul(bank[3][:, c8], k, w_gates[:, NP + s], start=False, stop=True)
                pe.matmul(bank[3][:, n8 + s * 2 * NH:n8 + (s + 1) * 2 * NH], v, w_gates[:, 2 * NP + s], start=True, stop=True)
                pe.transpose(bank[3][:, 2 * n8 + s * 8:2 * n8 + (s + 1) * 8], rows[:, c], ident[0:8, 0:8])
            pe.transpose(bank[3][:, 3 * n8:3 * n8 + NX], gate_rows[:], ident[0:NX, 0:NX]).then_inc(fold1_mm, 1)
            pe.wait_ge(fold1_out, 1)
            for s in range(NP):
                pe.matmul(bank[4][:, s * P:(s + 1) * P], w_up_t[:, s], v_center[:, s], start=True, stop=True)
            for s in range(NP):
                i = pe.matmul(bank[4][:, INNER:INNER + 2 * NH], w_up_t[:, s], g_v[:, s], start=(s == 0), stop=(s == NP - 1))
            i.then_inc(fold2_mm, 1)
            pe.wait_ge(weights_ready, 1)

            def phase1_gates(b, f):
                pe.wait_ge(xact_done[f], b + 1)
                if not (isinstance(b, int) and b == 0):
                    pe.wait_ge(gate_out[f], b)
                for k in range(NC):
                    o, c = bank[5 + f][:, k * 2 * NH:(k + 1) * 2 * NH], slice(k * P, (k + 1) * P)
                    pe.matmul(o, x_t[:, f, c], g_x[:], start=True, stop=False)
                    for p in range(NP):
                        i = pe.matmul(o, xact[:, f, p, c], g_act[:, p], start=False, stop=(p == NP - 1))
                i.then_inc(gate_mm[f], 1)

            def phase1_xt(b, f):
                pe.wait_ge(x_loaded[f], 16 * (b + 1))
                if f:
                    pe.wait_ge(xt_out[0], b + 1)
                elif not (isinstance(b, int) and b == 0):
                    pe.wait_ge(xt_out[1], b)
                for k in range(NC):
                    i = pe.transpose(bank[0][:, k * P:(k + 1) * P], x_in[:, f, k], ident[:])
                i.then_inc(xt_mm[f], 1)

            def phase1_up(b, f, q):
                if f:
                    pe.wait_ge(up_out[0], b * 2 * NP + q + 1)
                elif not (isinstance(b, int) and b == 0):
                    pe.wait_ge(up_out[1], (b - 1) * 2 * NP + q + 1)
                pe.matmul(bank[1 + q][:], w_up[:, q * P:(q + 1) * P], x_t[:, f], start=True, stop=True
                          ).then_inc(up_mm[f], 1)

            def phase1(b):
                first, last = isinstance(b, int) and b == 0, isinstance(b, int) and b == B - 1
                for f in range(HALVES):
                    if f == 0:
                        phase1_xt(b, 1)
                    elif not last:
                        phase1_xt(b + 1, 0)
                    pe.wait_ge(xt_out[f], b + 1)
                    for q in range(NP):
                        phase1_up(b, f, q)
                    if f == 1:
                        phase1_gates(b, 0)
                    elif not first:
                        phase1_gates(b - 1, 1)
                    for q in range(NP, 2 * NP):
                        phase1_up(b, f, q)

            phase1_xt(0, 0)
            phase1(0)
            with pe.Fori(1, B - 1) as b:
                phase1(b)
            phase1(B - 1)
            phase1_gates(B - 1, 1)

            for f in range(HALVES):
                pe.wait_ge(gate_out[f], B)
            for c in range(CS):
                for t in range(2):
                    i = pe.transpose(bank[2 * t + c // 4][0:R, (c % 4) * P:(c % 4 + 1) * P], gates[:, c, t], ident[:])
            i.then_inc(row_mm, 1)
            pe.wait_ge(dve_scan, 3)
            for n, src in enumerate((rows_a, rows_w, rows_floor)):
                if n:
                    pe.wait_ge(act_scan, 7 + n)
                for c in range(CS):
                    i = pe.transpose(bank[4 + n][:, c * R:(c + 1) * R], src[:, c * P:(c + 1) * P], ident[0:R, 0:R])
                i.then_inc(back_mm, 1)

            def mix_front(g):
                pe.wait_ge(x_new_in, 16 * (g + 1))
                prev(pe, state_done[NC - 1], g)
                for k in range(NC):
                    i = pe.transpose(bank[0][:, k * P:(k + 1) * P], x_new[:, k], ident[:])
                i.then_inc(xT_mm, 1)
                pe.wait_ge(xa_in, 16 * (g + 1))
                for p in range(NP):
                    prev(pe, mixed_done[p], g)
                    pe.matmul(bank[1 + p][:], w_key[:, p], xa[:, p], start=True, stop=True).then_inc(key_mm[p], 1)
                pe.wait_ge(xT_out, g + 1)
                prev(pe, y1_done, g)
                for i in range(2):
                    for k in range(2):
                        c = 2 * i + k
                        ins = pe.matmul(bank[3 if i == 0 else 0][:, k * INNER:(k + 1) * INNER],
                                        xT2[:, c * P:(c + 1) * P], w_val[:], start=True, stop=True)
                    ins.then_inc(val_mm[i], 1)

            def scores(g, kp):
                for p in range(NP):
                    if kp == 0:
                        pe.wait_ge(key_out[p], g + 1)
                for par in range(2):
                    if kp:
                        pe.wait_ge(C_done[0][par], g + 1)
                    r = slice(par * DH, (par + 1) * DH)
                    for k in range(2):
                        c = slice((2 * kp + k) * P, (2 * kp + k + 1) * P)
                        for p in range(NP):
                            i = pe.matmul(bank[1 + par][:, (k * NP + p) * P:(k * NP + p + 1) * P],
                                          keyT[r, p, c], xa[r, p, c], start=True, stop=True)
                    i.then_inc(score_mm[kp][par], 1)

            def key_tokens(g, kp):
                pe.wait_ge(state_done[1] if kp else val_out[1], g + 1)
                for k in range(2):
                    for p in range(NP):
                        i = pe.transpose(bank[0][:, k * INNER + p * P:k * INNER + (p + 1) * P],
                                         keyT[:, p, (2 * kp + k) * P:(2 * kp + k + 1) * P], ident[:])
                i.then_inc(keytok_mm[kp], 1)

            def chunk(g, k):
                kp, kk = k // 2, k % 2
                pe.wait_ge(u_out[k - 1] if k else val_out[0], g + 1)
                if k == 0:
                    pe.wait_ge(qs_done, g + 1)
                    pe.wait_ge(val_out[1], g + 1)
                    prev(pe, state_done[NC - 1], g)
                else:
                    pe.wait_ge(state_done[k - 1], g + 1)
                for par in range(2):
                    pe.wait_ge(C_done[kp][par], g + 1)
                c = slice(k * P, (k + 1) * P)
                for p in range(NP):
                    o = bank[3][:, p * 2 * DV:(p + 1) * 2 * DV]
                    pe.matmul(o, qs[:, p, c], state[:, p], start=True, stop=False, skip_group_check=True)
                    for par in range(2):
                        i = pe.matmul(o[:, par * DV:(par + 1) * DV], C[:, par, kk, p], vals[:, k, 2 * p + par],
                                      start=False, stop=True, skip_group_check=True)
                i.then_inc(u_mm[k], 1)
                pe.wait_ge(state_done[k - 1] if kk else keytok_out[kp], g + 1)
                for p in range(NP):
                    i = pe.matmul(bank[0][:, p * 2 * DV:(p + 1) * 2 * DV], keys[:, kk, p * P:(p + 1) * P],
                                  vals[:, k, 2 * p:2 * p + 2].rearrange("p h d -> p (h d)"), start=True, stop=True)
                i.then_inc(upd_mm[k], 1)

            def head_transposes(g):
                pe.wait_ge(hn_done, g + 1)
                for p in range(NP):
                    pe.wait_ge(C_done[1][p], g + 1)
                    for k in range(NC):
                        i = pe.transpose(bank[1 + p][:, k * P:(k + 1) * P], hn[:, k, p * P:(p + 1) * P], ident[:])
                    i.then_inc(hnT_mm[p], 1)

            def down(g):
                pe.wait_ge(u_out[NC - 1], g + 1)
                for p in range(NP):
                    pe.wait_ge(hs_done[p], g + 1)
                for k in range(NC):
                    for p in range(NP):
                        i = pe.matmul(bank[3][:, k * P:(k + 1) * P], hs[:, p, k * P:(k + 1) * P], w_down[:, p],
                                      start=(p == 0), stop=(p == NP - 1))
                i.then_inc(down_mm, 1)

            def ffn_head(f):
                pe.wait_ge(Y_done, f + 1)
                prev2(pe, z2_done, f)
                for k in range(NC):
                    i = pe.transpose(bank[7][:, k * P:(k + 1) * P], Y[:, k], ident[:])
                i.then_inc(yT_mm, 1)
                pe.wait_ge(yT_out, f + 1)
                for k in range(NC):
                    i = pe.matmul(bank[6][:, k * NX:(k + 1) * NX], yT[:, k * P:(k + 1) * P], w_gate[:], start=True, stop=True)
                i.then_inc(logit_mm, 1)

            def ffn_in(f, j):
                if j:
                    pe.wait_ge(silu_done, nth(f, NJ + 1, j - 1))
                w = wsin[:] if j == 0 else ewin[:, 2 * j - 2:2 * j].rearrange("p e h -> p (e h)")
                pe.matmul(bank[4][:], w, yT[:], start=True, stop=True).then_inc(hin_mm, 1)
                if j:
                    pe.wait_ge(h1_done, nth(f, NJ + 1, j - 1))
                w = vsin[:] if j == 0 else evin[:, 2 * j - 2:2 * j].rearrange("p e h -> p (e h)")
                pe.matmul(bank[5][:], w, yT[:], start=True, stop=True).then_inc(vin_mm, 1)

            def combine_transposes(f):
                pe.wait_ge(route, (f + 1) * ROUTE)
                pe.wait_ge(ge_done, f + 1)
                for k in range(NC):
                    i = pe.transpose(bank[6][:, k * P // 2:(k + 1) * P // 2].bitcast(BF16),
                                     comb3[:, k].rearrange("p t e -> p (t e)"), ident_bf[:])
                i.then_inc(combT_mm, 1)

            def combine_rows(f, j):
                if j > 1:
                    pe.wait_ge(h2_done, nth(f, NJ, j - 2))
                else:
                    pe.wait_ge(combT_out, f + 1)
                pe.matmul(bank[6][:], pair_rows[:, j - 1], combT[:], start=True, stop=True).then_inc(bc_mm, 1)

            def ffn_out(f, j):
                if j:
                    pe.wait_ge(h2_done, nth(f, NJ, j - 1))
                else:
                    pe.wait_ge(h1_done, nth(f, NJ + 1, 0))
                w = ewout[:, j - 1] if j else wsout[:]
                i = pe.matmul(bank[7][:], w, h2[:, j % 2], start=(j == 0), stop=(j == NJ))
                if j == NJ:
                    i.then_inc(o_mm, 1)

            def ffn_back(f):
                pe.wait_ge(oT_out, f + 1)
                pe.wait_ge(silu_done, nth(f, NJ + 1, NJ))
                for k in range(NC):
                    i = pe.transpose(bank[4][:, k * P:(k + 1) * P], oT[:, k * P:(k + 1) * P], ident[:])
                i.then_inc(ob_mm, 1)

            def mix(g, f):
                mix_front(g)
                if f is not None:
                    ffn_head(f)
                    ffn_in(f, 0)
                for what, arg in PE_START:
                    {"S": scores, "K": key_tokens}[what](g, arg)
                for j in range(NJ + 1):
                    if f is not None and j:
                        ffn_in(f, j)
                        if j == 1:
                            combine_transposes(f)
                        combine_rows(f, j)
                        ffn_out(f, j - 1)
                    for what, arg in PE_SLOT.get(j, ()):
                        {"S": scores, "K": key_tokens, "C": chunk}[what](g, arg) if arg is not None \
                            else {"H": head_transposes, "D": down}[what](g)
                if f is not None:
                    ffn_out(f, NJ)
                    ffn_back(f)

            def ffn(f):
                ffn_head(f)
                ffn_in(f, 0)
                for j in range(1, NJ + 1):
                    ffn_in(f, j)
                    if j == 1:
                        combine_transposes(f)
                    combine_rows(f, j)
                    ffn_out(f, j - 1)
                ffn_out(f, NJ)
                ffn_back(f)

            pe.wait_ge(back_out, BACK)
            pe.wait_ge(phase2_const, 5)
            pe.wait_ge(ffn_w_in, 16 * FFN_DMAS)
            groups(pe, mix, ffn)


PE_START = (("S", 0), ("K", 0))
PE_SLOT = {1: (("C", 0),), 2: (("C", 1), ("S", 1), ("K", 1)), 3: (("C", 2),), 4: (("C", 3),),
           6: (("H", None),), 8: (("D", None),)}
DVE_SLOT = {0: (("C", 0), ("K", 0)), 1: (("S", 0),), 2: (("S", 1), ("C", 1), ("K", 1)), 3: (("S", 2),), 4: (("S", 3), ("R", None)),
            6: (("H", None),), 8: (("O", None),)}
U_SLOT = {1: (0,), 2: (1,), 3: (2,), 4: (3,)}
DVE_SCAN = 10
ACT_SCAN = 11
BACK = 3
ROUTE = 14


_INS = ['L0_attn_x', 'L0_attn_W_up', 'L0_attn_conv_w', 'L0_attn_conv_b', 'L0_attn_Wq', 'L0_attn_Wk', 'L0_attn_Wv',
        'L0_attn_W_ig', 'L0_attn_b_ig', 'L0_attn_W_fg', 'L0_attn_b_fg', 'L0_attn_norm_w', 'L0_attn_skip',
        'L0_attn_W_down', 'L0_ffn_gate_w', 'L0_ffn_ws_in', 'L0_ffn_vs_in', 'L0_ffn_ws_out', 'L0_ffn_e_win',
        'L0_ffn_e_vin', 'L0_ffn_e_wout']
_OUTS = [((8, 1024, 128), 'float32')]


def kernel(**inputs):
    import numpy as _np
    import concourse.bacc as _bacc
    from concourse import mybir as _mybir
    from concourse.bass_utils import run_bass_kernel_spmd as _run

    nc = _bacc.Bacc("TRN2", target_bir_lowering=False, num_devices=1)
    arrays, args = {}, []
    for name in _INS:
        a = _np.ascontiguousarray(inputs[name])
        arrays[f"in_{name}_dram"] = a
        args.append(nc.dram_tensor(f"in_{name}_dram", a.shape, _mybir.dt.from_np(a.dtype), kind="ExternalInput").ap())
    for i, (shape, dtype) in enumerate(_OUTS):
        dt = _mybir.dt.from_np(_np.dtype(dtype))
        args.append(nc.dram_tensor(f"out_{i}_dram", shape, dt, kind="ExternalOutput").ap())
    mixer_moe_block(nc, *args)
    r = _run(nc, [arrays], core_ids=[0])
    return r.results[0]["out_0_dram"]
```

```python
from contextlib import ExitStack

import concourse.bass as bass
from concourse import mybir

F32 = mybir.dt.float32
F32R = mybir.dt.float32r
BF16 = mybir.dt.bfloat16
ALU = mybir.AluOpType
ACT = mybir.ActivationFunctionType
AX = mybir.AxisListType

P = 128
EPS_MIX = 1e-6
EPS_LN = 1e-5
NEG = -1e30


def mixer_moe_block(nc, x, W_up, conv_w, conv_b, Wq, Wk, Wv, W_ig, b_ig, W_fg, b_fg, norm_w, skip,
                    W_down, gate_w, ws_in, vs_in, ws_out, e_win, e_vin, e_wout, out):
    B, S, E = x.shape
    INNER = W_up.shape[1] // 2
    NH = b_ig.shape[0]
    DH = INNER // NH
    DV = DH + 1
    TAPS = conv_w.shape[0]
    HALO = TAPS - 1
    NP = INNER // P
    NX, _, HX = e_win.shape
    NJ = NX * HX // P
    TOPK = 4
    G = 512
    NC = G // P
    HALVES = S // G
    NG = B * HALVES
    CS = S // P
    R = B * NH
    QD = Wq.shape[1]
    assert E == P and INNER == 2 * P and DH == 64 and NH == 4 and HX == 64 and HALVES == 2

    x_g = x.rearrange("b (f k p) e -> (b f) p k e", f=HALVES, p=P)
    out_g = out.rearrange("b (f k p) e -> (b f) p k e", f=HALVES, p=P)
    xact_d = nc.dram_tensor("xact_scratch", [NG, P, NP * G], F32).ap()
    max_d = nc.dram_tensor("max_scratch", [NG, NH, G], F32).ap()
    inter_d = nc.dram_tensor("inter_scratch", [NG, NH, G], F32).ap()
    decay_d = nc.dram_tensor("decay_scratch", [NH, B, CS], F32).ap()

    with ExitStack() as ctx:
        def sb(name, shape, dt=F32):
            return ctx.enter_context(nc.sbuf_tensor(name, shape, dt))

        def sem(name):
            return ctx.enter_context(nc.semaphore(name))

        def sems(name, *counts):
            if not counts:
                return sem(name)
            return [sems(f"{name}_{i}", *counts[1:]) for i in range(counts[0])]

        bank = [ctx.enter_context(nc.psum_tensor(f"bank{i}", [P, 512], F32)) for i in range(8)]

        ident = sb("ident", [P, P])
        ident_bf = sb("ident_bf", [P, P], BF16)
        block_mask = sb("block_mask", [P, P])
        center = sb("center", [P, P])
        pair_rows = sb("pair_rows", [3 * NX, NJ, P], BF16)
        w_up = sb("w_up", [P, 2 * INNER])
        qkv_small = sb("qkv_small", [P, 3, NP, QD])
        qkv_block = sb("qkv_block", [P, 3, NP, P])
        w_gates = sb("w_gates", [P, 3 * NP, 2 * NH])
        rows = sb("rows", [8, INNER])
        vecs = sb("vecs", [P, NP, 8])
        VB, VN, VS = TAPS, TAPS + 1, TAPS + 2
        b_i = sb("b_i", [R, 1])
        b_f = sb("b_f", [R, 1])
        gate_rows = sb("gate_rows", [NX, P])
        w_gate = sb("w_gate", [P, NX])
        w_down = sb("w_down", [P, NP, E])
        in_hi = sb("in_hi", [P, 2, NJ + 1, P], F32R)
        in_lo = sb("in_lo", [P, 2, NJ + 1, P], F32R)
        ewout = sb("ewout", [P, NJ, E])
        wsout = sb("wsout", [P, P])
        w_key = sb("w_key", [P, NP, P])
        g_act = sb("g_act", [P, NP, 2 * NH])
        g_x = sb("g_x", [P, 2 * NH])
        g_v = sb("g_v", [P, NP, 2 * NH])
        v_center = sb("v_center", [P, NP, P])
        w_up_t = sb("w_up_t", [P, NP, P])
        w_val = sb("w_val", [P, INNER])

        silu_z = sb("silu_z", [P, NP, B * S])
        a_tok = sb("a_tok", [P, B, HALVES, NC, NH])
        w_tok = sb("w_tok", [P, B, HALVES, NC, NH])
        floor_tok = sb("floor_tok", [P, B, HALVES, NC, NH])
        decay = sb("decay", [P, NP, B * CS])

        mixer_w_in = sem("mixer_w_in")
        ffn_w_in = sem("ffn_w_in")
        pool_const = sem("pool_const")
        blocks_made = sem("blocks_made")
        fold1_mm = sem("fold1_mm")
        fold1_out = sem("fold1_out")
        fold2_mm = sem("fold2_mm")
        weights_ready = sem("weights_ready")
        in_split = sem("in_split")

        waited = sem("waited")

        block = ctx.enter_context(nc.Block())
        MIXER_DMAS = 18
        FFN_DMAS = 6

        p1 = ExitStack()

        def sb1(name, shape, dt=F32):
            return p1.enter_context(nc.sbuf_tensor(name, shape, dt))

        in_w = sb1("in_w", [P, 2, NJ + 1, P])
        x_in = sb1("x_in", [P, HALVES, NC, E])
        x_t = sb1("x_t", [P, HALVES, G])
        xm = sb1("xm", [P, HALVES, NP, HALO + G])
        acc = sb1("acc", [P, HALVES, NP, G])
        xact = sb1("xact", [P, HALVES, NP, G])
        gates = sb1("gates", [P, CS, 2, R])
        pre_i = sb1("pre_i", [R, S])
        min_f = sb1("min_f", [R, S])
        abs_f = sb1("abs_f", [R, S])
        exp_f = sb1("exp_f", [R, S])
        log_f = sb1("log_f", [R, S])
        lfc = sb1("lfc", [R, S])
        run_max = sb1("run_max", [R, S])
        before = sb1("before", [R, CS])
        rows_a = sb1("rows_a", [R, S])
        rows_w = sb1("rows_w", [R, S])
        rows_floor = sb1("rows_floor", [R, S])
        rows_inter = sb1("rows_inter", [R, S])
        rows_decay = sb1("rows_decay", [R, CS])
        p1.close()

        x_loaded = sems("x_loaded", HALVES)
        xt_mm = sems("xt_mm", HALVES)
        xt_out = sems("xt_out", HALVES)
        up_mm = sems("up_mm", HALVES)
        up_out = sems("up_out", HALVES)
        halo_done = sem("halo_done")
        tap_done = sems("tap_done", HALVES)
        xact_done = sems("xact_done", HALVES)
        xact_stored = sems("xact_stored", HALVES)
        gate_mm = sems("gate_mm", HALVES)
        gate_out = sems("gate_out", HALVES)
        row_mm = sem("row_mm")
        act_scan = sem("act_scan")
        dve_scan = sem("dve_scan")
        back_mm = sem("back_mm")
        back_out = sem("back_out")
        max_stored = sem("max_stored")
        rows_stored = sem("rows_stored")
        decay_in = sem("decay_in")

        xa = sb("xa", [P, NP, G])
        x_new = sb("x_new", [P, NC, E])
        xT2 = sb("xT2", [P, G])
        keyT = sb("keyT", [P, NP, G])
        vals = sb("vals", [P, NC, NH, DV])
        max_b = sb("max_b", [P, NH, G])
        D = sb("D", [P, 2, 2, 2, NP, P])
        C = sb("C", [P, 2, 2, NP, P])
        inter_w = sb("inter_w", [P, NP, G])
        x_res = sb("x_res", [P, NC, E])
        keys = sb("keys", [P, 2, INNER])
        qs = sb("qs", [P, NP, G])
        state = sb("state", [P, NP, 2 * DV])
        kept = sb("kept", [P, NP, 2 * DV])
        u_sb = sb("u_sb", [P, NC, NH, DV])
        sq = sb("sq", [P, 2, NH, DH])
        ssq = sb("ssq", [P, NC, NH])
        nrm = sb("nrm", [P, NC, NH])
        nrm1 = sb("nrm1", [P, NC, NH])
        nrm2 = sb("nrm2", [P, NC, NH])
        var_h = sb("var_h", [P, NC, NH])
        r_h = sb("r_h", [P, NC, NH])
        half = sb("half", [P, NC * NH])
        hn = sb("hn", [P, NC, INNER])
        mixed = sb("mixed", [P, NP, G])
        y1 = sb("y1", [P, NC, E])
        st1 = sb("st1", [P, NC, 6])
        mv1 = sb("mv1", [P, NC, 2])
        ve1 = sb("ve1", [P, NC])
        rs1 = sb("rs1", [P, NC])
        Y = sb("Y", [P, NC, E])
        yT = sb("yT", [P, G])
        yT_hi = sb("yT_hi", [P, G], F32R)
        yT_lo = sb("yT_lo", [P, G], F32R)
        ge = sb("ge", [P, NC, NX])
        ge1 = sb("ge1", [P, NC, NX])
        gext = sb("gext", [P, NC, NX + TOPK])
        top = sb("top", [P, NC, 8])
        rest = sb("rest", [P, NC, NX + TOPK])
        chosen = sb("chosen", [P, NC, NX])
        csum = sb("csum", [P, NC])
        crec = sb("crec", [P, NC])
        comb = sb("comb", [P, NC, NX])
        comb_r = sb("comb_r", [P, 2, NC, NX])
        comb3 = sb("comb3", [P, NC, P // NX, NX], BF16)
        combT = sb("combT", [3 * NX, G], BF16)
        s_in = sb("s_in", [P, 2, G])
        h1 = sb("h1", [P, 2, G])
        h2 = sb("h2", [P, 2, G])
        oT = sb("oT", [P, G])
        z2 = sb("z2", [P, NC, E])
        st2 = sb("st2", [P, NC, 6])
        mv2 = sb("mv2", [P, NC, 2])
        ve2 = sb("ve2", [P, NC])
        rs2 = sb("rs2", [P, NC])
        out_sb = sb("out_sb", [P, NC, E])

        LOADS = ("xa_in", "x_new_in", "x_res_in", "max_in")
        xa_in, x_new_in, x_res_in, max_in = (sem(n) for n in LOADS)
        inter_in = sem("inter_in")
        out_stored = sem("out_stored")
        phase2_const = sem("phase2_const")
        arg_sub = sem("arg_sub")
        arg_masked = sem("arg_masked")
        D_done = sem("D_done")
        xT_mm, xT_out = sem("xT_mm"), sem("xT_out")
        key_mm, key_out = sems("key_mm", NP), sems("key_out", NP)
        val_mm, val_out = sems("val_mm", 2), sems("val_out", 2)
        qs_done = sem("qs_done")
        skip_done = sem("skip_done")
        score_mm, C_done = sems("score_mm", 2, 2), sems("C_done", 2, 2)
        keytok_mm, keytok_out = sems("keytok_mm", 2), sems("keytok_out", 2)
        u_mm, u_out = sems("u_mm", NC), sems("u_out", NC)
        upd_mm, kept_done, state_done = sems("upd_mm", NC), sems("kept_done", NC), sems("state_done", NC)
        sq_done, ssq_done = sem("sq_done"), sem("ssq_done")
        nrm_done = sems("nrm_done", 4)
        rh_done = sem("rh_done")
        hn_done = sem("hn_done")
        hnT_mm, mixed_done, hs_done = sems("hnT_mm", NP), sems("mixed_done", NP), sems("hs_done", NP)
        down_mm = sem("down_mm")
        y1_done, st1_done, mv1_done, ve1_done = sem("y1_done"), sem("st1_done"), sem("mv1_done"), sem("ve1_done")
        rs1_done = sem("rs1_done")
        Y_done = sem("Y_done")
        yT_mm, yT_out = sem("yT_mm"), sem("yT_out")
        yT_hi_done, yT_lo_done = sem("yT_hi_done"), sem("yT_lo_done")
        logit_mm, ge_done = sem("logit_mm"), sem("ge_done")
        route = sem("route")
        combT_mm, combT_out = sem("combT_mm"), sem("combT_out")
        hin_mm, vin_mm = sem("hin_mm"), sem("vin_mm")
        silu_done, h1_done = sem("silu_done"), sem("h1_done")
        bc_mm, h2_done = sem("bc_mm"), sem("h2_done")
        o_mm = sem("o_mm")
        oT_out, ob_mm = sem("oT_out"), sem("ob_mm")
        z2_done, st2_done, mv2_done, ve2_done = sem("z2_done"), sem("st2_done"), sem("mv2_done"), sem("ve2_done")
        rs2_done = sem("rs2_done")
        out_done = sem("out_done")

        def nth(g, per, i):
            return g * per + i + 1

        def alone(eng):
            eng.sem_inc(waited, 1)

        def groups(eng, mix, ffn):
            mix(0, None)
            with eng.Fori(1, NG - 1) as g:
                mix(g, g - 1)
            mix(NG - 1, NG - 2)
            ffn(NG - 1)

        def prev(eng, s, g, per=1):
            if isinstance(g, int) and g == 0:
                return
            eng.wait_ge(s, g * per)

        def prev2(eng, s, f):
            eng.wait_ge(s, f + 1)

        @block.sync
        def _(sp):
            n = [0]

            def load(dst, src, s):
                n[0] += 1
                sp.dma_start(dst, src).then_inc(s, 16)

            for f in range(HALVES):
                load(x_in[:, f], x_g[f], x_loaded[f])
            n[0] = 0
            load(w_up[:], W_up, mixer_w_in)
            for m, w in enumerate((Wq, Wk, Wv)):
                for s in range(NP):
                    load(qkv_small[:, m, s, :], w[s * (P // QD):(s + 1) * (P // QD)].rearrange("b o d -> (b o) d"), mixer_w_in)
            load(w_gates[:, :, 0:NH], W_ig.rearrange("(s p) h -> p s h", p=P), mixer_w_in)
            load(w_gates[:, :, NH:2 * NH], W_fg.rearrange("(s p) h -> p s h", p=P), mixer_w_in)
            load(rows[0:TAPS, :], conv_w, mixer_w_in)
            for i, v in ((VB, conv_b), (VN, norm_w), (VS, skip), (VS + 1, skip)):
                load(rows[i:i + 1, :], v.rearrange("(a n) -> a n", a=1), mixer_w_in)
            load(gate_rows[:], gate_w, mixer_w_in)
            load(b_i[:], b_ig.rearrange("(h a) -> h a", a=1).partition_broadcast(B), mixer_w_in)
            load(b_f[:], b_fg.rearrange("(h a) -> h a", a=1).partition_broadcast(B), mixer_w_in)
            load(w_down[:], W_down.rearrange("(s p) e -> p s e", p=P), mixer_w_in)
            assert n[0] == MIXER_DMAS, n[0]
            for m, (w, w_shared) in enumerate(((e_win, ws_in), (e_vin, vs_in))):
                load(in_w[:, m, 1:].rearrange("p j (t h) -> p (j t) h", h=HX), w.rearrange("e d h -> d e h"), ffn_w_in)
                load(in_w[:, m, 0], w_shared, ffn_w_in)
            load(ewout[:], e_wout.rearrange("(j t) h d -> (t h) j d", t=P // HX), ffn_w_in)
            load(wsout[:], ws_out, ffn_w_in)
            assert n[0] == MIXER_DMAS + FFN_DMAS

            def store_xact(b, f):
                sp.wait_ge(xact_done[f], b + 1)
                sp.dma_start(xact_d[HALVES * b + f], xact[:, f]).then_inc(xact_stored[f], 16)

            def phase1(b):
                first, last = isinstance(b, int) and b == 0, isinstance(b, int) and b == B - 1
                for f in range(HALVES):
                    if not last:
                        sp.wait_ge(xt_mm[f], b + 1)
                        sp.dma_start(x_in[:, f], x_g[HALVES * b + HALVES + f]).then_inc(x_loaded[f], 16)
                    if f == 1:
                        store_xact(b, 0)
                    elif not first:
                        store_xact(b - 1, 1)

            phase1(0)
            with sp.Fori(1, B - 1) as b:
                phase1(b)
            phase1(B - 1)
            store_xact(B - 1, 1)

            def load_max(g):
                sp.dma_start(max_b[:], max_d[g].rearrange("h t -> (h t)").partition_broadcast(P)).then_inc(max_in, 16)

            def load_inter(g):
                for par in range(2):
                    sp.dma_start(inter_w[par * DH:(par + 1) * DH],
                                 inter_d[g].rearrange("(p two) t -> two p t", two=2)[par].partition_broadcast(DH)
                                 ).then_inc(inter_in, 16)

            def load_xa(g):
                sp.dma_start(xa[:], xact_d[g].rearrange("p (s t) -> p s t", s=NP)).then_inc(xa_in, 16)

            for f in range(HALVES):
                sp.wait_ge(xact_stored[f], 16 * B)
                sp.wait_ge(gate_out[f], B)
            sp.wait_ge(in_split, 4)
            sp.dma_start(x_new[:], x_g[0]).then_inc(x_new_in, 16)
            load_xa(0)

            half_of = lambda t: t.rearrange("(b f) h t -> f b h t", f=HALVES)
            sp.wait_ge(dve_scan, SCAN_MAX)
            for f in range(HALVES):
                sp.dma_start(half_of(max_d)[f], run_max[:, f * G:(f + 1) * G]).then_inc(max_stored, 16)
            sp.wait_ge(act_scan, SCAN_INTER)
            for f in range(HALVES):
                sp.dma_start(half_of(inter_d)[f], rows_inter[:, f * G:(f + 1) * G]).then_inc(rows_stored, 16)
            sp.dma_start(decay_d.rearrange("h b c -> b h c"), rows_decay[:]).then_inc(rows_stored, 16)
            sp.wait_ge(max_stored, 16 * HALVES)
            load_max(0)
            sp.wait_ge(rows_stored, 16 * (HALVES + 1))
            sp.wait_ge(dve_scan, DVE_SCAN)
            load_inter(0)
            for par in range(2):
                for p in range(NP):
                    sp.dma_start(decay[par * DH:(par + 1) * DH, p, :],
                                 decay_d[2 * p + par].rearrange("b c -> (b c)").partition_broadcast(DH)
                                 ).then_inc(decay_in, 16)
            sp.dma_start(x_res[:], x_g[0]).then_inc(x_res_in, 16)

            def mix(g, f):
                sp.wait_ge(arg_sub, nth(g, 4, 3))
                if not (isinstance(g, int) and g == NG - 1):
                    load_max(g + 1)
                    sp.wait_ge(xT_mm, g + 1)
                    sp.dma_start(x_new[:], x_g[g + 1]).then_inc(x_new_in, 16)
                    sp.wait_ge(qs_done, g + 1)
                    load_inter(g + 1)
                    sp.wait_ge(skip_done, g + 1)
                    sp.wait_ge(score_mm[1][1], g + 1)
                    load_xa(g + 1)
                if f is not None:
                    store(f)
                if not (isinstance(g, int) and g == NG - 1):
                    sp.wait_ge(y1_done, g + 1)
                    sp.dma_start(x_res[:], x_g[g + 1]).then_inc(x_res_in, 16)

            def store(f):
                sp.wait_ge(out_done, f + 1)
                sp.dma_start(out_g[f], out_sb[:]).then_inc(out_stored, 16)

            groups(sp, mix, store)
            sp.wait_ge(out_stored, 16 * NG)

        @block.gpsimd
        def _(pool):
            pool.memset(ident[:], 0.0).then_inc(pool_const, 1)
            pool.memset(ident_bf[:], 0.0).then_inc(pool_const, 1)
            pool.memset(block_mask[:], 1.0).then_inc(pool_const, 1)
            pool.memset(center[:], -1.0 / DH).then_inc(pool_const, 1)
            pool.memset(pair_rows[:], 0.0).then_inc(pool_const, 1)
            pool.wait_ge(pool_const, 5)
            for m in (ident, ident_bf):
                pool.affine_select(out=m[:], in_=m[:], compare_op=ALU.not_equal, fill=1.0, base=0,
                                   pattern=[[-1, P]], channel_multiplier=1).then_inc(pool_const, 1)
            bm = block_mask[:].rearrange("p (b d) -> p b d", d=QD)
            pool.affine_select(out=bm, in_=bm, compare_op=ALU.is_ge, fill=0.0, base=0,
                               pattern=[[-QD, P // QD], [0, QD]], channel_multiplier=1).then_inc(pool_const, 1)
            pool.affine_select(out=center[:, 0:DH], in_=center[:, 0:DH], compare_op=ALU.is_ge, fill=0.0,
                               base=DH - 1, pattern=[[0, DH]], channel_multiplier=-1).then_inc(pool_const, 1)
            pool.affine_select(out=center[:, DH:P], in_=center[:, DH:P], compare_op=ALU.is_ge, fill=0.0,
                               base=-DH, pattern=[[0, DH]], channel_multiplier=1).then_inc(pool_const, 1)
            pool.wait_ge(pool_const, 10)
            pool.affine_select(out=bm, in_=bm, compare_op=ALU.is_ge, fill=0.0, base=QD - 1,
                               pattern=[[QD, P // QD], [0, QD]], channel_multiplier=-1).then_inc(pool_const, 1)
            pool.tensor_tensor(center[:], center[:], ident[:], ALU.add).then_inc(pool_const, 1)
            halves = pair_rows[:].rearrange("r j (t m) -> r j t m", t=P // HX)
            for part in range(3):
                pool.affine_select(out=halves, in_=halves, compare_op=ALU.not_equal, fill=1.0, base=-NX * part,
                                   pattern=[[-2, NJ], [-1, 2], [0, HX]], channel_multiplier=1).then_inc(pool_const, 1)
                pool.wait_ge(pool_const, 13 + part)
            pool.memset(xm[:, 0, :, 0:HALO], 0.0).then_inc(pool_const, 1)

            pool.wait_ge(ffn_w_in, 16 * FFN_DMAS)
            for m in range(2):
                pool.tensor_copy(in_hi[:, m], in_w[:, m]).then_inc(in_split, 1)
            for m in range(2):
                pool.wait_ge(in_split, 1 + m)
                pool.tensor_tensor(in_lo[:, m], in_w[:, m], in_hi[:, m].bitcast(F32), ALU.subtract).then_inc(in_split, 1)

            for f in range(HALVES):
                pool.wait_ge(xact_stored[f], 16 * B)
                pool.wait_ge(gate_out[f], B)
            pool.memset(vals[:, :, :, DH:DV], 1.0).then_inc(phase2_const, 1)
            masked = pool.to_reg(NEG)

            def args(g, kp):
                if kp == 0:
                    pool.wait_ge(max_in, 16 * (g + 1))
                a_g = a_tok[:].rearrange("p b f k h -> p (b f) k h")[:, bass.ds(g, 1)].rearrange("p g k h -> p (g k) h")
                for par in range(2):
                    prev(pool, C_done[kp][par], g)
                    pool.tensor_tensor(
                        D[:, kp, par],
                        a_g.rearrange("p k (s two) -> p two k s", two=2)[:, par, 2 * kp:2 * kp + 2]
                        .unsqueeze(3).to_broadcast([P, 2, NP, P]),
                        max_b[:].rearrange("p (s two) (k t) -> p two k s t", two=2, k=NC)[:, par, 2 * kp:2 * kp + 2],
                        ALU.subtract).then_inc(arg_sub, 1)
                for par in range(2):
                    pool.wait_ge(arg_sub, nth(g, 4, 2 * kp + par))
                    alone(pool)
                    d = D[:, kp, par].rearrange("p k s t -> p (k s) t")
                    pool.affine_select(out=d, in_=d, compare_op=ALU.is_ge, fill=masked, base=0,
                                       pattern=[[0, 2 * NP], [1, P]], channel_multiplier=-1).then_inc(arg_masked, 1)

            def power(dst, src, s):
                pool.tensor_tensor(dst, src, half[:, 0:NC], ALU.pow).then_inc(s, 1)

            def mix(g, f):
                pool.wait_ge(xa_in, 16 * (g + 1))
                pool.wait_ge(inter_in, 32 * (g + 1))
                prev(pool, u_mm[NC - 1], g)
                pool.tensor_tensor(qs[:], xa[:], inter_w[:], ALU.mult).then_inc(qs_done, 1)
                prev(pool, down_mm, g)
                alone(pool)
                for p in range(NP):
                    i = pool.tensor_scalar(mixed[:, p], xa[:, p], vecs[:, p, VS:VS + 1], None, ALU.mult)
                i.then_inc(skip_done, 1)
                dec = decay[:].rearrange("p s (g k) -> p g k s", k=NC)[:, bass.ds(g, 1)].rearrange("p g k s -> p (g k) s")
                for k in range(NC):
                    if k:
                        pool.wait_ge(state_done[k - 1], g + 1)
                    else:
                        prev(pool, state_done[NC - 1], g)
                    pool.tensor_tensor(kept[:], state[:], dec[:, k, :].unsqueeze(2).to_broadcast([P, NP, 2 * DV]),
                                       ALU.mult).then_inc(kept_done[k], 1)
                    if k in (1, 2) and not (isinstance(g, int) and g == NG - 1):
                        args(g + 1, k - 1)
                for kp in range(2):
                    c = slice(2 * kp, 2 * kp + 2)
                    pool.wait_ge(nrm_done[3], nth(g, 2, kp))
                    pool.tensor_tensor(r_h[:, c].rearrange("p k h -> p (k h)"), var_h[:, c].rearrange("p k h -> p (k h)"),
                                       half[:, 0:2 * NH], ALU.pow).then_inc(rh_done, 1)
                    pool.wait_ge(rh_done, nth(g, 2, kp))
                    pool.tensor_tensor(hn[:, c].rearrange("p k (h d) -> p (k h) d", d=DH),
                                       u_sb[:, c].rearrange("p k h d -> p (k h) d")[:, :, 0:DH],
                                       r_h[:, c].rearrange("p k h -> p (k h)").unsqueeze(2).to_broadcast([P, 2 * NH, DH]),
                                       ALU.mult).then_inc(hn_done, 1)
                pool.wait_ge(ve1_done, g + 1)
                power(rs1[:], ve1[:], rs1_done)
                if f is not None:
                    ffn(f)

            def ffn(f):
                pool.wait_ge(ve2_done, f + 1)
                power(rs2[:], ve2[:], rs2_done)

            pool.wait_ge(back_out, 1)
            for kp in range(2):
                args(0, kp)
            pool.wait_ge(back_out, BACK)
            pool.memset(state[:], 0.0).then_inc(phase2_const, 1)
            pool.memset(gext[:, :, NX:NX + TOPK], -1.0).then_inc(phase2_const, 1)
            pool.memset(half[:], -0.5).then_inc(phase2_const, 1)
            pool.memset(comb3[:], 0.0).then_inc(phase2_const, 1)
            pool.wait_ge(decay_in, 16 * 2 * NP)
            pool.wait_ge(phase2_const, 5)
            groups(pool, mix, ffn)

        @block.scalar
        def _(act):
            def copy(dst, src):
                return act.activation(dst, src, ACT.Copy)

            def phase1_xact(b, f):
                if not (isinstance(b, int) and b == 0):
                    act.wait_ge(xact_stored[f], 16 * b)
                    act.wait_ge(gate_mm[f], b)
                for p in range(NP):
                    act.wait_ge(tap_done[f], b * NP * TAPS + HALO * NP + p + 1)
                    i = act.activation(xact[:, f, p], acc[:, f, p], ACT.Silu)
                i.then_inc(xact_done[f], 1)

            def phase1_xt(b, f):
                act.wait_ge(xt_mm[f], b + 1)
                if not (isinstance(b, int) and b == 0):
                    act.wait_ge(gate_mm[f], b)
                copy(x_t[:, f], bank[0][:]).then_inc(xt_out[f], 1)

            def phase1(b):
                first, last = isinstance(b, int) and b == 0, isinstance(b, int) and b == B - 1
                for f in range(HALVES):
                    if f == 1:
                        phase1_xact(b, 0)
                    elif not first:
                        phase1_xact(b - 1, 1)
                    if not first:
                        act.wait_ge(tap_done[f], b * NP * TAPS)
                    for p in range(NP):
                        act.wait_ge(up_mm[f], b * 2 * NP + p + 1)
                        copy(xm[:, f, p, HALO:], bank[1 + p][:]).then_inc(up_out[f], 1)
                    if f == 0:
                        phase1_xt(b, 1)
                        act.wait_ge(up_out[0], b * 2 * NP + NP)
                        copy(xm[:, 1, :, 0:HALO], xm[:, 0, :, G:G + HALO]).then_inc(halo_done, 1)
                    elif not last:
                        phase1_xt(b + 1, 0)
                    for p in range(NP):
                        act.wait_ge(up_mm[f], b * 2 * NP + NP + p + 1)
                        act.activation(silu_z[:, p, bass.ds(b * S + f * G, G)], bank[3 + p][:], ACT.Silu
                                       ).then_inc(up_out[f], 1)

            def mix_front(g):
                act.wait_ge(xT_mm, g + 1)
                prev(act, val_mm[1], g)
                copy(xT2[:], bank[0][:]).then_inc(xT_out, 1)
                for p in range(NP):
                    act.wait_ge(key_mm[p], g + 1)
                    prev(act, keytok_mm[1], g)
                    copy(keyT[:, p], bank[1 + p][:]).then_inc(key_out[p], 1)
                act.wait_ge(val_mm[0], g + 1)
                copy(vals[:, 0:2, :, 0:DH].rearrange("p k h d -> p (k h) d"),
                     bank[3][:].rearrange("p (q d) -> p q d", d=DH)).then_inc(val_out[0], 1)

            def decays(g):
                for q in range(4):
                    act.wait_ge(arg_masked, nth(g, 4, q))
                    d = D[:, q // 2, q % 2].rearrange("p k s t -> p (k s t)")
                    act.activation(d, d, ACT.Exp).then_inc(D_done, 1)

            def mix(g, f):
                if f is not None:
                    ffn_head(f)
                for j in range(NJ + 1):
                    if f is not None:
                        ffn_slot(f, j)
                    if j in U_SLOT:
                        k = U_SLOT[j]
                        act.wait_ge(u_mm[k], g + 1)
                        if k == 0:
                            prev(act, hn_done, g, 2)
                        copy(u_sb[:, k].rearrange("p h d -> p (h d)"), bank[3][:, 0:NH * DV]).then_inc(u_out[k], 1)
                        if k % 2:
                            c = slice(k - 1, k + 1)
                            act.wait_ge(u_out[k], g + 1)
                            if k == 1:
                                prev(act, ssq_done, g, 2)
                            else:
                                act.wait_ge(ssq_done, nth(g, 2, 0))
                            act.activation(sq[:].rearrange("p k h d -> p (k h) d"),
                                           u_sb[:, c].rearrange("p k h d -> p (k h) d")[:, :, 0:DH],
                                           ACT.Square).then_inc(sq_done, 1)
                last = isinstance(g, int) and g == NG - 1
                if not last:
                    decays(g + 1)
                if f is not None:
                    ffn_tail(f)
                if not last:
                    mix_front(g + 1)

            def ffn_head(f):
                act.wait_ge(yT_mm, f + 1)
                prev2(act, z2_done, f)
                copy(yT[:], bank[7][:]).then_inc(yT_out, 1)
                copy(yT_hi[:], bank[7][:]).then_inc(yT_hi_done, 1)
                act.wait_ge(logit_mm, f + 1)
                act.activation(ge[:].rearrange("p k e -> p (k e)"), bank[6][:, 0:NC * NX], ACT.Exp,
                               scale=-1.0).then_inc(ge_done, 1)

            def ffn_slot(f, j):
                act.wait_ge(hin_mm, nth(f, NJ + 1, j))
                if j >= 2:
                    act.wait_ge(h1_done, nth(f, NJ + 1, j - 2))
                act.activation(s_in[:, j % 2], bank[4][:], ACT.Silu).then_inc(silu_done, 1)
                if j == 2:
                    act.wait_ge(combT_mm, f + 1)
                    copy(combT[:], bank[6][0:3 * NX, 0:G // 2].bitcast(BF16)).then_inc(combT_out, 1)

            def ffn_tail(f):
                act.wait_ge(o_mm, f + 1)
                copy(oT[:], bank[7][:]).then_inc(oT_out, 1)

            def ffn(f):
                ffn_head(f)
                for j in range(NJ + 1):
                    ffn_slot(f, j)
                ffn_tail(f)

            phase1_xt(0, 0)
            phase1(0)
            with act.Fori(1, B - 1) as b:
                phase1(b)
            phase1(B - 1)
            phase1_xact(B - 1, 1)

            act.wait_ge(row_mm, 1)
            for c in range(2):
                act.activation(abs_f[:, c * 512:(c + 1) * 512], bank[2 + c][0:R, :], ACT.Abs, bias=b_f[:]).then_inc(act_scan, 1)
            act.wait_ge(act_scan, 2)
            act.activation(exp_f[:], abs_f[:], ACT.Exp, scale=-1.0).then_inc(act_scan, 1)
            act.wait_ge(act_scan, 3)
            act.activation(log_f[:], exp_f[:], ACT.Ln, bias=1.0).then_inc(act_scan, 1)
            mix_front(0)
            for n, rows in ((9, rows_inter), (10, rows_decay), (11, rows_w)):
                act.wait_ge(dve_scan, n)
                act.activation(rows[:], rows[:], ACT.Exp).then_inc(act_scan, 1)
            act.wait_ge(dve_scan, 12)
            act.activation(rows_floor[:], rows_floor[:], ACT.Exp, scale=-1.0).then_inc(act_scan, 1)

            decays(0)
            groups(act, mix, ffn)

        @block.vector
        def _(dve):
            dve.wait_ge(pool_const, 16)
            dve.wait_ge(mixer_w_in, 16 * MIXER_DMAS)
            mask = block_mask[:].rearrange("p (b d) -> p b d", d=QD)
            for m in range(3):
                for s in range(NP):
                    i = dve.tensor_tensor(qkv_block[:, m, s].rearrange("p (b d) -> p b d", d=QD), mask,
                                          qkv_small[:, m, s].unsqueeze(1).to_broadcast([P, P // QD, QD]), ALU.mult)
            i.then_inc(blocks_made, 1)
            dve.wait_ge(fold1_mm, 1)
            dve.tensor_scalar(w_key[:].rearrange("p s d -> p (s d)"), bank[0][:, 0:INNER], DH ** -0.5, None, ALU.mult)
            dve.tensor_copy(v_center[:].rearrange("p s d -> p (s d)"), bank[1][:, 0:INNER])
            dve.tensor_copy(w_up_t[:].rearrange("p s d -> p (s d)"), bank[2][:, 0:INNER])
            n8 = 2 * NH * NP
            dve.tensor_copy(g_act[:].rearrange("p s d -> p (s d)"), bank[3][:, 0:n8])
            dve.tensor_copy(g_v[:].rearrange("p s d -> p (s d)"), bank[3][:, n8:2 * n8])
            dve.tensor_copy(vecs[:].rearrange("p s d -> p (s d)"), bank[3][:, 2 * n8:3 * n8])
            dve.tensor_copy(w_gate[:], bank[3][:, 3 * n8:3 * n8 + NX]).then_inc(fold1_out, 1)
            dve.wait_ge(fold2_mm, 1)
            dve.tensor_copy(w_val[:], bank[4][:, 0:INNER])
            dve.tensor_copy(g_x[:], bank[4][:, INNER:INNER + 2 * NH]).then_inc(weights_ready, 1)

            def phase1_gates(b, f):
                dve.wait_ge(gate_mm[f], b + 1)
                dst = gates[:, f * NC:(f + 1) * NC].rearrange("p k t r -> p (k t) r")[:, :, bass.ds(b * NH, NH)]
                dve.tensor_copy(dst, bank[5 + f][:, 0:NC * 2 * NH].rearrange("p (k h) -> p k h", h=NH)
                                ).then_inc(gate_out[f], 1)

            def phase1(b):
                first = isinstance(b, int) and b == 0
                for f in range(HALVES):
                    for t in range(TAPS):
                        for p in range(NP):
                            a, src = acc[:, f, p], xm[:, f, p, t:t + G]
                            if t == 0:
                                dve.wait_ge(up_out[f], b * 2 * NP + p + 1)
                                if f == 1:
                                    dve.wait_ge(halo_done, b + 1)
                                if not first:
                                    dve.wait_ge(xact_done[f], b)
                                i = dve.tensor_scalar(a, src, vecs[:, p, 0:1], vecs[:, p, VB:VB + 1], ALU.mult, ALU.add)
                            else:
                                dve.wait_ge(tap_done[f], b * NP * TAPS + (t - 1) * NP + p + 1)
                                i = dve.scalar_tensor_tensor(a, src, vecs[:, p, t:t + 1], a, ALU.mult, ALU.add)
                            i.then_inc(tap_done[f], 1)
                    if f == 1:
                        phase1_gates(b, 0)
                    elif not first:
                        phase1_gates(b - 1, 1)

            phase1(0)
            with dve.Fori(1, B) as b:
                phase1(b)
            phase1_gates(B - 1, 1)

            dve.wait_ge(row_mm, 1)
            for c in range(2):
                dve.tensor_scalar(pre_i[:, c * 512:(c + 1) * 512], bank[c][0:R, :], b_i[:], None, ALU.add
                                  ).then_inc(dve_scan, 1)
            for c in range(2):
                dve.wait_ge(act_scan, c + 1)
                dve.tensor_scalar(min_f[:, c * 512:(c + 1) * 512], bank[2 + c][0:R, :], b_f[:], 0.0, ALU.add, ALU.min
                                  ).then_inc(dve_scan, 1)
            dve.wait_ge(dve_scan, 4)
            dve.wait_ge(act_scan, 4)
            dve.tensor_tensor_scan(lfc[:], min_f[:], log_f[:], 0.0, ALU.add, ALU.subtract).then_inc(dve_scan, 1)
            dve.wait_ge(dve_scan, 5)
            dve.tensor_tensor(rows_a[:], pre_i[:], lfc[:], ALU.subtract).then_inc(dve_scan, 1)
            dve.wait_ge(dve_scan, 6)
            dve.tensor_tensor_scan(run_max[:], rows_a[:], rows_a[:], -3e38, ALU.max, ALU.max).then_inc(dve_scan, 1)
            dve.memset(before[:, 0:1], NEG)
            dve.wait_ge(dve_scan, SCAN_MAX)
            ends = run_max[:].rearrange("r (c t) -> r c t", t=P)[:, :, P - 1]
            dve.tensor_copy(before[:, 1:CS], ends[:, 0:CS - 1]).then_inc(dve_scan, 1)
            chunks = lambda t: t[:].rearrange("r (c t) -> r c t", t=P)
            wide = lambda t: t.unsqueeze(2).to_broadcast([R, CS, P])
            dve.wait_ge(dve_scan, 8)
            dve.tensor_tensor(chunks(rows_inter), wide(before[:]), chunks(run_max), ALU.subtract).then_inc(dve_scan, 1)
            dve.tensor_tensor(rows_decay[:], before[:], ends, ALU.subtract).then_inc(dve_scan, 1)

            def back(i, dst):
                dve.wait_ge(back_mm, i + 1)
                d = dst[:].rearrange("p b f k h -> p b (f k) h")
                s = bank[4 + i][:, 0:CS * R].rearrange("p (c b h) -> p b c h", b=B, h=NH)
                if dst is floor_tok:
                    dve.tensor_scalar(d, s, EPS_MIX, None, ALU.add).then_inc(back_out, 1)
                else:
                    dve.tensor_copy(d, s).then_inc(back_out, 1)

            back(0, a_tok)
            dve.tensor_tensor(chunks(rows_w), chunks(rows_a), wide(ends), ALU.subtract).then_inc(dve_scan, 1)
            dve.tensor_tensor(rows_floor[:], lfc[:], run_max[:], ALU.add).then_inc(dve_scan, 1)
            back(1, w_tok)
            back(2, floor_tok)

            dve.sem_inc(z2_done, 1)
            all_tok = lambda t: t[:].rearrange("p b f k h -> p (b f) (k h)")

            def of_group(t, g):
                return all_tok(t)[:, bass.ds(g, 1)].rearrange("p g (k h) -> p (g k) h", h=NH)

            def val_evac(g):
                dve.wait_ge(val_mm[1], g + 1)
                dve.tensor_copy(vals[:, 2:4, :, 0:DH].rearrange("p k h d -> p (k h) d"),
                                bank[0][:].rearrange("p (q d) -> p q d", d=DH)).then_inc(val_out[1], 1)

            def weigh_scores(g, kp):
                for par in range(2):
                    dve.wait_ge(D_done, nth(g, 4, 2 * kp + par))
                    dve.wait_ge(score_mm[kp][par], g + 1)
                    if kp:
                        dve.wait_ge(u_mm[1], g + 1)
                    dve.tensor_tensor(C[:, par].rearrange("p k s t -> p (k s t)"), bank[1 + par][:],
                                      D[:, kp, par].rearrange("p k s t -> p (k s t)"), ALU.mult
                                      ).then_inc(C_done[kp][par], 1)

            def weigh_keys(g, kp):
                dve.wait_ge(keytok_mm[kp], g + 1)
                dve.tensor_tensor(keys[:].rearrange("p k (h d) -> p (k h) d", d=DH),
                                  bank[0][:].rearrange("p (q d) -> p q d", d=DH),
                                  of_group(w_tok, g)[:, 2 * kp:2 * kp + 2, :].rearrange("p k h -> p (k h)")
                                  .unsqueeze(2).to_broadcast([P, 2 * NH, DH]), ALU.mult).then_inc(keytok_out[kp], 1)

            def update_state(g, k):
                dve.wait_ge(upd_mm[k], g + 1)
                dve.wait_ge(kept_done[k], g + 1)
                new = bank[0][:, 0:NP * 2 * DV].rearrange("p (s d) -> p s d", s=NP)
                for par in range(2):
                    r, c = slice(par * DH, (par + 1) * DH), slice(par * DV, (par + 1) * DV)
                    i = dve.tensor_tensor(state[r, :, c], kept[r, :, c], new[r, :, c], ALU.add)
                i.then_inc(state_done[k], 1)

            def head_scale(g, kp):
                c, now = slice(2 * kp, 2 * kp + 2), nth(g, 2, kp)
                dve.wait_ge(u_out[2 * kp + 1], g + 1)
                total = u_sb[:, c, :, DH]
                dve.scalar_tensor_tensor(nrm[:, c], total, -1.0, total, ALU.mult, ALU.max).then_inc(nrm_done[0], 1)
                dve.wait_ge(nrm_done[0], now)
                dve.scalar_tensor_tensor(nrm1[:, c], nrm[:, c], EPS_MIX, of_group(floor_tok, g)[:, c], ALU.add, ALU.max
                                         ).then_inc(nrm_done[1], 1)
                dve.wait_ge(nrm_done[1], now)
                dve.scalar_tensor_tensor(nrm2[:, c], nrm1[:, c], EPS_MIX, nrm1[:, c], ALU.mult, ALU.mult
                                         ).then_inc(nrm_done[2], 1)
                dve.wait_ge(sq_done, now)
                dve.tensor_reduce(ssq[:, c].rearrange("p k h -> p (k h)"), sq[:].rearrange("p k h d -> p (k h) d"),
                                  AX.X, ALU.add).then_inc(ssq_done, 1)
                dve.wait_ge(nrm_done[2], now)
                dve.wait_ge(ssq_done, now)
                dve.scalar_tensor_tensor(var_h[:, c], ssq[:, c], 1.0 / DH, nrm2[:, c], ALU.mult, ALU.add
                                         ).then_inc(nrm_done[3], 1)

            def gate_heads(g):
                dve.wait_ge(skip_done, g + 1)
                for p in range(NP):
                    dve.wait_ge(hnT_mm[p], g + 1)
                    dve.scalar_tensor_tensor(mixed[:, p], bank[1 + p][:], vecs[:, p, VN:VN + 1], mixed[:, p],
                                             ALU.mult, ALU.add).then_inc(mixed_done[p], 1)
                for p in range(NP):
                    dve.wait_ge(mixed_done[p], g + 1)
                    dve.tensor_tensor(mixed[:, p], mixed[:, p], silu_z[:, p, bass.ds(g * G, G)], ALU.mult
                                      ).then_inc(hs_done[p], 1)

            flat = lambda t: t[:].rearrange("p k e -> p (k e)")

            def statistics(g, src, st, mv, ve, st_s, mv_s, ve_s):
                for k in range(NC):
                    i = dve.bn_stats(st[:, k], src[:, k])
                i.then_inc(st_s, 1)
                dve.wait_ge(st_s, g + 1)
                alone(dve)
                for k in range(NC):
                    i = dve.bn_aggr(mv[:, k], st[:, k])
                i.then_inc(mv_s, 1)
                dve.wait_ge(mv_s, g + 1)
                dve.tensor_scalar(ve[:], mv[:, :, 1], EPS_LN, None, ALU.add).then_inc(ve_s, 1)

            def normalise(dst, src, mv, rs, s):
                for k in range(NC):
                    i = dve.tensor_scalar(dst[:, k], src[:, k], mv[:, k, 0:1], rs[:, k:k + 1], ALU.subtract, ALU.mult)
                i.then_inc(s, 1)

            def mixer_out(g):
                dve.wait_ge(down_mm, g + 1)
                dve.wait_ge(x_res_in, 16 * (g + 1))
                dve.tensor_tensor(flat(y1), bank[3][:], flat(x_res), ALU.add).then_inc(y1_done, 1)
                dve.wait_ge(y1_done, g + 1)
                statistics(g, y1, st1, mv1, ve1, st1_done, mv1_done, ve1_done)

            def mixer_norm(g):
                dve.wait_ge(rs1_done, g + 1)
                normalise(Y, y1, mv1, rs1, Y_done)

            def mix_front(g):
                val_evac(g)
                weigh_scores(g, 0)

            def mix(g, f):
                if f is not None:
                    yT_low(f)
                weigh_keys(g, 0)
                if f is not None:
                    routing(f, 0)
                for j in range(NJ + 2):
                    if f is not None:
                        ffn_slot(f, j)
                    for what, arg in DVE_SLOT.get(j, ()):
                        if what == "route":
                            if f is not None:
                                routing(f, arg)
                        else:
                            {"C": weigh_scores, "K": weigh_keys, "S": update_state, "R": head_scale}[what](g, arg) \
                                if arg is not None else gate_heads(g)
                mixer_out(g)
                if f is not None:
                    ffn_sum(f)
                mixer_norm(g)
                if not (isinstance(g, int) and g == NG - 1):
                    mix_front(g + 1)
                if f is not None:
                    ffn_norm(f)

            def yT_low(f):
                dve.wait_ge(yT_hi_done, f + 1)
                dve.tensor_tensor(yT_lo[:], bank[7][:], yT_hi[:].bitcast(F32), ALU.subtract).then_inc(yT_lo_done, 1)

            def routing(f, part):
                def after(n):
                    dve.wait_ge(route, f * ROUTE + n)

                if part == 0:
                    dve.wait_ge(ge_done, f + 1)
                    dve.tensor_scalar(ge1[:], ge[:], 1.0, None, ALU.add).then_inc(route, 1)
                    after(1)
                    dve.reciprocal(gext[:, :, 0:NX], ge1[:]).then_inc(route, 1)
                    after(2)
                    alone(dve)
                    for k in range(NC):
                        i = dve.max(top[:, k], gext[:, k])
                    i.then_inc(route, 1)
                    after(3)
                    dve.memset(top[:, :, TOPK:8], -1.0).then_inc(route, 1)
                    after(4)
                    alone(dve)
                    for k in range(NC):
                        i = dve.match_replace(rest[:, k], top[:, k], gext[:, k], 0.0)
                    i.then_inc(route, 1)
                elif part == 1:
                    after(5)
                    dve.tensor_tensor(chosen[:], gext[:, :, 0:NX], rest[:, :, 0:NX], ALU.subtract).then_inc(route, 1)
                    after(6)
                    dve.tensor_reduce(csum[:], chosen[:], AX.X, ALU.add).then_inc(route, 1)
                    after(7)
                    dve.reciprocal(crec[:], csum[:]).then_inc(route, 1)
                    after(8)
                    dve.tensor_tensor(comb[:], chosen[:], crec[:].unsqueeze(2).to_broadcast([P, NC, NX]), ALU.mult
                                      ).then_inc(route, 1)
                else:
                    after(9)
                    dve.tensor_copy(comb3[:, :, 0], comb[:]).then_inc(route, 1)
                    after(10)
                    dve.tensor_tensor(comb_r[:, 0], comb[:], comb3[:, :, 0], ALU.subtract).then_inc(route, 1)
                    after(11)
                    dve.tensor_copy(comb3[:, :, 1], comb_r[:, 0]).then_inc(route, 1)
                    after(12)
                    dve.tensor_tensor(comb_r[:, 1], comb_r[:, 0], comb3[:, :, 1], ALU.subtract).then_inc(route, 1)
                    after(13)
                    dve.tensor_copy(comb3[:, :, 2], comb_r[:, 1]).then_inc(route, 1)

            def ffn_slot(f, j):
                if j <= NJ:
                    dve.wait_ge(silu_done, nth(f, NJ + 1, j))
                    dve.wait_ge(vin_mm, nth(f, NJ + 1, j))
                    if j >= 3:
                        dve.wait_ge(h2_done, nth(f, NJ, j - 3))
                    dst = h2 if j == 0 else h1
                    dve.tensor_tensor(dst[:, j % 2], s_in[:, j % 2], bank[5][:], ALU.mult).then_inc(h1_done, 1)
                if j >= 2:
                    dve.wait_ge(h1_done, nth(f, NJ + 1, j - 1))
                    dve.wait_ge(bc_mm, nth(f, NJ, j - 2))
                    dve.tensor_tensor(h2[:, (j - 1) % 2], h1[:, (j - 1) % 2], bank[6][:], ALU.mult).then_inc(h2_done, 1)

            def ffn_sum(f):
                dve.wait_ge(ob_mm, f + 1)
                dve.tensor_tensor(flat(z2), bank[4][:], flat(Y), ALU.add).then_inc(z2_done, 1)
                dve.wait_ge(z2_done, f + 2)
                statistics(f, z2, st2, mv2, ve2, st2_done, mv2_done, ve2_done)

            def ffn_norm(f):
                dve.wait_ge(rs2_done, f + 1)
                prev(dve, out_stored, f, 16)
                normalise(out_sb, z2, mv2, rs2, out_done)

            def ffn(f):
                yT_low(f)
                routing(f, 0)
                for j in range(NJ + 2):
                    ffn_slot(f, j)
                    if j < 2:
                        routing(f, j + 1)
                ffn_sum(f)
                ffn_norm(f)

            mix_front(0)
            dve.wait_ge(phase2_const, 5)
            groups(dve, mix, ffn)

        @block.tensor
        def _(pe):
            pe.wait_ge(blocks_made, 1)
            pe.wait_ge(pool_const, 16)
            n8 = 2 * NH * NP
            for s in range(NP):
                q, k, v = (qkv_block[:, m, s] for m in range(3))
                c = slice(s * P, (s + 1) * P)
                pe.matmul(bank[0][:, c], k, q, start=True, stop=True)
                pe.matmul(bank[1][:, c], v, center[:], start=True, stop=True)
                pe.transpose(bank[2][:, c], w_up[:, c], ident[:])
                c8 = slice(s * 2 * NH, (s + 1) * 2 * NH)
                pe.matmul(bank[3][:, c8], q, w_gates[:, s], start=True, stop=False)
                pe.matmul(bank[3][:, c8], k, w_gates[:, NP + s], start=False, stop=True)
                pe.matmul(bank[3][:, n8 + s * 2 * NH:n8 + (s + 1) * 2 * NH], v, w_gates[:, 2 * NP + s], start=True, stop=True)
                pe.transpose(bank[3][:, 2 * n8 + s * 8:2 * n8 + (s + 1) * 8], rows[:, c], ident[0:8, 0:8])
            pe.transpose(bank[3][:, 3 * n8:3 * n8 + NX], gate_rows[:], ident[0:NX, 0:NX]).then_inc(fold1_mm, 1)
            pe.wait_ge(fold1_out, 1)
            for s in range(NP):
                pe.matmul(bank[4][:, s * P:(s + 1) * P], w_up_t[:, s], v_center[:, s], start=True, stop=True)
            for s in range(NP):
                i = pe.matmul(bank[4][:, INNER:INNER + 2 * NH], w_up_t[:, s], g_v[:, s], start=(s == 0), stop=(s == NP - 1))
            i.then_inc(fold2_mm, 1)
            pe.wait_ge(weights_ready, 1)

            def phase1_gates(b, f):
                pe.wait_ge(xact_done[f], b + 1)
                if not (isinstance(b, int) and b == 0):
                    pe.wait_ge(gate_out[f], b)
                for k in range(NC):
                    o, c = bank[5 + f][:, k * 2 * NH:(k + 1) * 2 * NH], slice(k * P, (k + 1) * P)
                    pe.matmul(o, x_t[:, f, c], g_x[:], start=True, stop=False)
                    for p in range(NP):
                        i = pe.matmul(o, xact[:, f, p, c], g_act[:, p], start=False, stop=(p == NP - 1))
                i.then_inc(gate_mm[f], 1)

            def phase1_xt(b, f):
                pe.wait_ge(x_loaded[f], 16 * (b + 1))
                if f:
                    pe.wait_ge(xt_out[0], b + 1)
                elif not (isinstance(b, int) and b == 0):
                    pe.wait_ge(xt_out[1], b)
                for k in range(NC):
                    i = pe.transpose(bank[0][:, k * P:(k + 1) * P], x_in[:, f, k], ident[:])
                i.then_inc(xt_mm[f], 1)

            def phase1_up(b, f, q):
                if f:
                    pe.wait_ge(up_out[0], b * 2 * NP + q + 1)
                elif not (isinstance(b, int) and b == 0):
                    pe.wait_ge(up_out[1], (b - 1) * 2 * NP + q + 1)
                pe.matmul(bank[1 + q][:], w_up[:, q * P:(q + 1) * P], x_t[:, f], start=True, stop=True
                          ).then_inc(up_mm[f], 1)

            def phase1(b):
                first, last = isinstance(b, int) and b == 0, isinstance(b, int) and b == B - 1
                for f in range(HALVES):
                    if f == 0:
                        phase1_xt(b, 1)
                    elif not last:
                        phase1_xt(b + 1, 0)
                    pe.wait_ge(xt_out[f], b + 1)
                    for q in range(NP):
                        phase1_up(b, f, q)
                    if f == 1:
                        phase1_gates(b, 0)
                    elif not first:
                        phase1_gates(b - 1, 1)
                    for q in range(NP, 2 * NP):
                        phase1_up(b, f, q)

            phase1_xt(0, 0)
            phase1(0)
            with pe.Fori(1, B - 1) as b:
                phase1(b)
            phase1(B - 1)
            phase1_gates(B - 1, 1)

            def mix_front(g):
                pe.wait_ge(x_new_in, 16 * (g + 1))
                prev(pe, state_done[NC - 1], g)
                for k in range(NC):
                    i = pe.transpose(bank[0][:, k * P:(k + 1) * P], x_new[:, k], ident[:])
                i.then_inc(xT_mm, 1)
                pe.wait_ge(xa_in, 16 * (g + 1))
                for p in range(NP):
                    prev(pe, mixed_done[p], g)
                    pe.matmul(bank[1 + p][:], w_key[:, p], xa[:, p], start=True, stop=True).then_inc(key_mm[p], 1)
                pe.wait_ge(xT_out, g + 1)
                prev(pe, y1_done, g)
                for i in range(2):
                    for k in range(2):
                        c = 2 * i + k
                        ins = pe.matmul(bank[3 if i == 0 else 0][:, k * INNER:(k + 1) * INNER],
                                        xT2[:, c * P:(c + 1) * P], w_val[:], start=True, stop=True)
                    ins.then_inc(val_mm[i], 1)
                scores(g, 0)

            def scores(g, kp):
                for p in range(NP):
                    if kp == 0:
                        pe.wait_ge(key_out[p], g + 1)
                for par in range(2):
                    if kp:
                        pe.wait_ge(C_done[0][par], g + 1)
                    r = slice(par * DH, (par + 1) * DH)
                    for k in range(2):
                        c = slice((2 * kp + k) * P, (2 * kp + k + 1) * P)
                        for p in range(NP):
                            i = pe.matmul(bank[1 + par][:, (k * NP + p) * P:(k * NP + p + 1) * P],
                                          keyT[r, p, c], xa[r, p, c], start=True, stop=True)
                    i.then_inc(score_mm[kp][par], 1)

            def key_tokens(g, kp):
                pe.wait_ge(state_done[1] if kp else val_out[1], g + 1)
                for k in range(2):
                    for p in range(NP):
                        i = pe.transpose(bank[0][:, k * INNER + p * P:k * INNER + (p + 1) * P],
                                         keyT[:, p, (2 * kp + k) * P:(2 * kp + k + 1) * P], ident[:])
                i.then_inc(keytok_mm[kp], 1)

            def chunk(g, k):
                kp, kk = k // 2, k % 2
                pe.wait_ge(u_out[k - 1] if k else val_out[0], g + 1)
                if k == 0:
                    pe.wait_ge(qs_done, g + 1)
                    pe.wait_ge(val_out[1], g + 1)
                    prev(pe, state_done[NC - 1], g)
                else:
                    pe.wait_ge(state_done[k - 1], g + 1)
                for par in range(2):
                    pe.wait_ge(C_done[kp][par], g + 1)
                c = slice(k * P, (k + 1) * P)
                for p in range(NP):
                    o = bank[3][:, p * 2 * DV:(p + 1) * 2 * DV]
                    pe.matmul(o, qs[:, p, c], state[:, p], start=True, stop=False, skip_group_check=True)
                    for par in range(2):
                        i = pe.matmul(o[:, par * DV:(par + 1) * DV], C[:, par, kk, p], vals[:, k, 2 * p + par],
                                      start=False, stop=True, skip_group_check=True)
                i.then_inc(u_mm[k], 1)
                pe.wait_ge(state_done[k - 1] if kk else keytok_out[kp], g + 1)
                for p in range(NP):
                    i = pe.matmul(bank[0][:, p * 2 * DV:(p + 1) * 2 * DV], keys[:, kk, p * P:(p + 1) * P],
                                  vals[:, k, 2 * p:2 * p + 2].rearrange("p h d -> p (h d)"), start=True, stop=True)
                i.then_inc(upd_mm[k], 1)

            def head_transposes(g):
                pe.wait_ge(hn_done, nth(g, 2, 1))
                for p in range(NP):
                    pe.wait_ge(C_done[1][p], g + 1)
                    for k in range(NC):
                        i = pe.transpose(bank[1 + p][:, k * P:(k + 1) * P], hn[:, k, p * P:(p + 1) * P], ident[:])
                    i.then_inc(hnT_mm[p], 1)

            def down(g, half):
                if half == 0:
                    pe.wait_ge(u_out[NC - 1], g + 1)
                    for p in range(NP):
                        pe.wait_ge(hs_done[p], g + 1)
                for k in range(2 * half, 2 * half + 2):
                    for p in range(NP):
                        i = pe.matmul(bank[3][:, k * P:(k + 1) * P], mixed[:, p, k * P:(k + 1) * P], w_down[:, p],
                                      start=(p == 0), stop=(p == NP - 1))
                if half:
                    i.then_inc(down_mm, 1)

            def ffn_head(f):
                pe.wait_ge(Y_done, f + 1)
                prev2(pe, z2_done, f)
                for k in range(NC):
                    i = pe.transpose(bank[7][:, k * P:(k + 1) * P], Y[:, k], ident[:])
                i.then_inc(yT_mm, 1)

            def ffn_logits(f):
                pe.wait_ge(yT_out, f + 1)
                for k in range(NC):
                    i = pe.matmul(bank[6][:, k * NX:(k + 1) * NX], yT[:, k * P:(k + 1) * P], w_gate[:], start=True, stop=True)
                i.then_inc(logit_mm, 1)

            def ffn_in(f, j):
                for m, (done, free) in enumerate(((hin_mm, silu_done), (vin_mm, h1_done))):
                    if j:
                        pe.wait_ge(free, nth(f, NJ + 1, j - 1))
                    elif m == 0:
                        pe.wait_ge(yT_hi_done, f + 1)
                    o = bank[4 + m][:]
                    pe.matmul(o, in_hi[:, m, j], yT_hi[:], start=True, stop=False)
                    pe.matmul(o, in_lo[:, m, j], yT_hi[:], start=False, stop=False)
                    if j == 0 and m == 0:
                        pe.wait_ge(yT_lo_done, f + 1)
                    pe.matmul(o, in_hi[:, m, j], yT_lo[:], start=False, stop=True).then_inc(done, 1)

            def combine_transposes(f):
                pe.wait_ge(route, (f + 1) * ROUTE)
                pe.wait_ge(ge_done, f + 1)
                for k in range(NC):
                    i = pe.transpose(bank[6][:, k * P // 2:(k + 1) * P // 2].bitcast(BF16),
                                     comb3[:, k].rearrange("p t e -> p (t e)"), ident_bf[:])
                i.then_inc(combT_mm, 1)

            def combine_rows(f, j):
                if j > 1:
                    pe.wait_ge(h2_done, nth(f, NJ, j - 2))
                else:
                    pe.wait_ge(combT_out, f + 1)
                pe.matmul(bank[6][:], pair_rows[:, j - 1], combT[:], start=True, stop=True).then_inc(bc_mm, 1)

            def ffn_out(f, j):
                if j:
                    pe.wait_ge(h2_done, nth(f, NJ, j - 1))
                else:
                    pe.wait_ge(h1_done, nth(f, NJ + 1, 0))
                w = ewout[:, j - 1] if j else wsout[:]
                i = pe.matmul(bank[7][:], w, h2[:, j % 2], start=(j == 0), stop=(j == NJ))
                if j == NJ:
                    i.then_inc(o_mm, 1)

            def ffn_back(f):
                pe.wait_ge(oT_out, f + 1)
                pe.wait_ge(silu_done, nth(f, NJ + 1, NJ))
                for k in range(NC):
                    i = pe.transpose(bank[4][:, k * P:(k + 1) * P], oT[:, k * P:(k + 1) * P], ident[:])
                i.then_inc(ob_mm, 1)

            def ffn_slot(f, j):
                if j == 2:
                    combine_transposes(f)
                if j <= NJ:
                    ffn_in(f, j)
                if 2 <= j <= NJ + 1:
                    combine_rows(f, j - 1)
                if j >= 2:
                    ffn_out(f, j - 2)

            def mix(g, f):
                if f is not None:
                    ffn_head(f)
                key_tokens(g, 0)
                if f is not None:
                    ffn_logits(f)
                for j in range(NJ + 3):
                    if f is not None:
                        ffn_slot(f, j)
                    for what, arg in PE_SLOT.get(j, ()):
                        {"S": scores, "K": key_tokens, "C": chunk, "D": down}[what](g, arg) \
                            if arg is not None else head_transposes(g)
                if f is not None:
                    ffn_back(f)
                if not (isinstance(g, int) and g == NG - 1):
                    mix_front(g + 1)

            def ffn(f):
                ffn_head(f)
                ffn_logits(f)
                for j in range(NJ + 3):
                    ffn_slot(f, j)
                ffn_back(f)

            for f in range(HALVES):
                pe.wait_ge(gate_out[f], B)
            for c in range(CS):
                for t in range(2):
                    i = pe.transpose(bank[2 * t + c // 4][0:R, (c % 4) * P:(c % 4 + 1) * P], gates[:, c, t], ident[:])
            i.then_inc(row_mm, 1)
            pe.wait_ge(dve_scan, 4)
            pe.wait_ge(act_scan, 2)
            mix_front(0)
            pe.wait_ge(dve_scan, 6)
            for n, src in enumerate((rows_a, rows_w, rows_floor)):
                if n:
                    pe.wait_ge(act_scan, 6 + n)
                for c in range(CS):
                    i = pe.transpose(bank[4 + n][:, c * R:(c + 1) * R], src[:, c * P:(c + 1) * P], ident[0:R, 0:R])
                i.then_inc(back_mm, 1)

            pe.wait_ge(phase2_const, 5)
            pe.wait_ge(ffn_w_in, 16 * FFN_DMAS)
            pe.wait_ge(in_split, 4)
            groups(pe, mix, ffn)


PE_SLOT = {0: (("C", 0),), 1: (("C", 1), ("S", 1), ("K", 1)), 2: (("C", 2),), 3: (("C", 3),),
           6: (("H", None),), 9: (("D", 0),), 10: (("D", 1),)}
DVE_SLOT = {0: (("S", 0), ("route", 1)), 1: (("S", 1), ("route", 2), ("C", 1), ("K", 1)), 2: (("S", 2), ("R", 0)),
            3: (("S", 3),), 4: (("R", 1),), 6: (("H", None),)}
U_SLOT = {0: 0, 1: 1, 2: 2, 3: 3}
SCAN_MAX = 7
SCAN_INTER = 6
DVE_SCAN = 12
BACK = 3
ROUTE = 14


_INS = ['L0_attn_x', 'L0_attn_W_up', 'L0_attn_conv_w', 'L0_attn_conv_b', 'L0_attn_Wq', 'L0_attn_Wk', 'L0_attn_Wv',
        'L0_attn_W_ig', 'L0_attn_b_ig', 'L0_attn_W_fg', 'L0_attn_b_fg', 'L0_attn_norm_w', 'L0_attn_skip',
        'L0_attn_W_down', 'L0_ffn_gate_w', 'L0_ffn_ws_in', 'L0_ffn_vs_in', 'L0_ffn_ws_out', 'L0_ffn_e_win',
        'L0_ffn_e_vin', 'L0_ffn_e_wout']
_OUTS = [((8, 1024, 128), 'float32')]


def kernel(**inputs):
    import numpy as _np
    import concourse.bacc as _bacc
    from concourse import mybir as _mybir
    from concourse.bass_utils import run_bass_kernel_spmd as _run

    nc = _bacc.Bacc("TRN2", target_bir_lowering=False, num_devices=1)
    arrays, args = {}, []
    for name in _INS:
        a = _np.ascontiguousarray(inputs[name])
        arrays[f"in_{name}_dram"] = a
        args.append(nc.dram_tensor(f"in_{name}_dram", a.shape, _mybir.dt.from_np(a.dtype), kind="ExternalInput").ap())
    for i, (shape, dtype) in enumerate(_OUTS):
        dt = _mybir.dt.from_np(_np.dtype(dtype))
        args.append(nc.dram_tensor(f"out_{i}_dram", shape, dt, kind="ExternalOutput").ap())
    mixer_moe_block(nc, *args)
    r = _run(nc, [arrays], core_ids=[0])
    return r.results[0]["out_0_dram"]
```

```python
from contextlib import ExitStack

import concourse.bass as bass
from concourse import mybir

F32 = mybir.dt.float32
F32R = mybir.dt.float32r
BF16 = mybir.dt.bfloat16
ALU = mybir.AluOpType
ACT = mybir.ActivationFunctionType
AX = mybir.AxisListType

P = 128
EPS_MIX = 1e-6
EPS_LN = 1e-5
NEG = -1e30


def mixer_moe_block(nc, x, W_up, conv_w, conv_b, Wq, Wk, Wv, W_ig, b_ig, W_fg, b_fg, norm_w, skip,
                    W_down, gate_w, ws_in, vs_in, ws_out, e_win, e_vin, e_wout, out):
    B, S, E = x.shape
    INNER = W_up.shape[1] // 2
    NH = b_ig.shape[0]
    DH = INNER // NH
    DV = DH + 1
    TAPS = conv_w.shape[0]
    HALO = TAPS - 1
    NP = INNER // P
    NX, _, HX = e_win.shape
    NJ = NX * HX // P
    TOPK = 4
    G = 512
    NC = G // P
    HALVES = S // G
    NG = B * HALVES
    CS = S // P
    R = B * NH
    QD = Wq.shape[1]
    assert E == P and INNER == 2 * P and DH == 64 and NH == 4 and HX == 64 and HALVES == 2

    x_g = x.rearrange("b (f k p) e -> (b f) p k e", f=HALVES, p=P)
    out_g = out.rearrange("b (f k p) e -> (b f) p k e", f=HALVES, p=P)
    xact_d = nc.dram_tensor("xact_scratch", [NG, P, NP * G], F32).ap()
    xt_d = nc.dram_tensor("xt_scratch", [NG, P, G], F32).ap()
    max_d = nc.dram_tensor("max_scratch", [NG, NH, G], F32).ap()
    inter_d = nc.dram_tensor("inter_scratch", [NG, NH, G], F32).ap()
    decay_d = nc.dram_tensor("decay_scratch", [NH, B, CS], F32).ap()

    with ExitStack() as ctx:
        def sb(name, shape, dt=F32):
            return ctx.enter_context(nc.sbuf_tensor(name, shape, dt))

        def sem(name):
            return ctx.enter_context(nc.semaphore(name))

        def sems(name, *counts):
            if not counts:
                return sem(name)
            return [sems(f"{name}_{i}", *counts[1:]) for i in range(counts[0])]

        bank = [ctx.enter_context(nc.psum_tensor(f"bank{i}", [P, 512], F32)) for i in range(8)]

        ident = sb("ident", [P, P])
        ident_bf = sb("ident_bf", [P, P], BF16)
        block_mask = sb("block_mask", [P, P])
        center = sb("center", [P, P])
        pair_rows = sb("pair_rows", [3 * NX, NJ, P], BF16)
        qkv_small = sb("qkv_small", [P, 3, NP, QD])
        w_gates = sb("w_gates", [P, 3 * NP, 2 * NH])
        vecs = sb("vecs", [P, NP, 8])
        VB, VN, VS = TAPS, TAPS + 1, TAPS + 2
        b_i = sb("b_i", [R, 1])
        b_f = sb("b_f", [R, 1])
        gate_rows = sb("gate_rows", [NX, P])
        w_gate = sb("w_gate", [P, NX])
        w_down = sb("w_down", [P, NP, E])
        in_hi = sb("in_hi", [P, 2, NJ + 1, P], F32R)
        in_lo = sb("in_lo", [P, 2, NJ + 1, P], F32R)
        ewout = sb("ewout", [P, NJ, E])
        wsout = sb("wsout", [P, P])
        w_key = sb("w_key", [P, NP, P])
        g_act = sb("g_act", [P, NP, 2 * NH])
        g_x = sb("g_x", [P, 2 * NH])
        g_v = sb("g_v", [P, NP, 2 * NH])
        w_val = sb("w_val", [P, INNER])

        silu_z = sb("silu_z", [P, NP, B * S])
        a_tok = sb("a_tok", [P, B, HALVES, NC, NH])
        w_tok = sb("w_tok", [P, B, HALVES, NC, NH])
        floor_tok = sb("floor_tok", [P, B, HALVES, NC, NH])
        decay = sb("decay", [P, NP, B * CS])

        up_w_in = sem("up_w_in")
        vec_in = sem("vec_in")
        vec_mm = sem("vec_mm")
        vec_out = sem("vec_out")
        up_split = sem("up_split")
        mixer_w_in = sem("mixer_w_in")
        ffn_w_in = sem("ffn_w_in")
        pool_const = sem("pool_const")
        blocks_made = sem("blocks_made")
        fold1_mm = sem("fold1_mm")
        fold1_out = sem("fold1_out")
        fold2_mm = sem("fold2_mm")
        weights_ready = sem("weights_ready")
        in_split = sem("in_split")

        waited = sem("waited")

        block = ctx.enter_context(nc.Block())
        VEC_DMAS = 5
        MIXER_DMAS = 9
        FFN_DMAS = 6

        p1 = ExitStack()

        def sb1(name, shape, dt=F32):
            return p1.enter_context(nc.sbuf_tensor(name, shape, dt))

        w_up = sb1("w_up", [P, 2 * INNER])
        qkv_block = sb1("qkv_block", [P, 3, NP, P])
        rows = sb1("rows", [8, INNER])
        v_center = sb1("v_center", [P, NP, P])
        w_up_t = sb1("w_up_t", [P, NP, P])
        up_hi = sb1("up_hi", [P, 2 * INNER], F32R)
        up_lo = sb1("up_lo", [P, 2 * INNER], F32R)
        x_hi = sb1("x_hi", [P, HALVES, G], F32R)
        x_lo = sb1("x_lo", [P, HALVES, G], F32R)
        x_in = sb1("x_in", [P, HALVES, NC, E])
        x_t = sb1("x_t", [P, HALVES, G])
        xm = sb1("xm", [P, HALVES, NP, HALO + G])
        acc = sb1("acc", [P, HALVES, NP, G])
        xact = sb1("xact", [P, HALVES, NP, G])
        gates = sb1("gates", [P, CS, 2, R])
        pre_i = sb1("pre_i", [R, S])
        min_f = sb1("min_f", [R, S])
        abs_f = sb1("abs_f", [R, S])
        exp_f = sb1("exp_f", [R, S])
        log_f = sb1("log_f", [R, S])
        lfc = sb1("lfc", [R, S])
        run_max = sb1("run_max", [R, S])
        before = sb1("before", [R, CS])
        rows_a = sb1("rows_a", [R, S])
        rows_w = sb1("rows_w", [R, S])
        rows_floor = sb1("rows_floor", [R, S])
        rows_inter = sb1("rows_inter", [R, S])
        rows_decay = sb1("rows_decay", [R, CS])
        in_w = sb1("in_w", [P, 2, NJ + 1, P])
        p1.close()

        x_loaded = sems("x_loaded", HALVES)
        xt_mm = sems("xt_mm", HALVES)
        xt_out = sems("xt_out", HALVES)
        x_lo_done = sems("x_lo_done", HALVES)
        up_mm = sems("up_mm", HALVES)
        up_out = sems("up_out", HALVES)
        halo_done = sem("halo_done")
        tap_done = sems("tap_done", HALVES)
        xact_done = sems("xact_done", HALVES)
        xact_stored = sems("xact_stored", HALVES)
        xt_stored = sems("xt_stored", HALVES)
        gate_x_mm = sems("gate_x_mm", HALVES)
        gate_mm = sems("gate_mm", HALVES)
        gate_out = sems("gate_out", HALVES)
        row_mm = sem("row_mm")
        act_scan = sem("act_scan")
        dve_scan = sem("dve_scan")
        back_mm = sem("back_mm")
        back_out = sem("back_out")
        max_stored = sem("max_stored")
        rows_stored = sem("rows_stored")
        decay_in = sem("decay_in")

        xa = sb("xa", [P, NP, G])
        xT2 = sb("xT2", [P, G])
        keyT = sb("keyT", [P, NP, G])
        vals = sb("vals", [P, NC, NH, DV])
        max_b = sb("max_b", [P, NH, G])
        D = sb("D", [P, 2, 2, 2, NP, P])
        C = sb("C", [P, 2, 2, NP, P])
        inter_w = sb("inter_w", [P, NP, G])
        x_res = sb("x_res", [P, NC, E])
        keys = sb("keys", [P, 2, INNER])
        qs = sb("qs", [P, NP, G])
        state = sb("state", [P, NP, 2 * DV])
        kept = sb("kept", [P, NP, 2 * DV])
        u_sb = sb("u_sb", [P, NC, NH, DV])
        sq = sb("sq", [P, 2, NH, DH])
        ssq = sb("ssq", [P, NC, NH])
        nrm = sb("nrm", [P, NC, NH])
        nrm1 = sb("nrm1", [P, NC, NH])
        nrm2 = sb("nrm2", [P, NC, NH])
        var_h = sb("var_h", [P, NC, NH])
        r_h = sb("r_h", [P, NC, NH])
        half = sb("half", [P, NC * NH])
        hn = sb("hn", [P, NC, INNER])
        mixed = sb("mixed", [P, NP, G])
        y1 = sb("y1", [P, NC, E])
        st1 = sb("st1", [P, NC, 6])
        mv1 = sb("mv1", [P, NC, 2])
        ve1 = sb("ve1", [P, NC])
        rs1 = sb("rs1", [P, NC])
        Y = sb("Y", [P, NC, E])
        yT = sb("yT", [P, G])
        yT_hi = sb("yT_hi", [P, G], F32R)
        yT_lo = sb("yT_lo", [P, G], F32R)
        ge = sb("ge", [P, NC, NX])
        ge1 = sb("ge1", [P, NC, NX])
        gext = sb("gext", [P, NC, NX + TOPK])
        top = sb("top", [P, NC, 8])
        rest = sb("rest", [P, NC, NX + TOPK])
        chosen = sb("chosen", [P, NC, NX])
        csum = sb("csum", [P, NC])
        crec = sb("crec", [P, NC])
        comb = sb("comb", [P, NC, NX])
        comb_r = sb("comb_r", [P, 2, NC, NX])
        comb3 = sb("comb3", [P, NC, P // NX, NX], BF16)
        combT = sb("combT", [3 * NX, G], BF16)
        s_in = sb("s_in", [P, 2, G])
        h1 = sb("h1", [P, 2, G])
        h2 = sb("h2", [P, 2, G])
        z2 = sb("z2", [P, NC, E])
        st2 = sb("st2", [P, NC, 6])
        mv2 = sb("mv2", [P, NC, 2])
        ve2 = sb("ve2", [P, NC])
        rs2 = sb("rs2", [P, NC])
        out_sb = sb("out_sb", [P, NC, E])

        xa_in, xT_in, x_res_in = sem("xa_in"), sem("xT_in"), sem("x_res_in")
        max_in = sem("max_in")
        inter_in = sem("inter_in")
        out_stored = sem("out_stored")
        phase2_const = sem("phase2_const")
        arg_sub = sem("arg_sub")
        arg_masked = sem("arg_masked")
        D_done = sem("D_done")
        key_mm, key_out = sems("key_mm", NP), sems("key_out", NP)
        val_mm, val_out = sems("val_mm", 2), sems("val_out", 2)
        qs_done = sem("qs_done")
        skip_done = sem("skip_done")
        score_mm, C_done = sems("score_mm", 2, 2), sems("C_done", 2, 2)
        keytok_mm, keytok_out = sems("keytok_mm", 2), sems("keytok_out", 2)
        u_mm, u_out = sems("u_mm", NC), sems("u_out", NC)
        upd_mm, kept_done, state_done = sems("upd_mm", NC), sems("kept_done", NC), sems("state_done", NC)
        sq_done, ssq_done = sem("sq_done"), sem("ssq_done")
        nrm_done = sems("nrm_done", 4)
        rh_done = sem("rh_done")
        hn_done = sem("hn_done")
        hnT_mm, mixed_done, hs_done = sems("hnT_mm", NP), sems("mixed_done", NP), sems("hs_done", NP)
        down_mm = sem("down_mm")
        y1_done, st1_done, mv1_done, ve1_done = sem("y1_done"), sem("st1_done"), sem("mv1_done"), sem("ve1_done")
        rs1_done = sem("rs1_done")
        Y_done = sem("Y_done")
        yT_mm, yT_out = sem("yT_mm"), sem("yT_out")
        yT_hi_done, yT_lo_done = sem("yT_hi_done"), sem("yT_lo_done")
        logit_mm, ge_done = sem("logit_mm"), sem("ge_done")
        route = sem("route")
        combT_mm, combT_out = sem("combT_mm"), sem("combT_out")
        hin_mm, vin_mm = sem("hin_mm"), sem("vin_mm")
        silu_done, h1_done = sem("silu_done"), sem("h1_done")
        bc_mm, h2_done = sem("bc_mm"), sem("h2_done")
        o_mm = sem("o_mm")
        z2_done, st2_done, mv2_done, ve2_done = sem("z2_done"), sem("st2_done"), sem("mv2_done"), sem("ve2_done")
        rs2_done = sem("rs2_done")
        out_done = sem("out_done")

        def nth(g, per, i):
            return g * per + i + 1

        def alone(eng):
            eng.sem_inc(waited, 1)

        def groups(eng, mix, ffn):
            mix(0, None)
            with eng.Fori(1, NG - 1) as g:
                mix(g, g - 1)
            mix(NG - 1, NG - 2)
            ffn(NG - 1)

        def prev(eng, s, g, per=1):
            if isinstance(g, int) and g == 0:
                return
            eng.wait_ge(s, g * per)

        def prev2(eng, s, f):
            eng.wait_ge(s, f + 1)

        @block.sync
        def _(sp):
            n = [0]

            def load(dst, src, s):
                n[0] += 1
                sp.dma_start(dst, src).then_inc(s, 16)

            load(x_in[:, 0], x_g[0], x_loaded[0])
            load(w_up[:], W_up, up_w_in)
            load(rows[0:TAPS, :], conv_w, vec_in)
            for i, v in ((VB, conv_b), (VN, norm_w), (VS, skip), (VS + 1, skip)):
                load(rows[i:i + 1, :], v.rearrange("(a n) -> a n", a=1), vec_in)
            load(x_in[:, 1], x_g[1], x_loaded[1])
            n[0] = 0
            for m, w in enumerate((Wq, Wk, Wv)):
                load(qkv_small[:, m], w.rearrange("(s b) o d -> (b o) s d", s=NP), mixer_w_in)
            load(w_gates[:, :, 0:NH], W_ig.rearrange("(s p) h -> p s h", p=P), mixer_w_in)
            load(w_gates[:, :, NH:2 * NH], W_fg.rearrange("(s p) h -> p s h", p=P), mixer_w_in)
            load(gate_rows[:], gate_w, mixer_w_in)
            load(b_i[:], b_ig.rearrange("(h a) -> h a", a=1).partition_broadcast(B), mixer_w_in)
            load(b_f[:], b_fg.rearrange("(h a) -> h a", a=1).partition_broadcast(B), mixer_w_in)
            load(w_down[:], W_down.rearrange("(s p) e -> p s e", p=P), mixer_w_in)
            assert n[0] == MIXER_DMAS, n[0]

            ffn_loads = [(ewout[:], e_wout.rearrange("(j t) h d -> (t h) j d", t=P // HX)), (wsout[:], ws_out)]
            for m, (w, w_shared) in enumerate(((e_win, ws_in), (e_vin, vs_in))):
                ffn_loads += [(in_w[:, m, 1:].rearrange("p j (t h) -> p (j t) h", h=HX), w.rearrange("e d h -> d e h")),
                              (in_w[:, m, 0], w_shared)]
            assert len(ffn_loads) == FFN_DMAS

            def store_xact(b, f):
                sp.wait_ge(xact_done[f], b + 1)
                sp.dma_start(xact_d[HALVES * b + f], xact[:, f]).then_inc(xact_stored[f], 16)

            def phase1(b):
                first, last = isinstance(b, int) and b == 0, isinstance(b, int) and b == B - 1
                for f in range(HALVES):
                    if not last:
                        sp.wait_ge(xt_mm[f], b + 1)
                        sp.dma_start(x_in[:, f], x_g[HALVES * b + HALVES + f]).then_inc(x_loaded[f], 16)
                    if isinstance(b, int) and HALVES * b + f < FFN_DMAS:
                        load(*ffn_loads[HALVES * b + f], ffn_w_in)
                    sp.wait_ge(xt_out[f], b + 1)
                    sp.dma_start(xt_d[HALVES * b + f], x_t[:, f]).then_inc(xt_stored[f], 16)
                    if f == 1:
                        store_xact(b, 0)
                    elif not first:
                        store_xact(b - 1, 1)

            assert FFN_DMAS % HALVES == 0
            for b in range(FFN_DMAS // HALVES):
                phase1(b)
            with sp.Fori(FFN_DMAS // HALVES, B - 1) as b:
                phase1(b)
            phase1(B - 1)
            store_xact(B - 1, 1)

            def load_max(g):
                sp.dma_start(max_b[:], max_d[g].rearrange("h t -> (h t)").partition_broadcast(P)).then_inc(max_in, 16)

            def load_inter(g):
                for par in range(2):
                    sp.dma_start(inter_w[par * DH:(par + 1) * DH],
                                 inter_d[g].rearrange("(p two) t -> two p t", two=2)[par].partition_broadcast(DH)
                                 ).then_inc(inter_in, 16)

            def load_xa(g):
                sp.dma_start(xa[:], xact_d[g].rearrange("p (s t) -> p s t", s=NP)).then_inc(xa_in, 16)

            for f in range(HALVES):
                sp.wait_ge(xact_stored[f], 16 * B)
                sp.wait_ge(xt_stored[f], 16 * B)
                sp.wait_ge(gate_out[f], B)
            sp.dma_start(xT2[:], xt_d[0]).then_inc(xT_in, 16)
            load_xa(0)

            half_of = lambda t: t.rearrange("(b f) h t -> f b h t", f=HALVES)
            sp.wait_ge(dve_scan, SCAN_MAX)
            for f in range(HALVES):
                sp.dma_start(half_of(max_d)[f], run_max[:, f * G:(f + 1) * G]).then_inc(max_stored, 16)
            sp.wait_ge(max_stored, 16 * HALVES)
            load_max(0)
            sp.wait_ge(act_scan, SCAN_INTER)
            for f in range(HALVES):
                sp.dma_start(half_of(inter_d)[f], rows_inter[:, f * G:(f + 1) * G]).then_inc(rows_stored, 16)
            sp.dma_start(decay_d.rearrange("h b c -> b h c"), rows_decay[:]).then_inc(rows_stored, 16)
            sp.wait_ge(rows_stored, 16 * (HALVES + 1))
            sp.wait_ge(dve_scan, DVE_SCAN)
            load_inter(0)
            for par in range(2):
                for p in range(NP):
                    sp.dma_start(decay[par * DH:(par + 1) * DH, p, :],
                                 decay_d[2 * p + par].rearrange("b c -> (b c)").partition_broadcast(DH)
                                 ).then_inc(decay_in, 16)
            sp.dma_start(x_res[:], x_g[0]).then_inc(x_res_in, 16)

            def mix(g, f):
                sp.wait_ge(arg_sub, nth(g, 4, 3))
                if not (isinstance(g, int) and g == NG - 1):
                    load_max(g + 1)
                    sp.wait_ge(val_mm[1], g + 1)
                    sp.dma_start(xT2[:], xt_d[g + 1]).then_inc(xT_in, 16)
                    sp.wait_ge(qs_done, g + 1)
                    load_inter(g + 1)
                    sp.wait_ge(skip_done, nth(g, NP, NP - 1))
                    sp.wait_ge(score_mm[1][1], g + 1)
                    load_xa(g + 1)
                if f is not None:
                    store(f)
                if not (isinstance(g, int) and g == NG - 1):
                    sp.wait_ge(y1_done, g + 1)
                    sp.dma_start(x_res[:], x_g[g + 1]).then_inc(x_res_in, 16)

            def store(f):
                sp.wait_ge(out_done, f + 1)
                sp.dma_start(out_g[f], out_sb[:]).then_inc(out_stored, 16)

            groups(sp, mix, store)
            sp.wait_ge(out_stored, 16 * NG)

        @block.gpsimd
        def _(pool):
            pool.memset(ident[:], 0.0).then_inc(pool_const, 1)
            pool.memset(ident_bf[:], 0.0).then_inc(pool_const, 1)
            pool.memset(block_mask[:], 1.0).then_inc(pool_const, 1)
            pool.memset(center[:], -1.0 / DH).then_inc(pool_const, 1)
            pool.memset(pair_rows[:], 0.0).then_inc(pool_const, 1)
            pool.memset(xm[:, 0, :, 0:HALO], 0.0).then_inc(pool_const, 1)
            pool.wait_ge(pool_const, 6)
            for m in (ident, ident_bf):
                pool.affine_select(out=m[:], in_=m[:], compare_op=ALU.not_equal, fill=1.0, base=0,
                                   pattern=[[-1, P]], channel_multiplier=1).then_inc(pool_const, 1)
            bm = block_mask[:].rearrange("p (b d) -> p b d", d=QD)
            pool.affine_select(out=bm, in_=bm, compare_op=ALU.is_ge, fill=0.0, base=0,
                               pattern=[[-QD, P // QD], [0, QD]], channel_multiplier=1).then_inc(pool_const, 1)
            pool.affine_select(out=center[:, 0:DH], in_=center[:, 0:DH], compare_op=ALU.is_ge, fill=0.0,
                               base=DH - 1, pattern=[[0, DH]], channel_multiplier=-1).then_inc(pool_const, 1)
            pool.affine_select(out=center[:, DH:P], in_=center[:, DH:P], compare_op=ALU.is_ge, fill=0.0,
                               base=-DH, pattern=[[0, DH]], channel_multiplier=1).then_inc(pool_const, 1)
            pool.wait_ge(pool_const, 11)
            pool.affine_select(out=bm, in_=bm, compare_op=ALU.is_ge, fill=0.0, base=QD - 1,
                               pattern=[[QD, P // QD], [0, QD]], channel_multiplier=-1).then_inc(pool_const, 1)
            pool.tensor_tensor(center[:], center[:], ident[:], ALU.add).then_inc(pool_const, 1)

            def x_low(b):
                for f in range(HALVES):
                    pool.wait_ge(xt_out[f], b + 1)
                    pool.tensor_tensor(x_lo[:, f], x_t[:, f], x_hi[:, f].bitcast(F32), ALU.subtract
                                       ).then_inc(x_lo_done[f], 1)

            x_low(0)

            pool.wait_ge(pool_const, CONSTS)
            pool.wait_ge(mixer_w_in, 16 * MIXER_DMAS)
            mask = block_mask[:].rearrange("p (b d) -> p b d", d=QD)
            for m in range(3):
                for s in range(NP):
                    i = pool.tensor_tensor(qkv_block[:, m, s].rearrange("p (b d) -> p b d", d=QD), mask,
                                           qkv_small[:, m, s].unsqueeze(1).to_broadcast([P, P // QD, QD]), ALU.mult)
            i.then_inc(blocks_made, 1)
            halves = pair_rows[:].rearrange("r j (t m) -> r j t m", t=P // HX)
            for part in range(3):
                pool.affine_select(out=halves, in_=halves, compare_op=ALU.not_equal, fill=1.0, base=-NX * part,
                                   pattern=[[-2, NJ], [-1, 2], [0, HX]], channel_multiplier=1).then_inc(pool_const, 1)
                pool.wait_ge(pool_const, 14 + part)

            with pool.Fori(1, B) as b:
                x_low(b)

            pool.wait_ge(ffn_w_in, 16 * FFN_DMAS)
            for m in range(2):
                pool.tensor_copy(in_hi[:, m], in_w[:, m]).then_inc(in_split, 1)
            for m in range(2):
                pool.wait_ge(in_split, 1 + m)
                pool.tensor_tensor(in_lo[:, m], in_w[:, m], in_hi[:, m].bitcast(F32), ALU.subtract).then_inc(in_split, 1)

            for f in range(HALVES):
                pool.wait_ge(xact_stored[f], 16 * B)
                pool.wait_ge(xt_stored[f], 16 * B)
                pool.wait_ge(gate_out[f], B)
            pool.memset(vals[:, :, :, DH:DV], 1.0).then_inc(phase2_const, 1)
            masked = pool.to_reg(NEG)

            def args(g, kp):
                if kp == 0:
                    pool.wait_ge(max_in, 16 * (g + 1))
                a_g = a_tok[:].rearrange("p b f k h -> p (b f) k h")[:, bass.ds(g, 1)].rearrange("p g k h -> p (g k) h")
                for par in range(2):
                    prev(pool, C_done[kp][par], g)
                    pool.tensor_tensor(
                        D[:, kp, par],
                        a_g.rearrange("p k (s two) -> p two k s", two=2)[:, par, 2 * kp:2 * kp + 2]
                        .unsqueeze(3).to_broadcast([P, 2, NP, P]),
                        max_b[:].rearrange("p (s two) (k t) -> p two k s t", two=2, k=NC)[:, par, 2 * kp:2 * kp + 2],
                        ALU.subtract).then_inc(arg_sub, 1)
                for par in range(2):
                    pool.wait_ge(arg_sub, nth(g, 4, 2 * kp + par))
                    alone(pool)
                    d = D[:, kp, par].rearrange("p k s t -> p (k s) t")
                    pool.affine_select(out=d, in_=d, compare_op=ALU.is_ge, fill=masked, base=0,
                                       pattern=[[0, 2 * NP], [1, P]], channel_multiplier=-1).then_inc(arg_masked, 1)

            def power(dst, src, s):
                pool.tensor_tensor(dst, src, half[:, 0:NC], ALU.pow).then_inc(s, 1)

            def weigh_queries(g):
                pool.wait_ge(xa_in, 16 * (g + 1))
                pool.wait_ge(inter_in, 32 * (g + 1))
                prev(pool, u_mm[NC - 1], g)
                pool.tensor_tensor(qs[:], xa[:], inter_w[:], ALU.mult).then_inc(qs_done, 1)

            def mix(g, f):
                dec = decay[:].rearrange("p s (g k) -> p g k s", k=NC)[:, bass.ds(g, 1)].rearrange("p g k s -> p (g k) s")
                for k in range(NC):
                    if k:
                        pool.wait_ge(state_done[k - 1], g + 1)
                    else:
                        prev(pool, state_done[NC - 1], g)
                    pool.tensor_tensor(kept[:], state[:], dec[:, k, :].unsqueeze(2).to_broadcast([P, NP, 2 * DV]),
                                       ALU.mult).then_inc(kept_done[k], 1)
                    if k == 0:
                        prev(pool, down_mm, g)
                        alone(pool)
                    if k < NP:
                        pool.tensor_scalar(mixed[:, k], xa[:, k], vecs[:, k, VS:VS + 1], None, ALU.mult
                                           ).then_inc(skip_done, 1)
                    if k in (1, 2) and not (isinstance(g, int) and g == NG - 1):
                        args(g + 1, k - 1)
                for kp in range(2):
                    c = slice(2 * kp, 2 * kp + 2)
                    pool.wait_ge(nrm_done[3], nth(g, 2, kp))
                    pool.tensor_tensor(r_h[:, c].rearrange("p k h -> p (k h)"), var_h[:, c].rearrange("p k h -> p (k h)"),
                                       half[:, 0:2 * NH], ALU.pow).then_inc(rh_done, 1)
                    pool.wait_ge(rh_done, nth(g, 2, kp))
                    pool.tensor_tensor(hn[:, c].rearrange("p k (h d) -> p (k h) d", d=DH),
                                       u_sb[:, c].rearrange("p k h d -> p (k h) d")[:, :, 0:DH],
                                       r_h[:, c].rearrange("p k h -> p (k h)").unsqueeze(2).to_broadcast([P, 2 * NH, DH]),
                                       ALU.mult).then_inc(hn_done, 1)
                pool.wait_ge(ve1_done, g + 1)
                power(rs1[:], ve1[:], rs1_done)
                if f is not None:
                    ffn(f)
                if not (isinstance(g, int) and g == NG - 1):
                    weigh_queries(g + 1)

            def ffn(f):
                pool.wait_ge(ve2_done, f + 1)
                power(rs2[:], ve2[:], rs2_done)

            pool.wait_ge(back_out, 1)
            args(0, 0)
            pool.wait_ge(back_out, BACK)
            pool.wait_ge(max_stored, 16 * HALVES)
            pool.wait_ge(rows_stored, 16 * (HALVES + 1))
            pool.memset(state[:], 0.0).then_inc(phase2_const, 1)
            pool.memset(gext[:, :, NX:NX + TOPK], -1.0).then_inc(phase2_const, 1)
            pool.memset(half[:], -0.5).then_inc(phase2_const, 1)
            pool.memset(comb3[:], 0.0).then_inc(phase2_const, 1)
            weigh_queries(0)
            args(0, 1)
            pool.wait_ge(decay_in, 16 * 2 * NP)
            pool.wait_ge(phase2_const, 5)
            groups(pool, mix, ffn)

        @block.scalar
        def _(act):
            def copy(dst, src):
                return act.activation(dst, src, ACT.Copy)

            def phase1_xact(b, f):
                if not (isinstance(b, int) and b == 0):
                    act.wait_ge(xact_stored[f], 16 * b)
                    act.wait_ge(gate_mm[f], b)
                for p in range(NP):
                    act.wait_ge(tap_done[f], b * NP * TAPS + HALO * NP + p + 1)
                    i = act.activation(xact[:, f, p], acc[:, f, p], ACT.Silu)
                i.then_inc(xact_done[f], 1)

            def phase1_xt(b, f):
                act.wait_ge(xt_mm[f], b + 1)
                if not (isinstance(b, int) and b == 0):
                    act.wait_ge(gate_x_mm[f], b)
                    act.wait_ge(xt_stored[f], 16 * b)
                copy(x_hi[:, f], bank[0][:])
                copy(x_t[:, f], bank[0][:]).then_inc(xt_out[f], 1)

            def phase1(b):
                first, last = isinstance(b, int) and b == 0, isinstance(b, int) and b == B - 1
                for f in range(HALVES):
                    if not first:
                        act.wait_ge(tap_done[f], b * NP * TAPS)
                    elif f == 0:
                        phase1_xt(0, 1)
                    for p in range(NP):
                        act.wait_ge(up_mm[f], b * 2 * NP + p + 1)
                        copy(xm[:, f, p, HALO:], bank[1 + p][:]).then_inc(up_out[f], 1)
                    if first:
                        if f == 1:
                            fold_parts()
                            fold_products()
                    elif f == 0:
                        phase1_xt(b, 1)
                    elif not last:
                        phase1_xt(b + 1, 0)
                    if f == 1:
                        phase1_xact(b, 0)
                        if first:
                            phase1_xt(1, 0)
                    elif not first:
                        phase1_xact(b - 1, 1)
                    if f == 0:
                        act.wait_ge(up_out[0], b * 2 * NP + NP)
                        copy(xm[:, 1, :, 0:HALO], xm[:, 0, :, G:G + HALO]).then_inc(halo_done, 1)
                    for p in range(NP):
                        act.wait_ge(up_mm[f], b * 2 * NP + NP + p + 1)
                        act.activation(silu_z[:, p, bass.ds(b * S + f * G, G)], bank[3 + p][:], ACT.Silu
                                       ).then_inc(up_out[f], 1)
                    if not first:
                        phase1_gates(b - 1, f)

            def fold_parts():
                act.wait_ge(fold1_mm, 1)
                act.activation(w_key[:].rearrange("p s d -> p (s d)"), bank[5][:, 0:INNER], ACT.Copy, scale=DH ** -0.5)
                copy(v_center[:].rearrange("p s d -> p (s d)"), bank[5][:, INNER:])
                copy(w_up_t[:].rearrange("p s d -> p (s d)"), bank[6][:, 0:INNER])
                n8, small = 2 * NH * NP, bank[6][:, INNER:]
                copy(g_act[:].rearrange("p s d -> p (s d)"), small[:, 0:n8])
                copy(g_v[:].rearrange("p s d -> p (s d)"), small[:, n8:2 * n8])
                copy(w_gate[:], small[:, 2 * n8:2 * n8 + NX]).then_inc(fold1_out, 1)

            def fold_products():
                act.wait_ge(fold2_mm, 1)
                copy(w_val[:], bank[7][:, 0:INNER])
                copy(g_x[:], bank[7][:, INNER:INNER + 2 * NH]).then_inc(weights_ready, 1)

            def phase1_gates(b, f):
                act.wait_ge(gate_mm[f], b + 1)
                dst = gates[:, f * NC:(f + 1) * NC].rearrange("p k t r -> p (k t) r")[:, :, bass.ds(b * NH, NH)]
                copy(dst, bank[5 + f][:, 0:NC * 2 * NH].rearrange("p (k h) -> p k h", h=NH)).then_inc(gate_out[f], 1)

            def mix_front(g):
                for p in range(NP):
                    act.wait_ge(key_mm[p], g + 1)
                    prev(act, keytok_mm[1], g)
                    copy(keyT[:, p], bank[1 + p][:]).then_inc(key_out[p], 1)
                act.wait_ge(val_mm[0], g + 1)
                copy(vals[:, 0:2, :, 0:DH].rearrange("p k h d -> p (k h) d"),
                     bank[3][:].rearrange("p (q d) -> p q d", d=DH)).then_inc(val_out[0], 1)

            def decays(g):
                for q in range(4):
                    act.wait_ge(arg_masked, nth(g, 4, q))
                    d = D[:, q // 2, q % 2].rearrange("p k s t -> p (k s t)")
                    act.activation(d, d, ACT.Exp).then_inc(D_done, 1)

            def mix(g, f):
                if f is not None:
                    ffn_head(f)
                for j in range(NJ + 1):
                    if f is not None:
                        ffn_slot(f, j)
                    if j in U_SLOT:
                        k = U_SLOT[j]
                        act.wait_ge(u_mm[k], g + 1)
                        if k == 0:
                            prev(act, hn_done, g, 2)
                        copy(u_sb[:, k].rearrange("p h d -> p (h d)"), bank[3][:, 0:NH * DV]).then_inc(u_out[k], 1)
                        if k % 2:
                            c = slice(k - 1, k + 1)
                            act.wait_ge(u_out[k], g + 1)
                            if k == 1:
                                prev(act, ssq_done, g, 2)
                            else:
                                act.wait_ge(ssq_done, nth(g, 2, 0))
                            act.activation(sq[:].rearrange("p k h d -> p (k h) d"),
                                           u_sb[:, c].rearrange("p k h d -> p (k h) d")[:, :, 0:DH],
                                           ACT.Square).then_inc(sq_done, 1)
                last = isinstance(g, int) and g == NG - 1
                if not last:
                    decays(g + 1)
                if not last:
                    mix_front(g + 1)

            def ffn_head(f):
                act.wait_ge(yT_mm, f + 1)
                prev2(act, z2_done, f)
                copy(yT[:], bank[7][:]).then_inc(yT_out, 1)
                copy(yT_hi[:], bank[7][:]).then_inc(yT_hi_done, 1)
                act.wait_ge(logit_mm, f + 1)
                act.activation(ge[:].rearrange("p k e -> p (k e)"), bank[6][:, 0:NC * NX], ACT.Exp,
                               scale=-1.0).then_inc(ge_done, 1)

            def ffn_slot(f, j):
                if j == 2:
                    act.wait_ge(combT_mm, f + 1)
                    copy(combT[:], bank[6][0:3 * NX, 0:G // 2].bitcast(BF16)).then_inc(combT_out, 1)
                act.wait_ge(hin_mm, nth(f, NJ + 1, j))
                if j >= 2:
                    act.wait_ge(h1_done, nth(f, NJ + 1, j - 2))
                act.activation(s_in[:, j % 2], bank[4][:], ACT.Silu).then_inc(silu_done, 1)

            def ffn(f):
                ffn_head(f)
                for j in range(NJ + 1):
                    ffn_slot(f, j)

            phase1_xt(0, 0)
            phase1(0)
            with act.Fori(1, B - 1) as b:
                phase1(b)
            phase1(B - 1)
            phase1_gates(B - 1, 0)
            phase1_xact(B - 1, 1)
            phase1_gates(B - 1, 1)

            act.wait_ge(row_mm, 1)
            for c in range(2):
                act.activation(abs_f[:, c * 512:(c + 1) * 512], bank[2 + c][0:R, :], ACT.Abs, bias=b_f[:]).then_inc(act_scan, 1)
            act.wait_ge(act_scan, 2)
            act.activation(exp_f[:], abs_f[:], ACT.Exp, scale=-1.0).then_inc(act_scan, 1)
            act.wait_ge(act_scan, 3)
            act.activation(log_f[:], exp_f[:], ACT.Ln, bias=1.0).then_inc(act_scan, 1)
            mix_front(0)
            for n, rows in ((9, rows_inter), (10, rows_decay), (11, rows_w)):
                act.wait_ge(dve_scan, n)
                act.activation(rows[:], rows[:], ACT.Exp).then_inc(act_scan, 1)
            act.wait_ge(dve_scan, 12)
            act.activation(rows_floor[:], rows_floor[:], ACT.Exp, scale=-1.0).then_inc(act_scan, 1)

            decays(0)
            groups(act, mix, ffn)

        @block.vector
        def _(dve):
            dve.wait_ge(up_w_in, 16)
            dve.tensor_copy(up_hi[:], w_up[:]).then_inc(up_split, 1)
            dve.wait_ge(up_split, 1)
            dve.tensor_tensor(up_lo[:], w_up[:], up_hi[:].bitcast(F32), ALU.subtract).then_inc(up_split, 1)
            dve.wait_ge(vec_mm, 1)
            dve.tensor_copy(vecs[:].rearrange("p s d -> p (s d)"), bank[7][:, 0:NP * 8]).then_inc(vec_out, 1)
            dve.wait_ge(vec_out, 1)

            def phase1(b):
                first = isinstance(b, int) and b == 0
                for f in range(HALVES):
                    for t in range(TAPS):
                        for p in range(NP):
                            a, src = acc[:, f, p], xm[:, f, p, t:t + G]
                            if t == 0:
                                dve.wait_ge(up_out[f], b * 2 * NP + p + 1)
                                if f == 1:
                                    dve.wait_ge(halo_done, b + 1)
                                if not first:
                                    dve.wait_ge(xact_done[f], b)
                                i = dve.tensor_scalar(a, src, vecs[:, p, 0:1], vecs[:, p, VB:VB + 1], ALU.mult, ALU.add)
                            else:
                                dve.wait_ge(tap_done[f], b * NP * TAPS + (t - 1) * NP + p + 1)
                                i = dve.scalar_tensor_tensor(a, src, vecs[:, p, t:t + 1], a, ALU.mult, ALU.add)
                            i.then_inc(tap_done[f], 1)

            phase1(0)
            with dve.Fori(1, B) as b:
                phase1(b)

            for c in range(2):
                dve.wait_ge(act_scan, c + 1)
                dve.tensor_scalar(min_f[:, c * 512:(c + 1) * 512], bank[2 + c][0:R, :], b_f[:], 0.0, ALU.add, ALU.min
                                  ).then_inc(dve_scan, 1)
            dve.wait_ge(row_mm, 2)
            for c in range(2):
                dve.tensor_scalar(pre_i[:, c * 512:(c + 1) * 512], bank[c][0:R, :], b_i[:], None, ALU.add
                                  ).then_inc(dve_scan, 1)
            dve.wait_ge(dve_scan, 4)
            dve.wait_ge(act_scan, 4)
            dve.tensor_tensor_scan(lfc[:], min_f[:], log_f[:], 0.0, ALU.add, ALU.subtract).then_inc(dve_scan, 1)
            dve.wait_ge(dve_scan, 5)
            dve.tensor_tensor(rows_a[:], pre_i[:], lfc[:], ALU.subtract).then_inc(dve_scan, 1)
            dve.wait_ge(dve_scan, 6)
            dve.tensor_tensor_scan(run_max[:], rows_a[:], rows_a[:], -3e38, ALU.max, ALU.max).then_inc(dve_scan, 1)
            dve.memset(before[:, 0:1], NEG)
            dve.wait_ge(dve_scan, SCAN_MAX)
            ends = run_max[:].rearrange("r (c t) -> r c t", t=P)[:, :, P - 1]
            dve.tensor_copy(before[:, 1:CS], ends[:, 0:CS - 1]).then_inc(dve_scan, 1)
            chunks = lambda t: t[:].rearrange("r (c t) -> r c t", t=P)
            wide = lambda t: t.unsqueeze(2).to_broadcast([R, CS, P])
            dve.wait_ge(dve_scan, 8)
            dve.tensor_tensor(chunks(rows_inter), wide(before[:]), chunks(run_max), ALU.subtract).then_inc(dve_scan, 1)
            dve.tensor_tensor(rows_decay[:], before[:], ends, ALU.subtract).then_inc(dve_scan, 1)

            def back(i, dst):
                dve.wait_ge(back_mm, i + 1)
                d = dst[:].rearrange("p b f k h -> p b (f k) h")
                s = bank[4 + i][:, 0:CS * R].rearrange("p (c b h) -> p b c h", b=B, h=NH)
                if dst is floor_tok:
                    dve.tensor_scalar(d, s, EPS_MIX, None, ALU.add).then_inc(back_out, 1)
                else:
                    dve.tensor_copy(d, s).then_inc(back_out, 1)

            back(0, a_tok)
            dve.tensor_tensor(chunks(rows_w), chunks(rows_a), wide(ends), ALU.subtract).then_inc(dve_scan, 1)
            dve.tensor_tensor(rows_floor[:], lfc[:], run_max[:], ALU.add).then_inc(dve_scan, 1)
            back(1, w_tok)
            back(2, floor_tok)

            dve.sem_inc(z2_done, 1)
            all_tok = lambda t: t[:].rearrange("p b f k h -> p (b f) (k h)")

            def of_group(t, g):
                return all_tok(t)[:, bass.ds(g, 1)].rearrange("p g (k h) -> p (g k) h", h=NH)

            def val_evac(g):
                dve.wait_ge(val_mm[1], g + 1)
                dve.tensor_copy(vals[:, 2:4, :, 0:DH].rearrange("p k h d -> p (k h) d"),
                                bank[0][:].rearrange("p (q d) -> p q d", d=DH)).then_inc(val_out[1], 1)

            def weigh_scores(g, kp):
                for par in range(2):
                    dve.wait_ge(D_done, nth(g, 4, 2 * kp + par))
                    dve.wait_ge(score_mm[kp][par], g + 1)
                    if kp:
                        dve.wait_ge(u_mm[1], g + 1)
                    dve.tensor_tensor(C[:, par].rearrange("p k s t -> p (k s t)"), bank[1 + par][:],
                                      D[:, kp, par].rearrange("p k s t -> p (k s t)"), ALU.mult
                                      ).then_inc(C_done[kp][par], 1)

            def weigh_keys(g, kp):
                dve.wait_ge(keytok_mm[kp], g + 1)
                dve.tensor_tensor(keys[:].rearrange("p k (h d) -> p (k h) d", d=DH),
                                  bank[0][:].rearrange("p (q d) -> p q d", d=DH),
                                  of_group(w_tok, g)[:, 2 * kp:2 * kp + 2, :].rearrange("p k h -> p (k h)")
                                  .unsqueeze(2).to_broadcast([P, 2 * NH, DH]), ALU.mult).then_inc(keytok_out[kp], 1)

            def update_state(g, k):
                dve.wait_ge(upd_mm[k], g + 1)
                dve.wait_ge(kept_done[k], g + 1)
                new = bank[0][:, 0:NP * 2 * DV].rearrange("p (s d) -> p s d", s=NP)
                for par in range(2):
                    r, c = slice(par * DH, (par + 1) * DH), slice(par * DV, (par + 1) * DV)
                    i = dve.tensor_tensor(state[r, :, c], kept[r, :, c], new[r, :, c], ALU.add)
                i.then_inc(state_done[k], 1)

            def head_scale(g, kp):
                c, now = slice(2 * kp, 2 * kp + 2), nth(g, 2, kp)
                dve.wait_ge(u_out[2 * kp + 1], g + 1)
                total = u_sb[:, c, :, DH]
                dve.scalar_tensor_tensor(nrm[:, c], total, -1.0, total, ALU.mult, ALU.max).then_inc(nrm_done[0], 1)
                dve.wait_ge(nrm_done[0], now)
                dve.scalar_tensor_tensor(nrm1[:, c], nrm[:, c], EPS_MIX, of_group(floor_tok, g)[:, c], ALU.add, ALU.max
                                         ).then_inc(nrm_done[1], 1)
                dve.wait_ge(nrm_done[1], now)
                dve.scalar_tensor_tensor(nrm2[:, c], nrm1[:, c], EPS_MIX, nrm1[:, c], ALU.mult, ALU.mult
                                         ).then_inc(nrm_done[2], 1)
                dve.wait_ge(sq_done, now)
                dve.tensor_reduce(ssq[:, c].rearrange("p k h -> p (k h)"), sq[:].rearrange("p k h d -> p (k h) d"),
                                  AX.X, ALU.add).then_inc(ssq_done, 1)
                dve.wait_ge(nrm_done[2], now)
                dve.wait_ge(ssq_done, now)
                dve.scalar_tensor_tensor(var_h[:, c], ssq[:, c], 1.0 / DH, nrm2[:, c], ALU.mult, ALU.add
                                         ).then_inc(nrm_done[3], 1)

            def gate_heads(g):
                dve.wait_ge(skip_done, nth(g, NP, NP - 1))
                for p in range(NP):
                    dve.wait_ge(hnT_mm[p], g + 1)
                    dve.scalar_tensor_tensor(mixed[:, p], bank[1 + p][:], vecs[:, p, VN:VN + 1], mixed[:, p],
                                             ALU.mult, ALU.add).then_inc(mixed_done[p], 1)
                for p in range(NP):
                    dve.wait_ge(mixed_done[p], g + 1)
                    dve.tensor_tensor(mixed[:, p], mixed[:, p], silu_z[:, p, bass.ds(g * G, G)], ALU.mult
                                      ).then_inc(hs_done[p], 1)

            flat = lambda t: t[:].rearrange("p k e -> p (k e)")

            def statistics(g, src, st, mv, ve, st_s, mv_s, ve_s):
                for k in range(NC):
                    i = dve.bn_stats(st[:, k], src[:, k])
                i.then_inc(st_s, 1)
                dve.wait_ge(st_s, g + 1)
                alone(dve)
                for k in range(NC):
                    i = dve.bn_aggr(mv[:, k], st[:, k])
                i.then_inc(mv_s, 1)
                dve.wait_ge(mv_s, g + 1)
                dve.tensor_scalar(ve[:], mv[:, :, 1], EPS_LN, None, ALU.add).then_inc(ve_s, 1)

            def normalise(dst, src, mv, rs, s):
                for k in range(NC):
                    i = dve.tensor_scalar(dst[:, k], src[:, k], mv[:, k, 0:1], rs[:, k:k + 1], ALU.subtract, ALU.mult)
                i.then_inc(s, 1)

            def mixer_out(g):
                dve.wait_ge(down_mm, g + 1)
                dve.wait_ge(x_res_in, 16 * (g + 1))
                dve.tensor_tensor(flat(y1), bank[3][:], flat(x_res), ALU.add).then_inc(y1_done, 1)
                dve.wait_ge(y1_done, g + 1)
                statistics(g, y1, st1, mv1, ve1, st1_done, mv1_done, ve1_done)

            def mixer_norm(g):
                dve.wait_ge(rs1_done, g + 1)
                normalise(Y, y1, mv1, rs1, Y_done)

            def mix_front(g):
                val_evac(g)
                weigh_scores(g, 0)

            def mix(g, f):
                weigh_keys(g, 0)
                if f is not None:
                    routing(f, 0)
                for j in range(NJ + 2):
                    if f is not None:
                        ffn_slot(f, j)
                    for what, arg in DVE_SLOT.get(j, ()):
                        if what == "route":
                            if f is not None:
                                routing(f, arg)
                        else:
                            {"C": weigh_scores, "K": weigh_keys, "S": update_state, "R": head_scale}[what](g, arg) \
                                if arg is not None else gate_heads(g)
                mixer_out(g)
                if f is not None:
                    ffn_sum(f)
                mixer_norm(g)
                if not (isinstance(g, int) and g == NG - 1):
                    mix_front(g + 1)
                yT_low(g)
                if f is not None:
                    ffn_norm(f)

            def yT_low(f):
                dve.wait_ge(yT_hi_done, f + 1)
                dve.tensor_tensor(yT_lo[:], bank[7][:], yT_hi[:].bitcast(F32), ALU.subtract).then_inc(yT_lo_done, 1)

            def routing(f, part):
                def after(n):
                    dve.wait_ge(route, f * ROUTE + n)

                if part == 0:
                    dve.wait_ge(ge_done, f + 1)
                    dve.tensor_scalar(ge1[:], ge[:], 1.0, None, ALU.add).then_inc(route, 1)
                    after(1)
                    dve.reciprocal(gext[:, :, 0:NX], ge1[:]).then_inc(route, 1)
                elif part == 1:
                    after(2)
                    alone(dve)
                    for k in range(NC):
                        i = dve.max(top[:, k], gext[:, k])
                    i.then_inc(route, 1)
                    after(3)
                    dve.memset(top[:, :, TOPK:8], -1.0).then_inc(route, 1)
                    after(4)
                    alone(dve)
                    for k in range(NC):
                        i = dve.match_replace(rest[:, k], top[:, k], gext[:, k], 0.0)
                    i.then_inc(route, 1)
                elif part == 2:
                    after(5)
                    dve.tensor_tensor(chosen[:], gext[:, :, 0:NX], rest[:, :, 0:NX], ALU.subtract).then_inc(route, 1)
                    after(6)
                    dve.tensor_reduce(csum[:], chosen[:], AX.X, ALU.add).then_inc(route, 1)
                    after(7)
                    dve.reciprocal(crec[:], csum[:]).then_inc(route, 1)
                    after(8)
                    dve.tensor_tensor(comb[:], chosen[:], crec[:].unsqueeze(2).to_broadcast([P, NC, NX]), ALU.mult
                                      ).then_inc(route, 1)
                else:
                    after(9)
                    dve.tensor_copy(comb3[:, :, 0], comb[:]).then_inc(route, 1)
                    after(10)
                    dve.tensor_tensor(comb_r[:, 0], comb[:], comb3[:, :, 0], ALU.subtract).then_inc(route, 1)
                    after(11)
                    dve.tensor_copy(comb3[:, :, 1], comb_r[:, 0]).then_inc(route, 1)
                    after(12)
                    dve.tensor_tensor(comb_r[:, 1], comb_r[:, 0], comb3[:, :, 1], ALU.subtract).then_inc(route, 1)
                    after(13)
                    dve.tensor_copy(comb3[:, :, 2], comb_r[:, 1]).then_inc(route, 1)

            def ffn_slot(f, j):
                if j <= NJ:
                    dve.wait_ge(silu_done, nth(f, NJ + 1, j))
                    dve.wait_ge(vin_mm, nth(f, NJ + 1, j))
                    if j >= 3:
                        dve.wait_ge(h2_done, nth(f, NJ, j - 3))
                    dst = h2 if j == 0 else h1
                    dve.tensor_tensor(dst[:, j % 2], s_in[:, j % 2], bank[5][:], ALU.mult).then_inc(h1_done, 1)
                if j >= 2:
                    dve.wait_ge(h1_done, nth(f, NJ + 1, j - 1))
                    dve.wait_ge(bc_mm, nth(f, NJ, j - 2))
                    dve.tensor_tensor(h2[:, (j - 1) % 2], h1[:, (j - 1) % 2], bank[6][:], ALU.mult).then_inc(h2_done, 1)

            def ffn_sum(f):
                dve.wait_ge(o_mm, f + 1)
                dve.tensor_tensor(flat(z2), bank[7][:], flat(Y), ALU.add).then_inc(z2_done, 1)
                dve.wait_ge(z2_done, f + 2)
                statistics(f, z2, st2, mv2, ve2, st2_done, mv2_done, ve2_done)

            def ffn_norm(f):
                dve.wait_ge(rs2_done, f + 1)
                prev(dve, out_stored, f, 16)
                normalise(out_sb, z2, mv2, rs2, out_done)

            def ffn(f):
                routing(f, 0)
                for j in range(NJ + 2):
                    ffn_slot(f, j)
                    if j == 0:
                        routing(f, 1)
                        routing(f, 2)
                    elif j == 1:
                        routing(f, 3)
                ffn_sum(f)
                ffn_norm(f)

            mix_front(0)
            dve.wait_ge(phase2_const, 5)
            groups(dve, mix, ffn)

        @block.tensor
        def _(pe):
            pe.wait_ge(pool_const, IDENT)

            def fold_parts():
                pe.wait_ge(blocks_made, 1)
                pe.wait_ge(vec_out, 1)
                n8, small = 2 * NH * NP, bank[6][:, INNER:]
                for s in range(NP):
                    q, k, v = (qkv_block[:, m, s] for m in range(3))
                    c = slice(s * P, (s + 1) * P)
                    pe.matmul(bank[5][:, c], k, q, start=True, stop=True)
                    pe.matmul(bank[5][:, INNER + s * P:INNER + (s + 1) * P], v, center[:], start=True, stop=True)
                    pe.transpose(bank[6][:, c], w_up[:, c], ident[:])
                    c8 = slice(s * 2 * NH, (s + 1) * 2 * NH)
                    pe.matmul(small[:, c8], q, w_gates[:, s], start=True, stop=False)
                    pe.matmul(small[:, c8], k, w_gates[:, NP + s], start=False, stop=True)
                    pe.matmul(small[:, n8 + s * 2 * NH:n8 + (s + 1) * 2 * NH], v, w_gates[:, 2 * NP + s], start=True, stop=True)
                pe.transpose(small[:, 2 * n8:2 * n8 + NX], gate_rows[:], ident[0:NX, 0:NX]).then_inc(fold1_mm, 1)

            def fold_products():
                pe.wait_ge(fold1_out, 1)
                for s in range(NP):
                    pe.matmul(bank[7][:, s * P:(s + 1) * P], w_up_t[:, s], v_center[:, s], start=True, stop=True)
                for s in range(NP):
                    i = pe.matmul(bank[7][:, INNER:INNER + 2 * NH], w_up_t[:, s], g_v[:, s], start=(s == 0), stop=(s == NP - 1))
                i.then_inc(fold2_mm, 1)

            def gate_out_of(f, k):
                return bank[5 + f][:, k * 2 * NH:(k + 1) * 2 * NH], slice(k * P, (k + 1) * P)

            def phase1_gates_x(b, f):
                if isinstance(b, int) and b == 0:
                    pe.wait_ge(weights_ready, 1)
                else:
                    pe.wait_ge(gate_out[f], b)
                for k in range(NC):
                    o, c = gate_out_of(f, k)
                    i = pe.matmul(o, x_t[:, f, c], g_x[:], start=(k == 0), stop=False, skip_group_check=True)
                i.then_inc(gate_x_mm[f], 1)

            def phase1_gates(b, f):
                pe.wait_ge(xact_done[f], b + 1)
                for k in range(NC):
                    o, c = gate_out_of(f, k)
                    for p in range(NP):
                        i = pe.matmul(o, xact[:, f, p, c], g_act[:, p], start=False, stop=(p == NP - 1),
                                      skip_group_check=True)
                i.then_inc(gate_mm[f], 1)

            def phase1_xt(b, f):
                pe.wait_ge(x_loaded[f], 16 * (b + 1))
                if f:
                    pe.wait_ge(xt_out[0], b + 1)
                elif not (isinstance(b, int) and b == 0):
                    pe.wait_ge(xt_out[1], b)
                for k in range(NC):
                    i = pe.transpose(bank[0][:, k * P:(k + 1) * P], x_in[:, f, k], ident[:])
                i.then_inc(xt_mm[f], 1)

            def phase1_up(b, f, q):
                if f:
                    pe.wait_ge(up_out[0], b * 2 * NP + q + 1)
                elif not (isinstance(b, int) and b == 0):
                    pe.wait_ge(up_out[1], (b - 1) * 2 * NP + q + 1)
                hi, lo = (w[:, q * P:(q + 1) * P] for w in (up_hi, up_lo))
                pe.matmul(bank[1 + q][:], hi, x_hi[:, f], start=True, stop=False)
                pe.matmul(bank[1 + q][:], lo, x_hi[:, f], start=False, stop=False)
                if q == 0:
                    pe.wait_ge(x_lo_done[f], b + 1)
                pe.matmul(bank[1 + q][:], hi, x_lo[:, f], start=False, stop=True).then_inc(up_mm[f], 1)

            def phase1(b):
                first, last = isinstance(b, int) and b == 0, isinstance(b, int) and b == B - 1
                for f in range(HALVES):
                    if f == 0:
                        phase1_xt(b, 1)
                    elif not first and not last:
                        phase1_xt(b + 1, 0)
                    pe.wait_ge(xt_out[f], b + 1)
                    for q in range(NP):
                        phase1_up(b, f, q)
                    if first:
                        if f == 1:
                            fold_parts()
                            phase1_xt(1, 0)
                    elif f == 1:
                        phase1_gates_x(b, 0)
                    else:
                        phase1_gates_x(b - 1, 1)
                    phase1_up(b, f, NP)
                    if first and f == 1:
                        fold_products()
                    phase1_up(b, f, NP + 1)
                    if not first:
                        phase1_gates(b - 1, f)
                    elif f == 1:
                        phase1_gates_x(b, 0)

            phase1_xt(0, 0)
            pe.wait_ge(vec_in, 16 * VEC_DMAS)
            for s in range(NP):
                i = pe.transpose(bank[7][:, s * 8:(s + 1) * 8], rows[:, s * P:(s + 1) * P], ident[0:8, 0:8])
            i.then_inc(vec_mm, 1)
            pe.wait_ge(up_split, 2)
            phase1(0)
            with pe.Fori(1, B - 1) as b:
                phase1(b)
            phase1(B - 1)
            phase1_gates(B - 1, 0)
            phase1_gates_x(B - 1, 1)
            phase1_gates(B - 1, 1)

            def mix_front(g):
                pe.wait_ge(xa_in, 16 * (g + 1))
                for p in range(NP):
                    prev(pe, mixed_done[p], g)
                    pe.matmul(bank[1 + p][:], w_key[:, p], xa[:, p], start=True, stop=True).then_inc(key_mm[p], 1)
                pe.wait_ge(xT_in, 16 * (g + 1))
                prev(pe, y1_done, g)
                prev(pe, state_done[NC - 1], g)
                for i in range(2):
                    for k in range(2):
                        c = 2 * i + k
                        ins = pe.matmul(bank[3 if i == 0 else 0][:, k * INNER:(k + 1) * INNER],
                                        xT2[:, c * P:(c + 1) * P], w_val[:], start=True, stop=True)
                    ins.then_inc(val_mm[i], 1)
                scores(g, 0)

            def scores(g, kp):
                for p in range(NP):
                    if kp == 0:
                        pe.wait_ge(key_out[p], g + 1)
                    else:
                        pe.wait_ge(C_done[0][p], g + 1)
                for k in range(2):
                    c = slice((2 * kp + k) * P, (2 * kp + k + 1) * P)
                    for p in range(NP):
                        for par in range(2):
                            r = slice(par * DH, (par + 1) * DH)
                            i = pe.matmul(bank[1 + par][:, (k * NP + p) * P:(k * NP + p + 1) * P],
                                          keyT[r, p, c], xa[r, p, c], start=True, stop=True)
                            if k and p:
                                i.then_inc(score_mm[kp][par], 1)

            def key_tokens(g, kp):
                pe.wait_ge(state_done[1] if kp else val_out[1], g + 1)
                for k in range(2):
                    for p in range(NP):
                        i = pe.transpose(bank[0][:, k * INNER + p * P:k * INNER + (p + 1) * P],
                                         keyT[:, p, (2 * kp + k) * P:(2 * kp + k + 1) * P], ident[:])
                i.then_inc(keytok_mm[kp], 1)

            def chunk(g, k):
                kp, kk = k // 2, k % 2
                pe.wait_ge(u_out[k - 1] if k else val_out[0], g + 1)
                if k == 0:
                    if isinstance(g, int) and g == 0:
                        pe.wait_ge(phase2_const, 5)
                    pe.wait_ge(qs_done, g + 1)
                    pe.wait_ge(val_out[1], g + 1)
                    prev(pe, state_done[NC - 1], g)
                else:
                    pe.wait_ge(state_done[k - 1], g + 1)
                for par in range(2):
                    pe.wait_ge(C_done[kp][par], g + 1)
                c = slice(k * P, (k + 1) * P)
                for p in range(NP):
                    o = bank[3][:, p * 2 * DV:(p + 1) * 2 * DV]
                    pe.matmul(o, qs[:, p, c], state[:, p], start=True, stop=False, skip_group_check=True)
                    for par in range(2):
                        i = pe.matmul(o[:, par * DV:(par + 1) * DV], C[:, par, kk, p], vals[:, k, 2 * p + par],
                                      start=False, stop=True, skip_group_check=True)
                i.then_inc(u_mm[k], 1)
                pe.wait_ge(state_done[k - 1] if kk else keytok_out[kp], g + 1)
                for p in range(NP):
                    i = pe.matmul(bank[0][:, p * 2 * DV:(p + 1) * 2 * DV], keys[:, kk, p * P:(p + 1) * P],
                                  vals[:, k, 2 * p:2 * p + 2].rearrange("p h d -> p (h d)"), start=True, stop=True)
                i.then_inc(upd_mm[k], 1)

            def head_transposes(g):
                pe.wait_ge(hn_done, nth(g, 2, 1))
                for p in range(NP):
                    pe.wait_ge(C_done[1][p], g + 1)
                    for k in range(NC):
                        i = pe.transpose(bank[1 + p][:, k * P:(k + 1) * P], hn[:, k, p * P:(p + 1) * P], ident[:])
                    i.then_inc(hnT_mm[p], 1)

            def down(g, half):
                if half == 0:
                    pe.wait_ge(u_out[NC - 1], g + 1)
                    for p in range(NP):
                        pe.wait_ge(hs_done[p], g + 1)
                for k in range(2 * half, 2 * half + 2):
                    for p in range(NP):
                        i = pe.matmul(bank[3][:, k * P:(k + 1) * P], mixed[:, p, k * P:(k + 1) * P], w_down[:, p],
                                      start=(p == 0), stop=(p == NP - 1))
                if half:
                    i.then_inc(down_mm, 1)

            def ffn_head(f):
                pe.wait_ge(Y_done, f + 1)
                prev2(pe, z2_done, f)
                for k in range(NC):
                    i = pe.transpose(bank[7][:, k * P:(k + 1) * P], Y[:, k], ident[:])
                i.then_inc(yT_mm, 1)

            def ffn_logits(f):
                pe.wait_ge(yT_out, f + 1)
                for k in range(NC):
                    i = pe.matmul(bank[6][:, k * NX:(k + 1) * NX], yT[:, k * P:(k + 1) * P], w_gate[:], start=True, stop=True)
                i.then_inc(logit_mm, 1)

            def ffn_in(f, j):
                for m, (done, free) in enumerate(((hin_mm, silu_done), (vin_mm, h1_done))):
                    if j:
                        pe.wait_ge(free, nth(f, NJ + 1, j - 1))
                    elif m == 0:
                        pe.wait_ge(yT_hi_done, f + 1)
                    o = bank[4 + m][:]
                    pe.matmul(o, in_hi[:, m, j], yT_hi[:], start=True, stop=False)
                    pe.matmul(o, in_lo[:, m, j], yT_hi[:], start=False, stop=False)
                    if j == 0 and m == 0:
                        pe.wait_ge(yT_lo_done, f + 1)
                    pe.matmul(o, in_hi[:, m, j], yT_lo[:], start=False, stop=True).then_inc(done, 1)

            def combine_transposes(f):
                pe.wait_ge(route, (f + 1) * ROUTE)
                pe.wait_ge(ge_done, f + 1)
                for k in range(NC):
                    i = pe.transpose(bank[6][:, k * P // 2:(k + 1) * P // 2].bitcast(BF16),
                                     comb3[:, k].rearrange("p t e -> p (t e)"), ident_bf[:])
                i.then_inc(combT_mm, 1)

            def combine_rows(f, j):
                if j > 1:
                    pe.wait_ge(h2_done, nth(f, NJ, j - 2))
                else:
                    pe.wait_ge(combT_out, f + 1)
                pe.matmul(bank[6][:], pair_rows[:, j - 1], combT[:], start=True, stop=True).then_inc(bc_mm, 1)

            def ffn_out(f, j):
                if j:
                    pe.wait_ge(h2_done, nth(f, NJ, j - 1))
                else:
                    pe.wait_ge(h1_done, nth(f, NJ + 1, 0))
                w = ewout[:, j - 1] if j else wsout[:]
                for k in range(NC):
                    i = pe.matmul(bank[7][:, k * P:(k + 1) * P], h2[:, j % 2, k * P:(k + 1) * P], w,
                                  start=(j == k == 0), stop=(j == NJ), skip_group_check=True)
                if j == NJ:
                    i.then_inc(o_mm, 1)

            def ffn_slot(f, j):
                if j == 2:
                    combine_transposes(f)
                if j <= NJ:
                    ffn_in(f, j)
                if 2 <= j <= NJ + 1:
                    combine_rows(f, j - 1)
                if j >= 2:
                    ffn_out(f, j - 2)

            def mix(g, f):
                if f is not None:
                    ffn_head(f)
                key_tokens(g, 0)
                if f is not None:
                    ffn_logits(f)
                for j in range(NJ + 3):
                    if f is not None:
                        ffn_slot(f, j)
                    for what, arg in PE_SLOT.get(j, ()):
                        {"S": scores, "K": key_tokens, "C": chunk, "D": down}[what](g, arg) \
                            if arg is not None else head_transposes(g)
                if not (isinstance(g, int) and g == NG - 1):
                    mix_front(g + 1)

            def ffn(f):
                ffn_head(f)
                ffn_logits(f)
                for j in range(NJ + 3):
                    ffn_slot(f, j)

            for f in range(HALVES):
                pe.wait_ge(gate_out[f], B)
            for t in (1, 0):
                for c in range(CS):
                    i = pe.transpose(bank[2 * t + c // 4][0:R, (c % 4) * P:(c % 4 + 1) * P], gates[:, c, t], ident[:])
                i.then_inc(row_mm, 1)
            pe.wait_ge(dve_scan, 4)
            pe.wait_ge(act_scan, 2)
            mix_front(0)
            pe.wait_ge(dve_scan, 6)
            for n, src in enumerate((rows_a, rows_w, rows_floor)):
                if n:
                    pe.wait_ge(act_scan, 6 + n)
                for c in range(CS):
                    i = pe.transpose(bank[4 + n][:, c * R:(c + 1) * R], src[:, c * P:(c + 1) * P], ident[0:R, 0:R])
                i.then_inc(back_mm, 1)

            pe.wait_ge(ffn_w_in, 16 * FFN_DMAS)
            pe.wait_ge(in_split, 4)
            pe.wait_ge(pool_const, CONSTS + 3)
            groups(pe, mix, ffn)


PE_SLOT = {0: (("C", 0),), 1: (("C", 1), ("S", 1), ("K", 1)), 2: (("C", 2),), 3: (("C", 3),),
           6: (("H", None),), 8: (("D", 0),), 9: (("D", 1),)}
DVE_SLOT = {0: (("route", 1), ("S", 0), ("route", 2)), 1: (("S", 1), ("route", 3), ("C", 1), ("K", 1)), 2: (("S", 2), ("R", 0)),
            3: (("S", 3),), 4: (("R", 1),), 6: (("H", None),)}
U_SLOT = {0: 0, 1: 1, 2: 2, 3: 3}
IDENT = 8
CONSTS = 13
SCAN_MAX = 7
DVE_SCAN = 12
SCAN_INTER = 6
BACK = 3
ROUTE = 14


_INS = ['L0_attn_x', 'L0_attn_W_up', 'L0_attn_conv_w', 'L0_attn_conv_b', 'L0_attn_Wq', 'L0_attn_Wk', 'L0_attn_Wv',
        'L0_attn_W_ig', 'L0_attn_b_ig', 'L0_attn_W_fg', 'L0_attn_b_fg', 'L0_attn_norm_w', 'L0_attn_skip',
        'L0_attn_W_down', 'L0_ffn_gate_w', 'L0_ffn_ws_in', 'L0_ffn_vs_in', 'L0_ffn_ws_out', 'L0_ffn_e_win',
        'L0_ffn_e_vin', 'L0_ffn_e_wout']
_OUTS = [((8, 1024, 128), 'float32')]


def kernel(**inputs):
    import numpy as _np
    import concourse.bacc as _bacc
    from concourse import mybir as _mybir
    from concourse.bass_utils import run_bass_kernel_spmd as _run

    nc = _bacc.Bacc("TRN2", target_bir_lowering=False, num_devices=1)
    arrays, args = {}, []
    for name in _INS:
        a = _np.ascontiguousarray(inputs[name])
        arrays[f"in_{name}_dram"] = a
        args.append(nc.dram_tensor(f"in_{name}_dram", a.shape, _mybir.dt.from_np(a.dtype), kind="ExternalInput").ap())
    for i, (shape, dtype) in enumerate(_OUTS):
        dt = _mybir.dt.from_np(_np.dtype(dtype))
        args.append(nc.dram_tensor(f"out_{i}_dram", shape, dt, kind="ExternalOutput").ap())
    mixer_moe_block(nc, *args)
    r = _run(nc, [arrays], core_ids=[0])
    return r.results[0]["out_0_dram"]
```
